# Optimizing a Trainium2 kernel written in Bass

```python
import numpy as np
import jax
import jax.numpy as jnp

def _softmax(x, axis=-1):
    return jax.nn.softmax(x, axis=axis)

def _gelu(x):
    return jax.nn.gelu(x, approximate=True)

def _silu(x):
    return jax.nn.silu(x)

def _sigmoid(x):
    return jax.nn.sigmoid(x)

def _layernorm(x, axis=-1, eps=1e-05):
    m = jnp.mean(x, axis=axis, keepdims=True)
    v = jnp.var(x, axis=axis, keepdims=True)
    return (x - m) / jnp.sqrt(v + eps)

def _scatter_add(tgt, idx, src, axis=0):
    return tgt.at[idx].add(src)

def _segment_sum(src, seg, n):
    return jax.ops.segment_sum(src, seg, n)
kernel_name = 'mk_cond_seq_d2_seqx_r4_d7c5d6'

def setup_inputs(seed: int=0):
    np.random.seed(seed)
    _w = jnp.asarray

    def _rec_inputs():
        import jax
        import jax.numpy as jnp
        _rk = jax.random.key(seed)
        x = 0.5 + 0.2887 * jax.random.normal(jax.random.fold_in(_rk, 1), (64, 64, 512), jnp.float32)
        _lenS = 64 - jax.random.randint(jax.random.fold_in(_rk, 7), (64,), 0, max(1, 64 // 4) + 1, jnp.int32)
        _lenS2 = 64 - jax.random.randint(jax.random.fold_in(_rk, 8), (64,), 0, max(1, 64 // 4) + 1, jnp.int32)
        itok_B_17_1546 = jax.random.randint(jax.random.fold_in(_rk, 12), (64,), 17, 1547, jnp.int32)
        itok_B_1_2 = jax.random.randint(jax.random.fold_in(_rk, 13), (64,), 1, 3, jnp.int32)
        return (x, itok_B_17_1546, itok_B_1_2, _lenS)
    x, itok_B_17_1546, itok_B_1_2, _lenS = _rec_inputs()

    def _L0_cond_setup():
        import jax, jax.numpy as jnp
        import numpy as np
        B, T, V = (8, 128, 512)
        H = 4 * V
        key = jax.random.key(seed)
        ks = jax.random.split(key, 16)
        s = lambda n: 1.0 / np.sqrt(n)
        inp = {'x': jax.random.uniform(ks[0], (B, T, V), dtype=jnp.float32), 'lens': jax.random.randint(ks[1], (B,), 1, T, dtype=jnp.int64), 'target_codes': jax.random.randint(ks[2], (B,), 0, V, dtype=jnp.int64), 'Wq': jax.random.normal(ks[3], (V, V), jnp.float32) * s(V), 'Wk': jax.random.normal(ks[4], (V, V), jnp.float32) * s(V), 'Wv': jax.random.normal(ks[5], (V, V), jnp.float32) * s(V), 'Wp': jax.random.normal(ks[6], (V, V), jnp.float32) * s(V), 'bp': jnp.zeros((V,), jnp.float32), 'cW1': jax.random.normal(ks[7], (V, H), jnp.float32) * s(V), 'cb1': jnp.zeros((H,), jnp.float32), 'cW2': jax.random.normal(ks[8], (H, V), jnp.float32) * s(H), 'cb2': jnp.zeros((V,), jnp.float32), 'mW1': jax.random.normal(ks[9], (2 * V, H), jnp.float32) * s(2 * V), 'mb1': jnp.zeros((H,), jnp.float32), 'mW2': jax.random.normal(ks[10], (H, V), jnp.float32) * s(H), 'mb2': jnp.zeros((V,), jnp.float32)}
        return inp
    _L0_cond_all = _L0_cond_setup()
    _L0_cond_in = {k: v for k, v in _L0_cond_all.items() if k in ('Wq', 'Wk', 'Wv', 'Wp', 'bp', 'cW1', 'cb1', 'cW2', 'cb2', 'mW1', 'mb1', 'mW2', 'mb2')}
    del _L0_cond_all

    def _L1_cond_setup():
        import jax, jax.numpy as jnp
        import numpy as np
        H = 512
        K = 256
        R = 3
        B = 8
        S = 512
        LN_EPS = 1e-05
        key = jax.random.key(seed)
        ks = jax.random.split(key, 8)
        sd_d = 1.0 / np.sqrt(H)
        sd_u = 1.0 / np.sqrt(K)
        return {'role': jax.random.randint(ks[0], (B,), 0, R), 'hidden_states': jax.random.normal(ks[1], (B, S, H), dtype=jnp.float32), 'W_down': jax.random.uniform(ks[2], (R, H, K), jnp.float32, -sd_d, sd_d), 'b_down': jax.random.uniform(ks[3], (R, K), jnp.float32, -sd_d, sd_d), 'W_up': jax.random.uniform(ks[4], (R, K, H), jnp.float32, -sd_u, sd_u), 'b_up': jax.random.uniform(ks[5], (R, H), jnp.float32, -sd_u, sd_u), 'gamma': jnp.ones((R, H), jnp.float32), 'beta': jnp.zeros((R, H), jnp.float32)}
    _L1_cond_all = _L1_cond_setup()
    _L1_cond_in = {k: v for k, v in _L1_cond_all.items() if k in ('W_down', 'b_down', 'W_up', 'b_up', 'gamma', 'beta')}
    del _L1_cond_all
    return {'x': x, 'itok_B_17_1546': itok_B_17_1546, 'itok_B_1_2': itok_B_1_2, '_lenS': _lenS, 'L0_cond_Wq': _L0_cond_in['Wq'], 'L0_cond_Wk': _L0_cond_in['Wk'], 'L0_cond_Wv': _L0_cond_in['Wv'], 'L0_cond_Wp': _L0_cond_in['Wp'], 'L0_cond_bp': _L0_cond_in['bp'], 'L0_cond_cW1': _L0_cond_in['cW1'], 'L0_cond_cb1': _L0_cond_in['cb1'], 'L0_cond_cW2': _L0_cond_in['cW2'], 'L0_cond_cb2': _L0_cond_in['cb2'], 'L0_cond_mW1': _L0_cond_in['mW1'], 'L0_cond_mb1': _L0_cond_in['mb1'], 'L0_cond_mW2': _L0_cond_in['mW2'], 'L0_cond_mb2': _L0_cond_in['mb2'], 'L1_cond_W_down': _L1_cond_in['W_down'], 'L1_cond_b_down': _L1_cond_in['b_down'], 'L1_cond_W_up': _L1_cond_in['W_up'], 'L1_cond_b_up': _L1_cond_in['b_up'], 'L1_cond_gamma': _L1_cond_in['gamma'], 'L1_cond_beta': _L1_cond_in['beta']}

def reference(x, itok_B_17_1546, itok_B_1_2, _lenS, L0_cond_Wq, L0_cond_Wk, L0_cond_Wv, L0_cond_Wp, L0_cond_bp, L0_cond_cW1, L0_cond_cb1, L0_cond_cW2, L0_cond_cb2, L0_cond_mW1, L0_cond_mb1, L0_cond_mW2, L0_cond_mb2, L1_cond_W_down, L1_cond_b_down, L1_cond_W_up, L1_cond_b_up, L1_cond_gamma, L1_cond_beta):
    import jax
    import jax.numpy as jnp

    def _L0_cond_ref(x, lens, target_codes, Wq, Wk, Wv, Wp, bp, cW1, cb1, cW2, cb2, mW1, mb1, mW2, mb2):
        import jax, jax.numpy as jnp
        import numpy as np
        B, T, V = (8, 128, 512)
        H = 4 * V
        scale = V ** (-0.5)
        q = x @ Wq
        k = x @ Wk
        v = x @ Wv
        attn = jnp.einsum('btd,bTd->btT', q, k) * scale
        attn = jax.nn.softmax(attn, axis=-1)
        attn_out = jnp.einsum('btT,bTd->btd', attn, v) @ Wp + bp
        target_embed = jax.nn.one_hot(target_codes, V, dtype=x.dtype)[:, None, :]
        cms_out = jax.nn.gelu(attn_out @ cW1 + cb1, approximate=False) @ cW2 + cb2
        cms_out = cms_out + target_embed
        concat = jnp.concatenate([attn_out, cms_out], axis=-1)
        modifier = jax.nn.gelu(concat @ mW1 + mb1, approximate=False) @ mW2 + mb2
        out = jnp.clip(x + cms_out + modifier, 0.0, 1.0)
        return out

    def _L1_cond_ref(role, hidden_states, W_down, b_down, W_up, b_up, gamma, beta):
        import jax, jax.numpy as jnp
        import numpy as np
        H = 512
        K = 256
        R = 3
        B = 8
        S = 512
        LN_EPS = 1e-05
        h = jnp.einsum('bsh,bhk->bsk', hidden_states, W_down[role]) + b_down[role][:, None, :]
        h = jax.nn.gelu(h, approximate=False)
        u = jnp.einsum('bsk,bkh->bsh', h, W_up[role]) + b_up[role][:, None, :]
        y = hidden_states + u
        mean = jnp.mean(y, axis=-1, keepdims=True)
        var = jnp.mean(jnp.square(y - mean), axis=-1, keepdims=True)
        yn = (y - mean) * jax.lax.rsqrt(var + LN_EPS)
        return yn * gamma[role][:, None, :] + beta[role][:, None, :]
    x = _L0_cond_ref(x, _lenS, itok_B_17_1546, L0_cond_Wq, L0_cond_Wk, L0_cond_Wv, L0_cond_Wp, L0_cond_bp, L0_cond_cW1, L0_cond_cb1, L0_cond_cW2, L0_cond_cb2, L0_cond_mW1, L0_cond_mb1, L0_cond_mW2, L0_cond_mb2)
    x = _L1_cond_ref(itok_B_1_2, x, L1_cond_W_down, L1_cond_b_down, L1_cond_W_up, L1_cond_b_up, L1_cond_gamma, L1_cond_beta)
    return x

_drawn_inputs = setup_inputs


def setup_inputs(seed=0):
    import zlib

    import numpy as np

    out = dict(_drawn_inputs(seed))
    spreads = {'L0_cond_bp': (0.0, 0.1),
     'L0_cond_cb1': (0.0, 0.1),
     'L0_cond_cb2': (0.0, 0.1),
     'L0_cond_mb1': (0.0, 0.1),
     'L0_cond_mb2': (0.0, 0.1),
     'L1_cond_gamma': (1.0, 0.2),
     'L1_cond_beta': (0.0, 0.1)}
    factors = {'L0_cond_Wq': 5.584, 'L0_cond_Wk': 5.547, 'L1_cond_b_down': 2.712}
    for name, (base, spread) in spreads.items():
        noise = np.random.default_rng([zlib.crc32(name.encode()), seed]).standard_normal(out[name].shape)
        drawn = base * np.exp(spread * noise) if base else spread * noise
        out[name] = jnp.asarray(drawn.astype(out[name].dtype))
    for name, factor in factors.items():
        out[name] = (out[name] * factor).astype(out[name].dtype)
    return out
```

```python
from contextlib import ExitStack

import concourse.bass as bass
from concourse import mybir

P = 128
F32 = mybir.dt.float32
F32R = mybir.dt.float32r
I32 = mybir.dt.int32
ALU = mybir.AluOpType
ACT = mybir.ActivationFunctionType
AX_X = mybir.AxisListType.X

B, S, D = 64, 64, 512
H = 4 * D
R, KD = 3, 256
TOK = 512
NT = B * S // TOK
BT = TOK // S
DC = D // P
JH = H // P
NP = TOK // P
SCALE = float(D) ** -0.5
LN_EPS = 1e-5

W1_STAGE, W1_RING, W2_RING = 4, 8, 2
W1_AHEAD = 4
QT, QA, QC, QM = DC, DC, JH, 2 * JH
Q_PRE = QT + QA + QC
Q_ITER = QT + QM + QA + QC
G_PRE = DC + DC + JH
G_ITER = DC + JH + DC + JH

NPAIR = B // 2 + (R - 1) // 2
NSLOT = 2 * NPAIR
UNROLL = 4
LOOPS = (NPAIR - 2) // UNROLL

CB1, MB1, BP, CB2, MB2 = 0, JH, 2 * JH, 2 * JH + DC, 2 * JH + 2 * DC
NBIAS = 2 * JH + 3 * DC


def program(nc, xT, xk, w1c, w1m, w2c, w2m, wqT, wkT, wvT, wp, bias, target, role,
            wd, wu, bd, bu, gamma, beta, out):
    wa_dram = nc.dram_tensor("wa_blocks", (2 * DC, P, D), F32).ap()
    z_dram = nc.dram_tensor("z_by_batch", (B, P, DC * S), F32).ap()

    ctx = ExitStack()
    with ctx:
        main = ExitStack()

        def sb(name, shape, dt=F32, on=ctx):
            return on.enter_context(nc.sbuf_tensor(name, shape, dt))

        def sem(name):
            return ctx.enter_context(nc.semaphore(name))

        def hl(name, shape, on=ctx):
            return sb(name + "_hi", shape, F32R, on), sb(name + "_lo", shape, F32R, on)

        bias_sb = sb("bias_sb", [P, NBIAS])
        ident = sb("ident", [P, P])
        ident_r = sb("ident_r", [P, P], F32R)
        iota_p = sb("iota_p", [P, DC])
        iota_f = sb("iota_f", [P, NSLOT])
        ohb = sb("ohb", [P, DC, B])
        first_t = sb("first_t", [1, NPAIR], I32)
        second_t = sb("second_t", [1, NPAIR], I32)
        role_t = sb("role_t", [1, NPAIR], I32)

        w1_st = sb("w1_st", [P, W1_STAGE, D], on=main)
        w1_hi, w1_lo = hl("w1", [P, W1_RING, D], main)
        w2_st = sb("w2_st", [P, W2_RING, D], on=main)
        w2_hi, w2_lo = hl("w2", [P, W2_RING, D], main)
        x_st = sb("x_st", [P, DC, TOK], on=main)
        x_hi, x_lo = hl("x", [P, DC, TOK], main)
        xk_st = sb("xk_st", [P, 2, D], on=main)
        xk_hi, xk_lo = hl("xk", [P, D], main)
        t_hi, t_lo = hl("t", [P, DC, TOK], main)
        y_hi, y_lo = hl("y", [P, DC, TOK], main)
        a_hi, a_lo = hl("a", [P, DC, TOK], main)
        c_hi, c_lo = hl("c", [P, DC, TOK], main)
        xr = sb("xr", [P, DC, TOK], on=main)
        cf = sb("cf", [P, 2, TOK], on=main)
        zt = sb("zt", [P, 2, TOK], on=main)
        zb = sb("zb", [P, BT, DC, S], on=main)
        hf = sb("hf", [P, 2, TOK], on=main)
        h_hi, h_lo = hl("h", [P, 2, TOK], main)
        mx = sb("mx", [P, 1], on=main)
        nmx = sb("nmx", [P, 1], on=main)
        rs = sb("rs", [P, 1], on=main)
        rinv = sb("rinv", [P, 1], on=main)
        pe_ = sb("p_exp", [P, P], on=main)
        pn = sb("p_norm", [P, P], on=main)
        pt_hi, pt_lo = hl("pt", [P, P], main)
        tgt_i = sb("tgt_i", [P, B], I32, main)
        tgt_f = sb("tgt_f", [P, B], on=main)
        role_i = sb("role_i", [B, 1], I32, main)
        role_f = sb("role_f", [B, 1], on=main)
        batch_f = sb("batch_f", [B, 3], on=main)
        onehot = sb("onehot", [B, R], on=main)
        before = sb("before", [B, B], on=main)
        ones = sb("ones", [B, B], on=main)
        even = sb("even", [B, B // 2], on=main)
        flags = sb("flags", [B, B // 2], on=main)
        half = sb("half", [B, R], on=main)
        start = sb("start", [B, R], on=main)
        rank_r = sb("rank_r", [B, R], on=main)
        rank = sb("rank", [B, 1], on=main)
        slot1 = sb("slot1", [B, NSLOT], on=main)
        slots = sb("slots", [1, 3, NPAIR, 2], on=main)
        empty = sb("empty", [1, NPAIR, 2], on=main)
        fill = sb("fill", [1, 3, NPAIR], on=main)
        pick = sb("pick", [1, 3, NPAIR], on=main)
        main.close()

        wd_f = sb("wd_f", [P, R, DC, KD])
        wd_hi, wd_lo = hl("wd", [P, R, DC, KD])
        wu_f = sb("wu_f", [P, R, KD // P, D])
        wu_hi, wu_lo = hl("wu", [P, R, KD // P, D])
        brow_f = sb("brow_f", [1, R, KD + D])
        brow_lo = sb("brow_lo", [1, R, KD + D], F32R)
        brow = sb("brow", [2, R, KD + D], F32R)
        ones2f = sb("ones2f", [2, P])
        ones2 = sb("ones2", [2, P], F32R)
        gam = sb("gam", [P, R, D])
        bet = sb("bet", [P, R, D])
        zs = sb("zs", [P, 4, 2, DC, S])
        z_hi, z_lo = hl("z", [P, 4, DC, P])
        hs = sb("hs", [P, 2, KD])
        ht_hi, ht_lo = hl("ht", [P, 2, KD])
        st6 = sb("st6", [P, 6])
        mv = sb("mv", [P, 2])
        veps = sb("veps", [P, 2])
        negm = sb("negm", [P, 2])
        mhalf = sb("mhalf", [P, 1])
        rstd = sb("rstd", [P, 2])
        nbias = sb("nbias", [P, 2])
        yn = sb("yn", [P, 2, D])
        yg = sb("yg", [P, 2, D])
        yo = sb("yo", [P, 2, D])

        def bank(name):
            return ctx.enter_context(nc.psum_tensor(name, [P, 512], F32))

        hb = [bank("hb0"), bank("hb1")]
        acc = [bank(f"acc{c}") for c in range(DC)]
        sp_bank = bank("scores")
        y_bank = bank("yb")
        s_ps = sp_bank[:, 0:P]
        pt_ps = sp_bank[:, P:2 * P]
        d_ps = hb
        ht_ps = [sp_bank, y_bank]
        u_ps = acc

        w1_loaded = [sem(f"w1_loaded{k}") for k in range(W1_STAGE)]
        w2_loaded = [sem(f"w2_loaded{k}") for k in range(W2_RING)]
        w1_hi_s, w1_lo_s = sem("w1_hi_split"), sem("w1_lo_split")
        w2_hi_s, w2_lo_s = sem("w2_hi_split"), sem("w2_lo_split")
        h_mm = sem("h_mm")
        h_hi_s, h_lo_s = sem("h_hi_ready"), sem("h_lo_ready")
        acc_mm = sem("acc_mm")
        x_loaded, x_hi_s, x_lo_s = sem("x_loaded"), sem("x_hi_split"), sem("x_lo_split")
        xk_loaded = [sem("xk_loaded0"), sem("xk_loaded1")]
        xk_hi_s, xk_lo_s = sem("xk_hi_split"), sem("xk_lo_split")
        s_mm, mx_s, nmx_s, exp_s = sem("scores_mm"), sem("row_max"), sem("neg_max"), sem("exp_done")
        rinv_s, pn_s = sem("row_inverse"), sem("p_normalised")
        pt_mm, pt_hi_s, pt_lo_s = sem("pt_mm"), sem("pt_hi_ready"), sem("pt_lo_ready")
        y_mm, y_hi_s, y_lo_s = sem("y_mm"), sem("y_hi_ready"), sem("y_lo_ready")
        cf_s, c_hi_s, c_lo_s = sem("cms_f32"), sem("cms_hi_ready"), sem("cms_lo_ready")
        xr_loaded, xr_sum = sem("xr_loaded"), sem("xr_summed")
        zt_s, z_ready, z_stored = sem("z_unclipped"), sem("z_ready"), sem("z_stored")
        const_in, const_s, pool_c = sem("constants_loaded"), sem("dve_constants"), sem("pool_constants")
        ohb_s, zero_p = sem("onehot_bias"), sem("p_exp_zeroed")
        qw_loaded = [sem(f"projection_loaded{k}") for k in range(4)]
        qw_hi, qw_lo = sem("projection_hi"), sem("projection_lo")
        wa_mm, wa_out, wa_stored = sem("product_mm"), sem("product_out"), [sem("product_stored0"), sem("product_stored1")]
        sort_in, sort_v, sort_mm, sorted_s = sem("roles_loaded"), sem("sort_vector"), sem("sort_mm"), sem("order_ready")
        l1_loaded, l1_hi, l1_lo = sem("adapter_loaded"), sem("adapter_hi"), sem("adapter_lo")
        row_hi, row_lo, row_in = sem("bias_row_hi"), sem("bias_row_lo"), sem("bias_row_moved")
        gb_loaded, ones_s, mhalf_s = sem("gamma_beta_loaded"), sem("ones_ready"), sem("minus_half")
        zl = [sem(f"z_loaded{k}") for k in range(4)]
        zh_s, zl_s = sem("z_hi_split"), sem("z_lo_split")
        d_mm, gelu_s, ht_mm, ht_hi_s, ht_lo_s = sem("down_mm"), sem("gelu_done"), sem("ht_mm"), sem("ht_hi_ready"), sem("ht_lo_ready")
        u_mm, st_s, mv_s, ve_s = sem("up_mm"), sem("stats"), sem("mean_var"), sem("var_eps")
        rstd_s, nb_s, yn_s, yg_s, yo_s = sem("rstd"), sem("neg_mean_rstd"), sem("normalised"), sem("times_gamma"), sem("row_ready")
        a_stored = [sem("first_stored0"), sem("first_stored1")]
        b_stored = [sem("second_stored0"), sem("second_stored1")]

        def f32(ap):
            return ap.bitcast(F32)

        def bcol(col):
            return bias_sb[:, col:col + 1]

        block = ctx.enter_context(nc.Block())

        @block.sync
        def _(sp):
            sp.dma_start(role_i[:], role).then_inc(sort_in, 16)
            sp.dma_start(bias_sb[:], bias).then_inc(const_in, 16)
            sp.dma_start(tgt_i[:], target.to_broadcast([P, B])).then_inc(const_in, 16)
            for n, (dst, src) in enumerate([(x_st, wqT), (xr, wkT)]):
                sp.dma_start(dst[:], src).then_inc(qw_loaded[n], 16)
            for n, (dst, src) in enumerate([(x_st, wvT), (xr, wp)]):
                sp.wait_ge(qw_lo, n + 1)
                sp.dma_start(dst[:], src).then_inc(qw_loaded[2 + n], 16)

            for m in range(2 * DC):
                sp.wait_ge(wa_out, m + 1)
                first = m // DC * DC
                sp.dma_start(wa_dram[first:first + DC, :, (m % DC) * P:(m % DC + 1) * P].rearrange("j p n -> p j n"),
                             hf[:, m % 2, :].rearrange("p (j n) -> p j n", j=DC)).then_inc(wa_stored[m % 2], 16)

            def load_w1(q, k, src, reuse=True):
                if reuse:
                    sp.wait_ge(w1_lo_s, q - (W1_STAGE - 1))
                sp.dma_start(w1_st[:, k % W1_STAGE, :], src).then_inc(w1_loaded[k % W1_STAGE], 16)

            def load_w2(n, k, src, reuse=True):
                if reuse:
                    sp.wait_ge(w2_lo_s, n - (W2_RING - 1))
                sp.dma_start(w2_st[:, k % W2_RING, :], src).then_inc(w2_loaded[k % W2_RING], 16)

            def head(q, n_end, src, w2_last, w2_next):
                for c in range(W1_AHEAD):
                    load_w1(q + c, c, src[c])
                    if w2_last is w2c:
                        load_w2(n_end - 3 + c, JH - 3 + c, w2_last[JH - 3 + c] if c < 3 else w2_next[0])
                    elif c % 2:
                        load_w2(n_end - 1 + c // 2, JH - 1 + c // 2, w2_last[JH - 1] if c == 1 else w2_next[0])

            def body_m(q, n):
                for k in range(W1_AHEAD, QM):
                    load_w1(q + k, k, w1m[k])
                    if k % 2:
                        j = (k - W1_AHEAD) // 2 + 1
                        load_w2(n + j, j, w2m[j])

            def body_c(q, n):
                for k in range(W1_AHEAD, QC):
                    load_w1(q + k, k, w1c[k])
                    load_w2(n + k - 3, k - 3, w2c[k - 3], reuse=not (isinstance(n, int) and k - 3 < W2_RING))

            for s in range(2):
                sp.wait_ge(wa_stored[s], 16 * DC)
            for c in range(2 * DC):
                load_w1(c, c, wa_dram[c], reuse=c >= W1_STAGE)
            for k in range(W1_AHEAD):
                load_w1(2 * DC + k, k, w1c[k])
            load_w2(0, 0, w2c[0], reuse=False)
            body_c(2 * DC, 0)
            with sp.Fori(0, NT - 1) as i:
                q = i * Q_ITER + Q_PRE
                n = i * (2 * JH) + JH
                head(q, n, wa_dram, w2c, w2m)
                for k in range(W1_AHEAD):
                    load_w1(q + QT + k, k, w1m[k])
                body_m(q + QT, n)
                head(q + QT + QM, n + JH, wa_dram[DC:2 * DC], w2m, w2c)
                for k in range(W1_AHEAD):
                    load_w1(q + QT + QM + QA + k, k, w1c[k])
                body_c(q + QT + QM + QA, n + JH)
            q, n = (NT - 1) * Q_ITER + Q_PRE, (NT - 1) * 2 * JH + JH
            head(q, n, w1m, w2c, w2m)
            body_m(q, n)
            load_w2(n + JH - 1, JH - 1, w2m[JH - 1])

            sp.wait_ge(z_ready, NT * DC)
            sp.wait_ge(z_stored, NT * 16)
            sp.dma_start(wd_f[:], wd).then_inc(l1_loaded, 16)
            sp.dma_start(wu_f[:], wu).then_inc(l1_loaded, 16)
            sp.dma_start(brow_f[:, :, 0:KD], bd).then_inc(l1_loaded, 16)
            sp.dma_start(brow_f[:, :, KD:KD + D], bu).then_inc(l1_loaded, 16)
            sp.dma_start(gam[:], gamma.to_broadcast([P, R, D])).then_inc(gb_loaded, 16)
            sp.dma_start(bet[:], beta.to_broadcast([P, R, D])).then_inc(gb_loaded, 16)
            sp.wait_ge(row_lo, 1)
            sp.dma_start(f32(brow[1:2]), f32(brow_lo[:])).then_inc(row_in, 16)
            sp.wait_ge(sorted_s, 3)

            def load_z(n, slot):
                for k, table in enumerate((first_t, second_t)):
                    b = sp.value_load(table[0:1, bass.ds(n, 1)], min_val=0, max_val=B - 1)
                    sp.dma_start(zs[:, slot, k, :, :].rearrange("p c s -> p (c s)"),
                                 z_dram[bass.ds(b, 1)].rearrange("o p f -> (o p) f")).then_inc(zl[slot], 16)

            def store_second(n, slot):
                b = sp.value_load(second_t[0:1, bass.ds(n, 1)], min_val=0, max_val=B - 1)
                dst = out[bass.ds(b, 1)].rearrange("o s d -> (o s) d")
                sp.wait_ge(yo_s, n + 1)
                sp.wait_ge(a_stored[slot], (n - slot) * 8 + 16)
                sp.dma_start(dst, yo[S:2 * S, slot, :]).then_inc(b_stored[slot], 16)

            for n in range(4):
                load_z(n, n)
            for n in range(1):
                sp.wait_ge(zl_s, n + 1)
                load_z(n + 4, n % 4)

            def unit(n, u, load):
                if load:
                    sp.wait_ge(zl_s, n + 1)
                    load_z(n + 4, u % 4)
                store_second(n - 1, (u - 1) % 2)

            with sp.Fori(0, LOOPS) as k:
                for u in range(UNROLL):
                    unit(k * UNROLL + (1 + u), 1 + u, True)
            for n in range(LOOPS * UNROLL + 1, NPAIR):
                unit(n, n % 4, n + 4 < NPAIR)
            store_second(NPAIR - 1, (NPAIR - 1) % 2)
            for s in range(2):
                uses = (NPAIR + 1 - s) // 2
                sp.wait_ge(b_stored[s], 16 * uses)
                sp.wait_ge(a_stored[s], 16 * uses)

        @block.gpsimd
        def _(pool):
            nc.gpsimd.memset(ident[:], 0.0).then_inc(pool_c, 1)
            nc.gpsimd.memset(before[:], 1.0).then_inc(pool_c, 1)
            pool.wait_ge(pool_c, 2)
            nc.gpsimd.affine_select(out=ident[:], in_=ident[:], compare_op=ALU.not_equal, fill=1.0,
                                    base=0, pattern=[[-1, P]], channel_multiplier=1).then_inc(pool_c, 1)
            nc.gpsimd.affine_select(out=before[:], in_=before[:], compare_op=ALU.is_gt, fill=0.0,
                                    base=0, pattern=[[1, B]], channel_multiplier=-1).then_inc(pool_c, 1)
            nc.gpsimd.iota(iota_p[:], pattern=[[P, DC]], base=0, channel_multiplier=1,
                           allow_small_or_imprecise_dtypes=True).then_inc(pool_c, 1)
            nc.gpsimd.iota(iota_f[:], pattern=[[1, NSLOT]], base=0, channel_multiplier=0,
                           allow_small_or_imprecise_dtypes=True).then_inc(pool_c, 1)
            nc.gpsimd.iota(even[:], pattern=[[2, B // 2]], base=0, channel_multiplier=0,
                           allow_small_or_imprecise_dtypes=True).then_inc(pool_c, 1)

            def load_xk(t, p):
                pool.dma_start(xk_st[:, p % 2, :], xk[bass.ds(t * NP + p, 1)].rearrange("o p d -> (o p) d")
                               ).then_inc(xk_loaded[p % 2], 16)

            pool.wait_ge(qw_lo, 4)
            pool.dma_start(x_st[:], xT[0]).then_inc(x_loaded, 16)
            pool.dma_start(xr[:], xT[0]).then_inc(xr_loaded, 16)
            for p in range(NP):
                if p >= 2:
                    pool.wait_ge(xk_lo_s, p - 1)
                pool.dma_start(xk_st[:, p % 2, :], xk[p]).then_inc(xk_loaded[p % 2], 16)
            pool.wait_ge(x_lo_s, DC)
            pool.dma_start(x_st[:], xT[1]).then_inc(x_loaded, 16)
            with pool.Fori(0, NT - 1) as i:
                for p in range(NP):
                    pool.wait_ge(xk_lo_s, i * NP + (NP + p - 1))
                    load_xk(i + 1, p)
                pool.wait_ge(x_lo_s, i * DC + 2 * DC)
                nxt = (i + 2) % NT
                pool.dma_start(x_st[:], xT[bass.ds(nxt, 1)].rearrange("o p c n -> (o p) c n")).then_inc(x_loaded, 16)
                pool.wait_ge(z_ready, i * DC + DC)
                pool.dma_start(z_dram[bass.ds(i * BT, BT)].rearrange("b p f -> p b f"),
                               zb[:].rearrange("p b c s -> p b (c s)")).then_inc(z_stored, 16)
                pool.wait_ge(z_stored, i * 16 + 16)
                pool.dma_start(xr[:], xT[bass.ds(i + 1, 1)].rearrange("o p c n -> (o p) c n")).then_inc(xr_loaded, 16)
            pool.wait_ge(z_ready, NT * DC)
            pool.dma_start(z_dram[(NT - 1) * BT:NT * BT].rearrange("b p f -> p b f"),
                           zb[:].rearrange("p b c s -> p b (c s)")).then_inc(z_stored, 16)

            pool.wait_ge(z_stored, NT * 16)
            nc.gpsimd.memset(mhalf[:], -0.5).then_inc(mhalf_s, 1)
            pool.wait_ge(mhalf_s, 1)

            def unit(n, slot, reuse):
                pool.wait_ge(ve_s, n + 1)
                if reuse:
                    pool.wait_ge(yn_s, n - 1)
                nc.gpsimd.tensor_tensor(rstd[:, slot:slot + 1], veps[:, slot:slot + 1], mhalf[:],
                                        ALU.pow).then_inc(rstd_s, 1)
                pool.wait_ge(rstd_s, n + 1)
                nc.gpsimd.tensor_tensor(nbias[:, slot:slot + 1], negm[:, slot:slot + 1], rstd[:, slot:slot + 1],
                                        ALU.mult).then_inc(nb_s, 1)
                b = pool.value_load(first_t[0:1, bass.ds(n, 1)], min_val=0, max_val=B - 1)
                dst = out[bass.ds(b, 1)].rearrange("o s d -> (o s) d")
                pool.wait_ge(yo_s, n + 1)
                pool.dma_start(dst, yo[0:S, slot, :]).then_inc(a_stored[slot], 16)

            pool.wait_ge(sorted_s, 3)
            unit(0, 0, False)
            unit(1, 1, False)
            with pool.Fori(0, LOOPS) as k:
                for u in range(UNROLL):
                    unit(k * UNROLL + (2 + u), u % 2, True)
            for n in range(LOOPS * UNROLL + 2, NPAIR):
                unit(n, n % 2, True)
            for s in range(2):
                pool.wait_ge(a_stored[s], 16 * ((NPAIR + 1 - s) // 2))

        @block.scalar
        def _(act):
            act.wait_ge(qw_loaded[0], 16)
            nc.scalar.copy(t_hi[:], x_st[:]).then_inc(qw_hi, 1)
            act.wait_ge(qw_loaded[1], 16)
            nc.scalar.copy(y_hi[:], xr[:]).then_inc(qw_hi, 1)
            act.wait_ge(qw_loaded[2], 16)
            nc.scalar.copy(a_hi[:], x_st[:]).then_inc(qw_hi, 1)
            act.wait_ge(qw_loaded[3], 16)
            nc.scalar.copy(c_hi[:], xr[:]).then_inc(qw_hi, 1)

            def split_w1(q, k):
                act.wait_ge(w1_loaded[k % W1_STAGE], (q - k % W1_STAGE) * (16 // W1_STAGE) + 16)
                nc.scalar.copy(w1_hi[:, k % W1_RING, :], w1_st[:, k % W1_STAGE, :]).then_inc(w1_hi_s, 1)

            def split_w2(n, k):
                act.wait_ge(w2_loaded[k % W2_RING], (n - k % W2_RING) * (16 // W2_RING) + 16)
                act.wait_ge(acc_mm, n - 1)
                nc.scalar.copy(w2_hi[:, k % W2_RING, :], w2_st[:, k % W2_RING, :]).then_inc(w2_hi_s, 1)

            def split_x(t, c):
                act.wait_ge(x_loaded, t * 16 + 16)
                nc.scalar.copy(x_hi[:, c, :], x_st[:, c, :]).then_inc(x_hi_s, 1)

            def softmax(m):
                act.wait_ge(nmx_s, m + 1)
                for k in range(2):
                    r = slice(k * S, (k + 1) * S)
                    ins = nc.scalar.activation(pe_[r, r], s_ps[r, r], ACT.Exp, bias=nmx[r, :], scale=SCALE,
                                               accum_out=rs[r, :])
                ins.then_inc(exp_s, 1)

            def split_xk(m, p):
                act.wait_ge(xk_loaded[p % 2], (m - p % 2) * 8 + 16)
                nc.scalar.copy(xk_hi[:], xk_st[:, p % 2, :]).then_inc(xk_hi_s, 1)

            def split_pt(m):
                act.wait_ge(pt_mm, m + 1)
                nc.scalar.copy(pt_hi[:], pt_ps).then_inc(pt_hi_s, 1)

            def split_y(m, p):
                act.wait_ge(y_mm, m + 1)
                nc.scalar.copy(y_hi[:, :, p * P:(p + 1) * P],
                               y_bank[:].rearrange("p (c n) -> p c n", c=DC)).then_inc(y_hi_s, 1)

            def attention(m, s):
                p = s // 4
                if s % 4 == 0:
                    softmax(m + p)
                if s % 4 == 1:
                    split_pt(m + p)
                    split_xk(m + p, p)
                if s % 4 == 2:
                    split_y(m + p, p)

            def stage_a(g, q, pos):
                for c in range(DC):
                    split_w1(q + c + W1_AHEAD, pos + c + W1_AHEAD)
                    act.wait_ge(h_mm, g + c + 1)
                    nc.scalar.activation(a_hi[:, c, :], hb[c % 2][:], ACT.Identity,
                                         bias=bcol(BP + c)).then_inc(h_hi_s, 1)

            def gelu(g, j, col):
                act.wait_ge(h_mm, g + j + 1)
                act.wait_ge(h_lo_s, g + j - 1)
                nc.scalar.activation(h_hi[:, j % 2, :], hb[j % 2][:], ACT.Gelu, bias=bcol(col + j))
                nc.scalar.activation(hf[:, j % 2, :], hb[j % 2][:], ACT.Gelu,
                                     bias=bcol(col + j)).then_inc(h_hi_s, 1)

            def stage_c(g, q, pos, n, x_next):
                for j in range(JH):
                    split_w1(q + j + W1_AHEAD, pos + j + W1_AHEAD)
                    gelu(g, j, CB1)
                    split_w2(n + j + 1, j + 1)
                    if 4 <= j < 4 + DC:
                        split_x(x_next, j - 4)

            def stage_m(g, q, pos, n, pair, last=False):
                for j in range(JH):
                    for k in (2 * j, 2 * j + 1):
                        if not last or k + W1_AHEAD < QM:
                            split_w1(q + k + W1_AHEAD, pos + k + W1_AHEAD)
                    gelu(g, j, MB1)
                    if not last or j + 1 < JH:
                        split_w2(n + j + 1, j + 1)
                    if pair is not None:
                        attention(pair, j)

            def cms_hi(t):
                for c in range(DC):
                    act.wait_ge(cf_s, t * DC + c + 1)
                    nc.scalar.copy(c_hi[:, c, :], cf[:, c % 2, :]).then_inc(c_hi_s, 1)

            for c in range(DC):
                split_x(0, c)
            for k in range(W1_AHEAD):
                split_w1(k, k)
            act.wait_ge(zero_p, 1)
            for c in range(DC):
                split_w1(c + W1_AHEAD, c + W1_AHEAD)
                act.wait_ge(h_mm, c + 1)
                nc.scalar.copy(t_hi[:, c, :], hb[c % 2][:]).then_inc(h_hi_s, 1)
            for s in range(JH):
                attention(0, s)
            stage_a(DC, QT, QT)
            act.wait_ge(w2_loaded[0], 16)
            nc.scalar.copy(w2_hi[:, 0, :], w2_st[:, 0, :]).then_inc(w2_hi_s, 1)
            for j in range(JH):
                split_w1(QT + QA + j + W1_AHEAD, j + W1_AHEAD)
                gelu(2 * DC, j, CB1)
                if j == 0:
                    act.wait_ge(w2_loaded[1], 16)
                    nc.scalar.copy(w2_hi[:, 1, :], w2_st[:, 1, :]).then_inc(w2_hi_s, 1)
                else:
                    split_w2(j + 1, j + 1)
                if 4 <= j < 4 + DC:
                    split_x(1, j - 4)
            with act.Fori(0, NT - 1) as i:
                g = i * G_ITER + G_PRE
                q = i * Q_ITER + Q_PRE
                n = i * (2 * JH) + JH
                split_w1(q + W1_AHEAD, W1_AHEAD)
                act.wait_ge(h_mm, g + 1)
                nc.scalar.copy(t_hi[:, 0, :], hb[0][:]).then_inc(h_hi_s, 1)
                for c in range(1, DC):
                    split_w1(q + c + W1_AHEAD, c + W1_AHEAD)
                    for e in ([0, 1] if c == 1 else [c]):
                        act.wait_ge(cf_s, i * DC + e + 1)
                        nc.scalar.copy(c_hi[:, e, :], cf[:, e % 2, :]).then_inc(c_hi_s, 1)
                    act.wait_ge(h_mm, g + c + 1)
                    nc.scalar.copy(t_hi[:, c, :], hb[c % 2][:]).then_inc(h_hi_s, 1)
                stage_m(g + DC, q + QT, QT, n, i * NP + NP)
                stage_a(g + DC + JH, q + QT + QM, QT + QM)
                stage_c(g + 2 * DC + JH, q + QT + QM + QA, 0, n + JH, i + 2)
            cms_hi(NT - 1)
            g, q, n = (NT - 1) * G_ITER + G_PRE, (NT - 1) * Q_ITER + Q_PRE, (NT - 1) * 2 * JH + JH
            stage_m(g, q, 0, n, None, last=True)

            act.wait_ge(l1_loaded, 64)
            for r in range(R):
                nc.scalar.copy(wd_hi[:, r], wd_f[:, r]).then_inc(l1_hi, 1)
                nc.scalar.copy(wu_hi[:, r], wu_f[:, r]).then_inc(l1_hi, 1)

            def split_z(n, slot):
                act.wait_ge(zl[slot], (n - slot) * 8 + 32)
                nc.scalar.copy(z_hi[:, slot].rearrange("p c (k s) -> p c k s", k=2),
                               zs[:, slot].rearrange("p k c s -> p c k s")).then_inc(zh_s, 1)

            def gelu_pair(n, slot):
                act.wait_ge(d_mm, n + 1)
                nc.scalar.activation(hs[:, slot, :], d_ps[slot][:, 0:KD], ACT.Gelu).then_inc(gelu_s, 1)

            def normalise(n, slot):
                act.wait_ge(nb_s, n + 1)
                nc.scalar.activation(yn[:, slot, :], u_ps[slot][:], ACT.Identity, bias=nbias[:, slot:slot + 1],
                                     scale=rstd[:, slot:slot + 1]).then_inc(yn_s, 1)

            def unit(n, u, z, d, norm):
                if z:
                    act.wait_ge(u_mm, n - 1)
                    split_z(n + 2, (u + 2) % 4)
                act.wait_ge(ht_mm, n + 1)
                nc.scalar.copy(ht_hi[:, u % 2, :], ht_ps[u % 2][:, 0:KD]).then_inc(ht_hi_s, 1)
                if d:
                    gelu_pair(n + 1, (u + 1) % 2)
                if norm:
                    normalise(n - 1, (u - 1) % 2)

            split_z(0, 0)
            split_z(1, 1)
            gelu_pair(0, 0)
            split_z(2, 2)
            unit(0, 0, False, True, False)
            split_z(3, 3)
            unit(1, 1, False, True, True)
            with act.Fori(0, LOOPS) as k:
                for u in range(UNROLL):
                    unit(k * UNROLL + (2 + u), 2 + u, True, True, True)
            for n in range(LOOPS * UNROLL + 2, NPAIR):
                unit(n, n % 4, n + 2 < NPAIR, n + 1 < NPAIR, True)
            normalise(NPAIR - 1, (NPAIR - 1) % 2)

        @block.vector
        def _(dve):
            nc.vector.memset(pe_[:], 0.0).then_inc(zero_p, 1)
            nc.vector.memset(ones[:], 1.0).then_inc(const_s, 1)
            dve.wait_ge(pool_c, 7)
            nc.vector.tensor_copy(ident_r[:], ident[:]).then_inc(const_s, 1)

            def split_projection(n, lo, hi, src):
                dve.wait_ge(qw_hi, n + 1)
                nc.vector.tensor_tensor(lo[:], src[:], f32(hi[:]), ALU.subtract).then_inc(qw_lo, 1)

            split_projection(0, t_lo, t_hi, x_st)
            split_projection(1, y_lo, y_hi, xr)
            split_projection(2, a_lo, a_hi, x_st)
            split_projection(3, c_lo, c_hi, xr)

            for m in range(2 * DC):
                dve.wait_ge(wa_mm, m + 1)
                if m >= 2:
                    dve.wait_ge(wa_stored[m % 2], 16 * (m // 2))
                nc.vector.tensor_copy(hf[:, m % 2, :], hb[m % 2][:]).then_inc(wa_out, 1)

            dve.wait_ge(const_in, 32)
            nc.vector.tensor_copy(tgt_f[:], tgt_i[:]).then_inc(const_s, 1)
            dve.wait_ge(const_s, 3)
            for c in range(DC):
                nc.vector.tensor_scalar(ohb[:, c, :], tgt_f[:], iota_p[:, c:c + 1], bcol(CB2 + c),
                                        ALU.is_equal, ALU.add).then_inc(ohb_s, 1)

            did = [0]

            def link(ins):
                did[0] += 1
                ins.then_inc(sort_v, 1)
                dve.wait_ge(sort_v, did[0])

            dve.wait_ge(sort_in, 16)
            link(nc.vector.tensor_copy(role_f[:], role_i[:]))
            link(nc.vector.tensor_scalar(role_f[:], role_f[:], 0.0, float(R - 1), ALU.max, ALU.min))
            link(nc.vector.tensor_copy(batch_f[:, 0:1], iota_p[0:B, 0:1]))
            link(nc.vector.memset(batch_f[:, 1:2], 1.0))
            link(nc.vector.tensor_copy(batch_f[:, 2:3], role_f[:]))
            link(nc.vector.tensor_scalar(onehot[:], iota_f[0:B, 0:R], role_f[:], None, ALU.is_equal))
            dve.wait_ge(sort_mm, 2)
            for r in range(R):
                link(nc.vector.tensor_scalar(flags[:], even[:], y_bank[0:B, R + r:R + r + 1], None, ALU.is_lt))
                link(nc.vector.reduce_sum(half[:, r:r + 1], flags[:], AX_X))
            link(nc.vector.memset(start[:, 0:1], 0.0))
            for r in range(1, R):
                link(nc.vector.scalar_tensor_tensor(out=start[:, r:r + 1], in0=half[:, r - 1:r], scalar=2.0,
                                                    in1=start[:, r - 1:r], op0=ALU.mult, op1=ALU.add))
            link(nc.vector.tensor_tensor(rank_r[:], y_bank[0:B, 0:R], start[:], ALU.add))
            link(nc.vector.tensor_tensor(rank_r[:], rank_r[:], onehot[:], ALU.mult))
            link(nc.vector.reduce_sum(rank[:], rank_r[:], AX_X))
            link(nc.vector.tensor_scalar(slot1[:], iota_f[0:B, :], rank[:], None, ALU.is_equal))
            dve.wait_ge(sort_mm, 3)
            link(nc.vector.tensor_copy(slots[:].rearrange("o v n k -> o (v n k)"), y_bank[0:1, 64:64 + 3 * NSLOT]))
            link(nc.vector.tensor_scalar(empty[:], slots[:, 1], -1.0, 1.0, ALU.mult, ALU.add))
            for v, w in ((0, 0), (2, 1)):
                link(nc.vector.tensor_scalar(fill[:, w], empty[:, :, 0], slots[:, v, 0, 0:1], None, ALU.mult))
                link(nc.vector.tensor_tensor(pick[:, w], fill[:, w], slots[:, v, :, 0], ALU.add))
            link(nc.vector.tensor_tensor(fill[:, 2], empty[:, :, 1], pick[:, 0], ALU.mult))
            link(nc.vector.tensor_tensor(pick[:, 2], fill[:, 2], slots[:, 0, :, 1], ALU.add))
            nc.vector.tensor_copy(first_t[:], pick[:, 0]).then_inc(sorted_s, 1)
            nc.vector.tensor_copy(role_t[:], pick[:, 1]).then_inc(sorted_s, 1)
            nc.vector.tensor_copy(second_t[:], pick[:, 2]).then_inc(sorted_s, 1)

            def split_w1(q, k):
                dve.wait_ge(w1_hi_s, q + 1)
                nc.vector.tensor_tensor(w1_lo[:, k % W1_RING, :], w1_st[:, k % W1_STAGE, :],
                                        f32(w1_hi[:, k % W1_RING, :]), ALU.subtract).then_inc(w1_lo_s, 1)

            def split_w2(n, k):
                dve.wait_ge(w2_hi_s, n + 1)
                nc.vector.tensor_tensor(w2_lo[:, k % W2_RING, :], w2_st[:, k % W2_RING, :],
                                        f32(w2_hi[:, k % W2_RING, :]), ALU.subtract).then_inc(w2_lo_s, 1)

            def split_x(t, c):
                dve.wait_ge(x_hi_s, t * DC + c + 1)
                nc.vector.tensor_tensor(x_lo[:, c, :], x_st[:, c, :], f32(x_hi[:, c, :]),
                                        ALU.subtract).then_inc(x_lo_s, 1)

            def row_max(m):
                dve.wait_ge(s_mm, m + 1)
                for k in range(2):
                    r = slice(k * S, (k + 1) * S)
                    ins = nc.vector.reduce_max(mx[r, :], s_ps[r, r], AX_X)
                    ins.then_inc(mx_s, 1)
                dve.wait_ge(mx_s, m * 2 + 2)
                nc.vector.tensor_scalar(nmx[:], mx[:], -SCALE, None, ALU.mult).then_inc(nmx_s, 1)

            def normalise_p(m):
                dve.wait_ge(exp_s, m + 1)
                nc.vector.reciprocal(rinv[:], rs[:]).then_inc(rinv_s, 1)
                dve.wait_ge(rinv_s, m + 1)
                nc.vector.tensor_scalar(pn[:], pe_[:], rinv[:], None, ALU.mult).then_inc(pn_s, 1)

            def split_xk(m, p):
                dve.wait_ge(xk_hi_s, m + 1)
                nc.vector.tensor_tensor(xk_lo[:], xk_st[:, p % 2, :], f32(xk_hi[:]),
                                        ALU.subtract).then_inc(xk_lo_s, 1)

            def split_pt(m):
                dve.wait_ge(pt_hi_s, m + 1)
                nc.vector.tensor_tensor(pt_lo[:], pt_ps, f32(pt_hi[:]), ALU.subtract).then_inc(pt_lo_s, 1)

            def split_y(m, p):
                dve.wait_ge(y_hi_s, m + 1)
                cols = slice(p * P, (p + 1) * P)
                nc.vector.tensor_tensor(y_lo[:, :, cols], y_bank[:].rearrange("p (c n) -> p c n", c=DC),
                                        f32(y_hi[:, :, cols]), ALU.subtract).then_inc(y_lo_s, 1)

            def attention(m, s):
                p = s // 4
                if s % 4 == 0:
                    row_max(m + p)
                    normalise_p(m + p)
                if s % 4 == 1:
                    split_pt(m + p)
                    split_xk(m + p, p)
                if s % 4 == 2:
                    split_y(m + p, p)

            def t_lo_half(g, c):
                dve.wait_ge(h_hi_s, g + c + 1)
                nc.vector.tensor_tensor(t_lo[:, c, :], hb[c % 2][:], f32(t_hi[:, c, :]),
                                        ALU.subtract).then_inc(h_lo_s, 1)

            def stage_a(g, q, pos, between=None):
                for c in range(DC):
                    split_w1(q + c + W1_AHEAD, pos + c + W1_AHEAD)
                    if between and c:
                        between(c - 1)
                    dve.wait_ge(h_hi_s, g + c + 1)
                    nc.vector.scalar_tensor_tensor(out=a_lo[:, c, :], in0=hb[c % 2][:], scalar=bcol(BP + c),
                                                   in1=f32(a_hi[:, c, :]), op0=ALU.add,
                                                   op1=ALU.subtract).then_inc(h_lo_s, 1)
                if between:
                    between(DC - 1)

            def h_lo_half(g, j):
                dve.wait_ge(h_hi_s, g + j + 1)
                nc.vector.tensor_tensor(h_lo[:, j % 2, :], hf[:, j % 2, :], f32(h_hi[:, j % 2, :]),
                                        ALU.subtract).then_inc(h_lo_s, 1)

            def stage_c(g, q, pos, n, x_next):
                for j in range(JH):
                    split_w1(q + j + W1_AHEAD, pos + j + W1_AHEAD)
                    h_lo_half(g, j)
                    split_w2(n + j + 1, j + 1)
                    if 4 <= j < 4 + DC:
                        split_x(x_next, j - 4)

            def stage_m(g, q, pos, n, pair, last=False):
                for j in range(JH):
                    for k in (2 * j, 2 * j + 1):
                        if not last or k + W1_AHEAD < QM:
                            split_w1(q + k + W1_AHEAD, pos + k + W1_AHEAD)
                    h_lo_half(g, j)
                    if not last or j + 1 < JH:
                        split_w2(n + j + 1, j + 1)
                    if pair is not None:
                        attention(pair, j)

            def batches(ap):
                return ap.rearrange("p (b s) -> p b s", s=S)

            def cms_f32(t, c, n_end, reuse=True):
                if c == 0:
                    dve.wait_ge(acc_mm, n_end)
                    dve.wait_ge(xr_loaded, t * 16 + 16)
                if reuse:
                    dve.wait_ge(c_lo_s, t * DC + c - 1)
                oh = ohb[:, c, bass.ds(t * BT, BT)]
                nc.vector.tensor_tensor(batches(cf[:, c % 2, :]), batches(acc[c][:]),
                                        oh.unsqueeze(2).to_broadcast([P, BT, S]),
                                        ALU.add).then_inc(cf_s, 1)
                dve.wait_ge(cf_s, t * DC + c + 1)
                nc.vector.tensor_tensor(xr[:, c, :], xr[:, c, :], cf[:, c % 2, :], ALU.add).then_inc(xr_sum, 1)

            def cms_lo(t, c):
                dve.wait_ge(c_hi_s, t * DC + c + 1)
                nc.vector.tensor_tensor(c_lo[:, c, :], cf[:, c % 2, :], f32(c_hi[:, c, :]),
                                        ALU.subtract).then_inc(c_lo_s, 1)

            def z_chunk(t, c, n_end):
                if c == 0:
                    dve.wait_ge(acc_mm, n_end)
                    dve.wait_ge(xr_sum, t * DC + DC)
                nc.vector.scalar_tensor_tensor(out=zt[:, c % 2, :], in0=acc[c][:], scalar=bcol(MB2 + c),
                                               in1=xr[:, c, :], op0=ALU.add, op1=ALU.add).then_inc(zt_s, 1)
                dve.wait_ge(zt_s, t * DC + c + 1)
                nc.vector.tensor_scalar(zb[:, :, c, :], batches(zt[:, c % 2, :]), 0.0, 1.0,
                                        ALU.max, ALU.min).then_inc(z_ready, 1)

            for c in range(DC):
                split_x(0, c)
            for k in range(W1_AHEAD):
                split_w1(k, k)
            for c in range(DC):
                split_w1(c + W1_AHEAD, c + W1_AHEAD)
                t_lo_half(0, c)
            for s in range(JH):
                attention(0, s)
            stage_a(DC, QT, QT)
            split_w2(0, 0)
            stage_c(2 * DC, QT + QA, 0, 0, 1)
            dve.wait_ge(ohb_s, DC)
            with dve.Fori(0, NT - 1) as i:
                g = i * G_ITER + G_PRE
                q = i * Q_ITER + Q_PRE
                n = i * (2 * JH) + JH
                split_w1(q + W1_AHEAD, W1_AHEAD)
                t_lo_half(g, 0)
                cms_f32(i, 0, n, reuse=False)
                cms_f32(i, 1, n, reuse=False)
                split_w1(q + 1 + W1_AHEAD, 1 + W1_AHEAD)
                cms_lo(i, 0)
                cms_f32(i, 2, n)
                cms_lo(i, 1)
                t_lo_half(g, 1)
                cms_f32(i, 3, n)
                split_w1(q + 2 + W1_AHEAD, 2 + W1_AHEAD)
                cms_lo(i, 2)
                t_lo_half(g, 2)
                split_w1(q + 3 + W1_AHEAD, 3 + W1_AHEAD)
                cms_lo(i, 3)
                t_lo_half(g, 3)
                stage_m(g + DC, q + QT, QT, n, i * NP + NP)
                qa, ga = q + QT + QM, g + DC + JH
                stage_a(ga, qa, QT + QM, between=lambda c: z_chunk(i, c, n + JH))
                stage_c(ga + DC, qa + QA, 0, n + JH, i + 2)
            g, q, n = (NT - 1) * G_ITER + G_PRE, (NT - 1) * Q_ITER + Q_PRE, (NT - 1) * 2 * JH + JH
            for c in range(DC):
                cms_f32(NT - 1, c, n, reuse=c >= 2)
                if c:
                    cms_lo(NT - 1, c - 1)
            cms_lo(NT - 1, DC - 1)
            stage_m(g, q, 0, n, None, last=True)
            for c in range(DC):
                z_chunk(NT - 1, c, n + JH)

            dve.wait_ge(l1_loaded, 64)
            nc.vector.tensor_copy(brow[0:1], brow_f[:]).then_inc(row_hi, 1)
            dve.wait_ge(row_hi, 1)
            nc.vector.tensor_tensor(brow_lo[:], brow_f[:], f32(brow[0:1]), ALU.subtract).then_inc(row_lo, 1)
            nc.vector.memset(ones2f[:], 1.0).then_inc(ones_s, 1)
            dve.wait_ge(ones_s, 1)
            nc.vector.tensor_copy(ones2[:], ones2f[:]).then_inc(ones_s, 1)
            for r in range(R):
                dve.wait_ge(l1_hi, 2 * r + 1)
                nc.vector.tensor_tensor(wd_lo[:, r], wd_f[:, r], f32(wd_hi[:, r]), ALU.subtract).then_inc(l1_lo, 1)
                dve.wait_ge(l1_hi, 2 * r + 2)
                nc.vector.tensor_tensor(wu_lo[:, r], wu_f[:, r], f32(wu_hi[:, r]), ALU.subtract).then_inc(l1_lo, 1)

            def split_z(n, slot, stats_of=None):
                if stats_of is not None:
                    dve.wait_ge(st_s, stats_of + 1)
                dve.wait_ge(zh_s, n + 1)
                nc.vector.tensor_tensor(z_lo[:, slot].rearrange("p c (k s) -> p c k s", k=2),
                                        zs[:, slot].rearrange("p k c s -> p c k s"),
                                        f32(z_hi[:, slot]).rearrange("p c (k s) -> p c k s", k=2),
                                        ALU.subtract).then_inc(zl_s, 1)

            def stats(n, slot):
                dve.wait_ge(u_mm, n + 1)
                nc.vector.bn_stats(st6[:], u_ps[slot][:]).then_inc(st_s, 1)

            def moments(n, slot):
                nc.vector.bn_aggr(mv[:], st6[:]).then_inc(mv_s, 1)
                dve.wait_ge(mv_s, n + 1)
                nc.vector.tensor_scalar(negm[:, slot:slot + 1], mv[:, 0:1], -1.0, None, ALU.mult)
                nc.vector.tensor_scalar(veps[:, slot:slot + 1], mv[:, 1:2], LN_EPS, None, ALU.add).then_inc(ve_s, 1)

            def scale_shift(n, slot, reuse):
                r = dve.value_load(role_t[0:1, bass.ds(n, 1)], min_val=0, max_val=R - 1)
                dve.wait_ge(yn_s, n + 1)
                nc.vector.tensor_tensor(yg[:, slot, :], yn[:, slot, :],
                                        gam[:, bass.ds(r, 1), :].rearrange("p o d -> p (o d)"),
                                        ALU.mult).then_inc(yg_s, 1)
                if reuse:
                    dve.wait_ge(a_stored[slot], (n - slot) * 8)
                    dve.wait_ge(b_stored[slot], (n - slot) * 8)
                dve.wait_ge(yg_s, n + 1)
                nc.vector.tensor_tensor(yo[:, slot, :], yg[:, slot, :],
                                        bet[:, bass.ds(r, 1), :].rearrange("p o d -> p (o d)"),
                                        ALU.add).then_inc(yo_s, 1)

            def unit(n, u, z, tail, reuse):
                if tail:
                    stats(n - 1, (u - 1) % 2)
                if z:
                    split_z(n + 2, (u + 2) % 4, n - 1 if tail else None)
                elif tail:
                    dve.wait_ge(st_s, n)
                if tail:
                    moments(n - 1, (u - 1) % 2)
                dve.wait_ge(ht_hi_s, n + 1)
                nc.vector.tensor_tensor(ht_lo[:, u % 2, :], ht_ps[u % 2][:, 0:KD], f32(ht_hi[:, u % 2, :]),
                                        ALU.subtract).then_inc(ht_lo_s, 1)
                if tail:
                    scale_shift(n - 1, (u - 1) % 2, reuse)

            split_z(0, 0)
            split_z(1, 1)
            dve.wait_ge(gb_loaded, 32)
            unit(0, 0, True, False, False)
            unit(1, 1, True, True, False)
            unit(2, 2, True, True, False)
            with dve.Fori(0, LOOPS) as k:
                for u in range(UNROLL):
                    unit(k * UNROLL + (3 + u), 3 + u, True, True, True)
            for n in range(LOOPS * UNROLL + 3, NPAIR):
                unit(n, n % 4, n + 2 < NPAIR, True, True)
            stats(NPAIR - 1, (NPAIR - 1) % 2)
            dve.wait_ge(st_s, NPAIR)
            moments(NPAIR - 1, (NPAIR - 1) % 2)
            scale_shift(NPAIR - 1, (NPAIR - 1) % 2, True)

        @block.tensor
        def _(pe):
            def mm3(ps, w, x, first, last):
                nc.tensor.matmul(ps, w[0], x[0], start=first, stop=False)
                nc.tensor.matmul(ps, w[0], x[1], start=False, stop=False)
                return nc.tensor.matmul(ps, w[1], x[0], start=False, stop=last)

            def chunk(pair, k, cols):
                return [half[:, k, cols] for half in pair]

            ALL = slice(0, TOK)

            def w1_block(k, c):
                cols = slice(c * P, (c + 1) * P)
                return w1_hi[:, k % W1_RING, cols], w1_lo[:, k % W1_RING, cols]

            for m, (lhs, rhs) in enumerate([((t_hi, t_lo), (y_hi, y_lo))] * DC + [((a_hi, a_lo), (c_hi, c_lo))] * DC):
                pe.wait_ge(qw_lo, 2 if m < DC else 4)
                if m >= 2:
                    pe.wait_ge(wa_out, m - 1)
                rows = slice((m % DC) * P, (m % DC + 1) * P)
                for k in range(DC):
                    ins = mm3(hb[m % 2][:], chunk(lhs, k, rows), chunk(rhs, k, ALL), k == 0, k == DC - 1)
                ins.then_inc(wa_mm, 1)

            pe.wait_ge(const_s, 2)
            pe.wait_ge(sort_v, 6)
            nc.tensor.matmul(y_bank[0:B, 0:R], before[:], onehot[:], start=True, stop=True).then_inc(sort_mm, 1)
            nc.tensor.matmul(y_bank[0:B, R:2 * R], ones[:], onehot[:], start=True, stop=True).then_inc(sort_mm, 1)
            pe.wait_ge(sort_v, 6 + 2 * R + 1 + (R - 1) + 4)
            for v in range(3):
                ins = nc.tensor.matmul(y_bank[0:1, 64 + v * NSLOT:64 + (v + 1) * NSLOT], batch_f[:, v:v + 1],
                                       slot1[:], start=True, stop=True)
            ins.then_inc(sort_mm, 1)
            pe.wait_ge(sorted_s, 3)
            pe.wait_ge(wa_out, 2 * DC)

            def project(g, q, c, w, x, own_bank=True):
                pe.wait_ge(w1_lo_s, q + c + 1)
                if own_bank:
                    pe.wait_ge(h_lo_s, g + c - 1)
                for k in range(DC):
                    ins = mm3(hb[c % 2][:], w1_block(w + c, k), chunk(x, k, ALL), k == 0, k == DC - 1)
                ins.then_inc(h_mm, 1)

            def half_step(q, pos, bank, kq, x, first, last):
                pe.wait_ge(w1_lo_s, q + kq + 1)
                for k in range(DC):
                    ins = mm3(hb[bank][:], w1_block(pos + kq, k), chunk(x, k, ALL), first and k == 0, last and k == DC - 1)
                if last:
                    ins.then_inc(h_mm, 1)

            def second_layer(g_next, n, j, free=None):
                pe.wait_ge(w2_lo_s, n + j + 1)
                pe.wait_ge(h_lo_s, g_next)
                if free is not None:
                    pe.wait_ge(*free)
                for c in range(DC):
                    cols = slice(c * P, (c + 1) * P)
                    ins = mm3(acc[c][:], (w2_hi[:, j % W2_RING, cols], w2_lo[:, j % W2_RING, cols]),
                              (h_hi[:, j % 2, :], h_lo[:, j % 2, :]), j == 0, j == JH - 1)
                ins.then_inc(acc_mm, 1)

            def scores(m, p):
                cols = slice(p * P, (p + 1) * P)
                for k in range(DC):
                    ins = mm3(s_ps, chunk((t_hi, t_lo), k, cols), chunk((x_hi, x_lo), k, cols), k == 0, k == DC - 1)
                ins.then_inc(s_mm, 1)

            def attention(m, s):
                p = s // 4
                if s % 4 == 0:
                    scores(m + p, p)
                if s % 4 == 1:
                    pe.wait_ge(pn_s, m + p + 1)
                    nc.tensor.transpose(pt_ps, pn[:], ident[:]).then_inc(pt_mm, 1)
                if s % 4 == 2:
                    pe.wait_ge(pt_lo_s, m + p + 1)
                    pe.wait_ge(xk_lo_s, m + p + 1)
                    if not isinstance(m, int) or m + p:
                        pe.wait_ge(y_lo_s, m + p)
                    for c in range(DC):
                        cols = slice(c * P, (c + 1) * P)
                        ins = mm3(y_bank[:, cols], (xk_hi[:, cols], xk_lo[:, cols]), (pt_hi[:], pt_lo[:]), True, True)
                    ins.then_inc(y_mm, 1)

            def stage_c(g, q, n, free):
                for j in range(JH):
                    half_step(q, 0, j % 2, j, (a_hi, a_lo), True, True)
                    if j:
                        second_layer(g + j, n, j - 1, free if j == 1 else None)

            def stage_m(g, q, pos, n, t, pair, flush=None):
                pe.wait_ge(h_lo_s, g - 1)
                half_step(q, pos, 0, 0, (a_hi, a_lo), True, False)
                if flush:
                    flush()
                pe.wait_ge(h_lo_s, g)
                half_step(q, pos, 1, 2, (a_hi, a_lo), True, False)
                pe.wait_ge(c_lo_s, t * DC + DC)
                half_step(q, pos, 0, 1, (c_hi, c_lo), False, True)
                if pair is not None:
                    attention(pair, 0)
                half_step(q, pos, 1, 3, (c_hi, c_lo), False, True)
                second_layer(g + 1, n, 0, (cf_s, t * DC + DC))
                if pair is not None:
                    attention(pair, 1)
                for j in range(2, JH):
                    half_step(q, pos, j % 2, 2 * j, (a_hi, a_lo), True, False)
                    half_step(q, pos, j % 2, 2 * j + 1, (c_hi, c_lo), False, True)
                    second_layer(g + j, n, j - 1)
                    if pair is not None:
                        attention(pair, j)

            pe.wait_ge(x_lo_s, DC)
            for c in range(DC):
                project(0, 0, c, 0, (x_hi, x_lo), own_bank=c >= 2)
            pe.wait_ge(h_lo_s, DC)
            for s in range(JH):
                attention(0, s)
            pe.wait_ge(y_lo_s, NP)
            for c in range(DC):
                project(DC, QT, c, QT, (y_hi, y_lo))
            pe.wait_ge(h_lo_s, 2 * DC)
            stage_c(2 * DC, QT + QA, 0, None)
            with pe.Fori(0, NT - 1) as i:
                g = i * G_ITER + G_PRE
                q = i * Q_ITER + Q_PRE
                n = i * (2 * JH) + JH
                pe.wait_ge(x_lo_s, i * DC + 2 * DC)
                project(g, q, 0, 0, (x_hi, x_lo))
                second_layer(g, n - JH, JH - 1)
                for c in range(1, DC):
                    project(g, q, c, 0, (x_hi, x_lo))
                stage_m(g + DC, q + QT, QT, n, i, i * NP + NP)
                ga, qa = g + DC + JH, q + QT + QM
                pe.wait_ge(y_lo_s, i * NP + 2 * NP)
                project(ga, qa, 0, QT + QM, (y_hi, y_lo))
                second_layer(ga, n, JH - 1)
                for c in range(1, DC):
                    project(ga, qa, c, QT + QM, (y_hi, y_lo))
                pe.wait_ge(h_lo_s, ga + DC)
                stage_c(ga + DC, qa + QA, n + JH, (zt_s, i * DC + DC))
            g, q, n = (NT - 1) * G_ITER + G_PRE, (NT - 1) * Q_ITER + Q_PRE, (NT - 1) * 2 * JH + JH
            stage_m(g, q, 0, n, NT - 1, None, flush=lambda: second_layer(g, n - JH, JH - 1))
            second_layer(g + JH, n, JH - 1)

            pe.wait_ge(z_ready, NT * DC)
            pe.wait_ge(l1_lo, 2 * R)
            pe.wait_ge(ones_s, 2)
            pe.wait_ge(row_in, 16)
            pe.wait_ge(sorted_s, 3)

            def pair_role(n):
                return pe.value_load(role_t[0:1, bass.ds(n, 1)], min_val=0, max_val=R - 1)

            def rows(ap, r):
                return ap[:, bass.ds(r, 1)].rearrange("p o n -> p (o n)")

            def down(n, u):
                r = pair_role(n)
                pe.wait_ge(zl_s, n + 1)
                ps = d_ps[u % 2][:, 0:KD]
                nc.tensor.matmul(ps, ones2[:], rows(brow[:, :, 0:KD], r), start=True, stop=False)
                for k in range(DC):
                    w = [rows(half[:, :, k, :], r) for half in (wd_hi, wd_lo)]
                    ins = mm3(ps, (z_hi[:, u % 4, k, :], z_lo[:, u % 4, k, :]), w, False, k == DC - 1)
                ins.then_inc(d_mm, 1)

            def up(n, u, reuse):
                r = pair_role(n)
                pe.wait_ge(gelu_s, n + 1)
                for k in range(KD // P):
                    ins = nc.tensor.transpose(ht_ps[u % 2][:, k * P:(k + 1) * P], hs[:, u % 2, k * P:(k + 1) * P],
                                              ident[:])
                ins.then_inc(ht_mm, 1)
                ps = u_ps[u % 2]
                if reuse:
                    pe.wait_ge(yn_s, n - 1)
                nc.tensor.matmul(ps[:], ones2[:], rows(brow[:, :, KD:KD + D], r), start=True, stop=False)
                for k in range(DC):
                    for z in (z_hi, z_lo):
                        nc.tensor.matmul(ps[:, k * P:(k + 1) * P], z[:, u % 4, k, :], ident_r[:], start=False,
                                         stop=False)
                pe.wait_ge(ht_lo_s, n + 1)
                for k in range(KD // P):
                    w = [rows(half[:, :, k, :], r) for half in (wu_hi, wu_lo)]
                    cols = slice(k * P, (k + 1) * P)
                    ins = mm3(ps[:], (ht_hi[:, u % 2, cols], ht_lo[:, u % 2, cols]), w, False, k == KD // P - 1)
                ins.then_inc(u_mm, 1)

            down(0, 0)
            for n in range(2):
                down(n + 1, n + 1)
                up(n, n, False)
            with pe.Fori(0, LOOPS) as k:
                for u in range(UNROLL):
                    n = k * UNROLL + (2 + u)
                    down(n + 1, 3 + u)
                    up(n, 2 + u, True)
            for n in range(LOOPS * UNROLL + 2, NPAIR):
                if n + 1 < NPAIR:
                    down(n + 1, n + 1)
                up(n, n, True)


def kernel(**inputs):
    import numpy as np
    import concourse.bacc as bacc
    from concourse.bass_utils import run_bass_kernel_spmd

    a = {k.removeprefix("L0_cond_").removeprefix("L1_cond_"): np.asarray(v) for k, v in inputs.items()}

    def rows(w):
        return w.reshape(-1, P, w.shape[-1]).transpose(1, 0, 2)

    def blocks(w):
        k, n = w.shape
        return w.reshape(k // D, DC, P, n // P, P).transpose(3, 0, 2, 1, 4).reshape(-1, P, D)

    x = a["x"].reshape(NT, TOK, DC, P)
    arrays = {
        "xT": x.transpose(0, 3, 2, 1),
        "xk": a["x"].reshape(NT * NP, P, D),
        "w1c": blocks(a["cW1"]),
        "w1m": blocks(a["mW1"]),
        "w2c": a["cW2"].reshape(JH, P, D),
        "w2m": a["mW2"].reshape(JH, P, D),
        "wqT": rows(a["Wq"].T),
        "wkT": rows(a["Wk"].T),
        "wvT": rows(a["Wv"].T),
        "wp": rows(a["Wp"]),
        "bias": np.concatenate([a[n].reshape(-1, P).T for n in ("cb1", "mb1", "bp", "cb2", "mb2")], axis=1),
        "target": a["itok_B_17_1546"].reshape(1, B),
        "role": a["itok_B_1_2"].reshape(B, 1),
        "wd": a["W_down"].reshape(R, DC, P, KD).transpose(2, 0, 1, 3),
        "wu": a["W_up"].reshape(R, KD // P, P, D).transpose(2, 0, 1, 3),
        "bd": a["b_down"].reshape(1, R, KD),
        "bu": a["b_up"].reshape(1, R, D),
        "gamma": a["gamma"].reshape(1, R, D),
        "beta": a["beta"].reshape(1, R, D),
    }
    arrays = {n: np.ascontiguousarray(v) for n, v in arrays.items()}
    nc = bacc.Bacc("TRN2", target_bir_lowering=False, num_devices=1)
    args = [nc.dram_tensor(n, v.shape, mybir.dt.from_np(v.dtype), kind="ExternalInput").ap() for n, v in arrays.items()]
    out = nc.dram_tensor("out", (B, S, D), F32, kind="ExternalOutput").ap()
    program(nc, *args, out)
    r = run_bass_kernel_spmd(nc, [arrays], core_ids=[0])
    return r.results[0]["out"]
```

```python
from contextlib import ExitStack

import concourse.bass as bass
from concourse import mybir

P = 128
F32 = mybir.dt.float32
F32R = mybir.dt.float32r
I32 = mybir.dt.int32
ALU = mybir.AluOpType
ACT = mybir.ActivationFunctionType
AX_X = mybir.AxisListType.X

B, S, D = 64, 64, 512
H = 4 * D
R, KD = 3, 256
TOK = 512
NT = B * S // TOK
BT = TOK // S
DC = D // P
JH = H // P
NP = TOK // P
SCALE = float(D) ** -0.5
LN_EPS = 1e-5

W1_STAGE, W1_RING, W2_RING = 4, 8, 2
W1_AHEAD = 4
QT, QA, QC, QM = DC, DC, JH, 2 * JH
Q_PRE = QT + QA + QC
Q_ITER = QT + QM + QA + QC
G_PRE = DC + DC + JH
G_ITER = DC + JH + DC + JH

NPAIR = B // 2 + (R - 1) // 2
NSLOT = 2 * NPAIR
UNROLL = 4
LOOPS = (NPAIR - 2) // UNROLL

CB1, MB1, BP, CB2, MB2 = 0, JH, 2 * JH, 2 * JH + DC, 2 * JH + 2 * DC
NBIAS = 2 * JH + 3 * DC


def program(nc, xT, xk, w1c, w1m, w2c, w2m, wqT, wkT, wvT, wp, bias, target, role,
            wd, wu, bd, bu, gamma, beta, out):
    wa_dram = nc.dram_tensor("wa_blocks", (2 * DC, P, D), F32).ap()
    z_dram = nc.dram_tensor("z_by_batch", (B, P, DC * S), F32).ap()

    ctx = ExitStack()
    with ctx:
        def sb(name, shape, dt=F32, on=ctx):
            return on.enter_context(nc.sbuf_tensor(name, shape, dt))

        def sem(name):
            return ctx.enter_context(nc.semaphore(name))

        def hl(name, shape, on=ctx):
            return sb(name + "_hi", shape, F32R, on), sb(name + "_lo", shape, F32R, on)

        bias_sb = sb("bias_sb", [P, NBIAS])
        ident = sb("ident", [P, P])
        ident_r = sb("ident_r", [P, P], F32R)
        iota_p = sb("iota_p", [P, DC])
        iota_f = sb("iota_f", [P, NSLOT])
        ohb = sb("ohb", [P, DC, B])
        first_t = sb("first_t", [1, NPAIR], I32)
        second_t = sb("second_t", [1, NPAIR], I32)
        role_t = sb("role_t", [1, NPAIR], I32)

        brow = sb("brow", [2, R, KD + D], F32R)
        ones2f = sb("ones2f", [2, P])
        ones2 = sb("ones2", [2, P], F32R)

        early = ExitStack()
        x_st = sb("x_st", [P, DC, TOK], on=early)
        x_hi, x_lo = hl("x", [P, DC, TOK], early)
        xk_st = sb("xk_st", [P, 2, D], on=early)
        xk_hi, xk_lo = hl("xk", [P, D], early)
        t_hi, t_lo = hl("t", [P, DC, TOK], early)
        y_hi, y_lo = hl("y", [P, DC, TOK], early)

        with ExitStack() as rows_made:
            brow_f = sb("brow_f", [1, R, KD + D], on=rows_made)
            brow_lo = sb("brow_lo", [1, R, KD + D], F32R, rows_made)

        main = ExitStack()
        zt = sb("zt", [P, 2, TOK], on=main)
        h_hi, h_lo = hl("h", [P, 2, TOK], main)
        w2_hi, w2_lo = hl("w2", [P, W2_RING, D], main)
        cf = sb("cf", [P, DC, TOK], on=main)
        w2_st = sb("w2_st", [P, W2_RING, D], on=main)
        w1_st = sb("w1_st", [P, W1_STAGE, D], on=main)
        w1_hi, w1_lo = hl("w1", [P, W1_RING, D], main)
        a_hi, a_lo = hl("a", [P, DC, TOK], main)
        c_hi, c_lo = hl("c", [P, DC, TOK], main)
        xr = sb("xr", [P, DC, TOK], on=main)
        zb = sb("zb", [P, BT, DC, S], on=main)
        hf = sb("hf", [P, 2, TOK], on=main)
        mx = sb("mx", [P, 1], on=main)
        nmx = sb("nmx", [P, 1], on=main)
        rs = sb("rs", [P, 1], on=main)
        rinv = sb("rinv", [P, 1], on=main)
        pe_ = sb("p_exp", [P, P], on=main)
        pn = sb("p_norm", [P, P], on=main)
        pt_hi, pt_lo = hl("pt", [P, P], main)
        tgt_i = sb("tgt_i", [P, B], I32, main)
        tgt_f = sb("tgt_f", [P, B], on=main)
        role_i = sb("role_i", [B, 1], I32, main)
        role_f = sb("role_f", [B, 1], on=main)
        batch_f = sb("batch_f", [B, 3], on=main)
        onehot = sb("onehot", [B, R], on=main)
        before = sb("before", [B, B], on=main)
        ones = sb("ones", [B, B], on=main)
        even = sb("even", [B, B // 2], on=main)
        flags = sb("flags", [B, B // 2], on=main)
        half = sb("half", [B, R], on=main)
        start = sb("start", [B, R], on=main)
        rank_r = sb("rank_r", [B, R], on=main)
        rank = sb("rank", [B, 1], on=main)
        slot1 = sb("slot1", [B, NSLOT], on=main)
        slots = sb("slots", [1, 3, NPAIR, 2], on=main)
        empty = sb("empty", [1, NPAIR, 2], on=main)
        fill = sb("fill", [1, 3, NPAIR], on=main)
        pick = sb("pick", [1, 3, NPAIR], on=main)
        main.close()
        early.close()

        wd_hi, wd_lo = hl("wd", [P, R, DC, KD])
        wu_hi, wu_lo = hl("wu", [P, R, KD // P, D])
        l1_st = sb("l1_st", [P, R, DC * KD])
        sb("fence", [P, D])
        gam = sb("gam", [P, R, D])
        bet = sb("bet", [P, R, D])
        zs = sb("zs", [P, 4, 2, DC, S])
        z_hi, z_lo = hl("z", [P, 4, DC, P])
        hs = sb("hs", [P, 2, KD])
        ht_hi, ht_lo = hl("ht", [P, 2, KD])
        st6 = sb("st6", [P, 6])
        mv = sb("mv", [P, 2])
        veps = sb("veps", [P, 2])
        negm = sb("negm", [P, 2])
        mhalf = sb("mhalf", [P, 1])
        rstd = sb("rstd", [P, 2])
        nbias = sb("nbias", [P, 2])
        yn = sb("yn", [P, 2, D])
        yg = sb("yg", [P, 2, D])
        yo = sb("yo", [P, 2, D])

        def bank(name):
            return ctx.enter_context(nc.psum_tensor(name, [P, 512], F32))

        hb = [bank("hb0"), bank("hb1")]
        acc = [bank(f"acc{c}") for c in range(DC)]
        sp_bank = bank("scores")
        y_bank = bank("yb")
        s_ps = sp_bank[:, 0:P]
        pt_ps = sp_bank[:, P:2 * P]
        d_ps = hb
        ht_ps = [sp_bank, y_bank]
        u_ps = acc

        w1_loaded = [sem(f"w1_loaded{k}") for k in range(W1_STAGE)]
        w2_loaded = [sem(f"w2_loaded{k}") for k in range(W2_RING)]
        w1_hi_s, w1_lo_s = sem("w1_hi_split"), sem("w1_lo_split")
        w2_hi_s, w2_lo_s = sem("w2_hi_split"), sem("w2_lo_split")
        h_mm = sem("h_mm")
        h_hi_s, h_lo_s = sem("h_hi_ready"), sem("h_lo_ready")
        acc_mm = sem("acc_mm")
        x_loaded, x_hi_s, x_lo_s = sem("x_loaded"), sem("x_hi_split"), sem("x_lo_split")
        xk_loaded = [sem("xk_loaded0"), sem("xk_loaded1")]
        xk_hi_s, xk_lo_s = sem("xk_hi_split"), sem("xk_lo_split")
        s_mm, mx_s, nmx_s, exp_s = sem("scores_mm"), sem("row_max"), sem("neg_max"), sem("exp_done")
        rinv_s, pn_s = sem("row_inverse"), sem("p_normalised")
        pt_mm, pt_hi_s, pt_lo_s = sem("pt_mm"), sem("pt_hi_ready"), sem("pt_lo_ready")
        y_mm, y_hi_s, y_lo_s = sem("y_mm"), sem("y_hi_ready"), sem("y_lo_ready")
        cf_s, c_hi_s, c_lo_s = sem("cms_f32"), sem("cms_hi_ready"), sem("cms_lo_ready")
        xr_loaded, xr_sum = sem("xr_loaded"), sem("xr_summed")
        zt_s, z_ready, z_stored = sem("z_unclipped"), sem("z_ready"), sem("z_stored")
        const_in, const_s, pool_c = sem("constants_loaded"), sem("dve_constants"), sem("pool_constants")
        ohb_s, zero_p = sem("onehot_bias"), sem("p_exp_zeroed")
        qk_loaded = [sem(f"wq_wk_loaded{k}") for k in range(DC)]
        wv_loaded, wp_loaded = sem("wv_loaded"), sem("wp_loaded")
        qw_hi, qw_lo = sem("projection_hi"), sem("projection_lo")
        wa_mm, wa_out, wa_stored = sem("product_mm"), sem("product_out"), sem("product_stored")
        sort_in, sort_v, sort_mm, sorted_s = sem("roles_loaded"), sem("sort_vector"), sem("sort_mm"), sem("order_ready")
        l1_loaded, l1_hi, l1_lo = [sem("down_loaded"), sem("up_loaded")], sem("adapter_hi"), sem("adapter_lo")
        rows_loaded = sem("bias_rows_loaded")
        row_hi, row_lo, row_in = sem("bias_row_hi"), sem("bias_row_lo"), sem("bias_row_moved")
        gb_loaded, ones_s, mhalf_s = sem("gamma_beta_loaded"), sem("ones_ready"), sem("minus_half")
        zl = [sem(f"z_loaded{k}") for k in range(4)]
        zh_s, zl_s = sem("z_hi_split"), sem("z_lo_split")
        d_mm, gelu_s, ht_mm, ht_hi_s, ht_lo_s = sem("down_mm"), sem("gelu_done"), sem("ht_mm"), sem("ht_hi_ready"), sem("ht_lo_ready")
        u_mm, st_s, mv_s, ve_s = sem("up_mm"), sem("stats"), sem("mean_var"), sem("var_eps")
        rstd_s, nb_s, yn_s, yg_s, yo_s = sem("rstd"), sem("neg_mean_rstd"), sem("normalised"), sem("times_gamma"), sem("row_ready")
        a_stored = [sem("first_stored0"), sem("first_stored1")]
        b_stored = [sem("second_stored0"), sem("second_stored1")]

        zb_rows = zb[:].rearrange("p b c s -> p (b c s)").rearrange("p (k n) -> p k n", k=DC)

        def f32(ap):
            return ap.bitcast(F32)

        def bcol(col):
            return bias_sb[:, col:col + 1]

        block = ctx.enter_context(nc.Block())

        @block.sync
        def _(sp):
            for k in range(DC):
                sp.dma_start(x_st[:, k, :], wqT[:, k, :]).then_inc(qk_loaded[k], 16)
                sp.dma_start(zb_rows[:, k, :], wkT[:, k, :]).then_inc(qk_loaded[k], 16)
            sp.dma_start(brow_f[:, :, 0:KD], bd).then_inc(rows_loaded, 16)
            sp.dma_start(brow_f[:, :, KD:KD + D], bu).then_inc(rows_loaded, 16)
            sp.dma_start(role_i[:], role).then_inc(sort_in, 16)
            sp.dma_start(bias_sb[:], bias).then_inc(const_in, 16)
            sp.dma_start(tgt_i[:], target.to_broadcast([P, B])).then_inc(const_in, 16)
            sp.dma_start(xr[:], wvT).then_inc(wv_loaded, 16)
            sp.wait_ge(qw_lo, 2 * DC)
            sp.dma_start(zb_rows, wp).then_inc(wp_loaded, 16)
            sp.wait_ge(row_lo, 1)
            sp.dma_start(f32(brow[1:2]), f32(brow_lo[:])).then_inc(row_in, 16)
            for k in range(2):
                sp.wait_ge(wa_out, DC * (k + 1))
                sp.dma_start(wa_dram[k * DC:(k + 1) * DC].rearrange("j p n -> p j n"), w1_st[:]).then_inc(wa_stored, 16)
            sp.wait_ge(wa_stored, 32)

            def load_w1(q, k, src, reuse=True):
                if reuse:
                    sp.wait_ge(w1_lo_s, q - (W1_STAGE - 1))
                sp.dma_start(w1_st[:, k % W1_STAGE, :], src).then_inc(w1_loaded[k % W1_STAGE], 16)

            def load_w2(n, k, src, reuse=True):
                if reuse:
                    sp.wait_ge(w2_lo_s, n - (W2_RING - 1))
                sp.dma_start(w2_st[:, k % W2_RING, :], src).then_inc(w2_loaded[k % W2_RING], 16)

            def head(q, n_end, src, w2_last, w2_next):
                for c in range(W1_AHEAD):
                    load_w1(q + c, c, src[c])
                    if w2_last is w2c:
                        load_w2(n_end - 3 + c, JH - 3 + c, w2_last[JH - 3 + c] if c < 3 else w2_next[0])
                    elif c % 2:
                        load_w2(n_end - 1 + c // 2, JH - 1 + c // 2, w2_last[JH - 1] if c == 1 else w2_next[0])

            def body_m(q, n):
                for k in range(W1_AHEAD, QM):
                    load_w1(q + k, k, w1m[k])
                    if k % 2:
                        j = (k - W1_AHEAD) // 2 + 1
                        load_w2(n + j, j, w2m[j])

            def body_c(q, n):
                for k in range(W1_AHEAD, QC):
                    load_w1(q + k, k, w1c[k])
                    load_w2(n + k - 3, k - 3, w2c[k - 3], reuse=not (isinstance(n, int) and k - 3 < W2_RING))

            for k in range(W1_AHEAD):
                load_w1(2 * DC + k, k, w1c[k])
            load_w2(0, 0, w2c[0], reuse=False)
            body_c(2 * DC, 0)
            with sp.Fori(0, NT - 1) as i:
                q = i * Q_ITER + Q_PRE
                n = i * (2 * JH) + JH
                head(q, n, wa_dram, w2c, w2m)
                for k in range(W1_AHEAD):
                    load_w1(q + QT + k, k, w1m[k])
                body_m(q + QT, n)
                head(q + QT + QM, n + JH, wa_dram[DC:2 * DC], w2m, w2c)
                for k in range(W1_AHEAD):
                    load_w1(q + QT + QM + QA + k, k, w1c[k])
                body_c(q + QT + QM + QA, n + JH)
            q, n = (NT - 1) * Q_ITER + Q_PRE, (NT - 1) * 2 * JH + JH
            head(q, n, w1m, w2c, w2m)
            body_m(q, n)
            load_w2(n + JH - 1, JH - 1, w2m[JH - 1])

            sp.wait_ge(z_ready, NT * DC)
            sp.wait_ge(z_stored, NT * 16)

            def load_z(n, slot):
                for k, table in enumerate((first_t, second_t)):
                    b = sp.value_load(table[0:1, bass.ds(n, 1)], min_val=0, max_val=B - 1)
                    sp.dma_start(zs[:, slot, k, :, :].rearrange("p c s -> p (c s)"),
                                 z_dram[bass.ds(b, 1)].rearrange("o p f -> (o p) f")).then_inc(zl[slot], 16)

            def store_second(n, slot):
                b = sp.value_load(second_t[0:1, bass.ds(n, 1)], min_val=0, max_val=B - 1)
                dst = out[bass.ds(b, 1)].rearrange("o s d -> (o s) d")
                sp.wait_ge(yo_s, n + 1)
                sp.wait_ge(a_stored[slot], (n - slot) * 8 + 16)
                sp.dma_start(dst, yo[S:2 * S, slot, :]).then_inc(b_stored[slot], 16)

            for n in range(4):
                load_z(n, n)
            sp.dma_start(gam[:], gamma.to_broadcast([P, R, D])).then_inc(gb_loaded, 16)
            sp.dma_start(bet[:], beta.to_broadcast([P, R, D])).then_inc(gb_loaded, 16)

            for n in range(2):
                sp.wait_ge(zl_s, n + 1)
                load_z(n + 4, n)

            def unit(m, u, load):
                if load:
                    sp.wait_ge(zl_s, m + 3)
                    load_z(m + 6, (u + 2) % 4)
                store_second(m, u % 2)

            sp_loops = (NPAIR - 6) // UNROLL
            with sp.Fori(0, sp_loops) as k:
                for u in range(UNROLL):
                    unit(k * UNROLL + u, u, True)
            for m in range(sp_loops * UNROLL, NPAIR):
                unit(m, m % 4, m + 6 < NPAIR)
            for s in range(2):
                uses = (NPAIR + 1 - s) // 2
                sp.wait_ge(b_stored[s], 16 * uses)
                sp.wait_ge(a_stored[s], 16 * uses)

        @block.gpsimd
        def _(pool):
            nc.gpsimd.memset(ident[:], 0.0).then_inc(pool_c, 1)
            nc.gpsimd.memset(before[:], 1.0).then_inc(pool_c, 1)
            pool.wait_ge(pool_c, 2)
            nc.gpsimd.affine_select(out=ident[:], in_=ident[:], compare_op=ALU.not_equal, fill=1.0,
                                    base=0, pattern=[[-1, P]], channel_multiplier=1).then_inc(pool_c, 1)
            nc.gpsimd.affine_select(out=before[:], in_=before[:], compare_op=ALU.is_gt, fill=0.0,
                                    base=0, pattern=[[1, B]], channel_multiplier=-1).then_inc(pool_c, 1)
            nc.gpsimd.iota(iota_p[:], pattern=[[P, DC]], base=0, channel_multiplier=1,
                           allow_small_or_imprecise_dtypes=True).then_inc(pool_c, 1)
            nc.gpsimd.iota(iota_f[:], pattern=[[1, NSLOT]], base=0, channel_multiplier=0,
                           allow_small_or_imprecise_dtypes=True).then_inc(pool_c, 1)
            nc.gpsimd.iota(even[:], pattern=[[2, B // 2]], base=0, channel_multiplier=0,
                           allow_small_or_imprecise_dtypes=True).then_inc(pool_c, 1)

            def load_xk(t, p):
                pool.dma_start(xk_st[:, p % 2, :], xk[bass.ds(t * NP + p, 1)].rearrange("o p d -> (o p) d")
                               ).then_inc(xk_loaded[p % 2], 16)

            pool.wait_ge(qw_lo, 2 * DC)
            pool.dma_start(x_st[:], xT[0]).then_inc(x_loaded, 16)
            pool.wait_ge(qw_lo, 2 * DC + 1)
            pool.dma_start(xr[:], xT[0]).then_inc(xr_loaded, 16)
            for p in range(NP):
                if p >= 2:
                    pool.wait_ge(xk_lo_s, p - 1)
                pool.dma_start(xk_st[:, p % 2, :], xk[p]).then_inc(xk_loaded[p % 2], 16)
            pool.wait_ge(x_lo_s, DC)
            pool.dma_start(x_st[:], xT[1]).then_inc(x_loaded, 16)
            with pool.Fori(0, NT - 1) as i:
                for p in range(NP):
                    pool.wait_ge(xk_lo_s, i * NP + (NP + p - 1))
                    load_xk(i + 1, p)
                pool.wait_ge(x_lo_s, i * DC + 2 * DC)
                nxt = (i + 2) % NT
                pool.dma_start(x_st[:], xT[bass.ds(nxt, 1)].rearrange("o p c n -> (o p) c n")).then_inc(x_loaded, 16)
                pool.wait_ge(z_ready, i * DC + DC)
                pool.dma_start(z_dram[bass.ds(i * BT, BT)].rearrange("b p f -> p b f"),
                               zb[:].rearrange("p b c s -> p b (c s)")).then_inc(z_stored, 16)
                pool.wait_ge(z_stored, i * 16 + 16)
                pool.dma_start(xr[:], xT[bass.ds(i + 1, 1)].rearrange("o p c n -> (o p) c n")).then_inc(xr_loaded, 16)
            pool.wait_ge(x_lo_s, (NT + 1) * DC)
            pool.dma_start(l1_st[:], wd.rearrange("p r k n -> p r (k n)")).then_inc(l1_loaded[0], 16)
            pool.wait_ge(l1_lo, R)
            pool.dma_start(l1_st[:], wu.rearrange("p r k n -> p r (k n)")).then_inc(l1_loaded[1], 16)
            pool.wait_ge(z_ready, NT * DC)
            pool.dma_start(z_dram[(NT - 1) * BT:NT * BT].rearrange("b p f -> p b f"),
                           zb[:].rearrange("p b c s -> p b (c s)")).then_inc(z_stored, 16)

            pool.wait_ge(z_stored, NT * 16)
            nc.gpsimd.memset(mhalf[:], -0.5).then_inc(mhalf_s, 1)
            pool.wait_ge(mhalf_s, 1)

            def inverse_std(n, slot, reuse):
                pool.wait_ge(ve_s, n + 1)
                if reuse:
                    pool.wait_ge(yn_s, n - 1)
                nc.gpsimd.tensor_tensor(rstd[:, slot:slot + 1], veps[:, slot:slot + 1], mhalf[:],
                                        ALU.pow).then_inc(rstd_s, 1)
                pool.wait_ge(rstd_s, n + 1)
                nc.gpsimd.tensor_tensor(nbias[:, slot:slot + 1], negm[:, slot:slot + 1], rstd[:, slot:slot + 1],
                                        ALU.mult).then_inc(nb_s, 1)

            def store_first(n, slot):
                b = pool.value_load(first_t[0:1, bass.ds(n, 1)], min_val=0, max_val=B - 1)
                dst = out[bass.ds(b, 1)].rearrange("o s d -> (o s) d")
                pool.wait_ge(yo_s, n + 1)
                pool.dma_start(dst, yo[0:S, slot, :]).then_inc(a_stored[slot], 16)

            inverse_std(0, 0, False)
            inverse_std(1, 1, False)
            store_first(0, 0)
            with pool.Fori(0, LOOPS) as k:
                for u in range(UNROLL):
                    inverse_std(k * UNROLL + (2 + u), u % 2, True)
                    store_first(k * UNROLL + (1 + u), (1 + u) % 2)
            for n in range(LOOPS * UNROLL + 2, NPAIR):
                inverse_std(n, n % 2, True)
                store_first(n - 1, (n - 1) % 2)
            store_first(NPAIR - 1, (NPAIR - 1) % 2)
            for s in range(2):
                pool.wait_ge(a_stored[s], 16 * ((NPAIR + 1 - s) // 2))

        @block.scalar
        def _(act):
            for k in range(DC):
                act.wait_ge(qk_loaded[k], 32)
                nc.scalar.copy(t_hi[:, k, :], x_st[:, k, :]).then_inc(qw_hi, 1)
                nc.scalar.copy(y_hi[:, k, :], zb_rows[:, k, :]).then_inc(qw_hi, 1)
            act.wait_ge(wv_loaded, 16)
            nc.scalar.copy(a_hi[:], xr[:]).then_inc(qw_hi, 1)

            def split_w1(q, k):
                if isinstance(q, int) and q < 2 * DC:
                    act.wait_ge(wa_out, DC if q < DC else 2 * DC)
                else:
                    act.wait_ge(w1_loaded[k % W1_STAGE], (q - 2 * DC - k % W1_STAGE) * (16 // W1_STAGE) + 16)
                nc.scalar.copy(w1_hi[:, k % W1_RING, :], w1_st[:, k % W1_STAGE, :]).then_inc(w1_hi_s, 1)

            def split_w2(n, k):
                act.wait_ge(w2_loaded[k % W2_RING], (n - k % W2_RING) * (16 // W2_RING) + 16)
                act.wait_ge(acc_mm, n - 1)
                nc.scalar.copy(w2_hi[:, k % W2_RING, :], w2_st[:, k % W2_RING, :]).then_inc(w2_hi_s, 1)

            def split_x(t, c):
                act.wait_ge(x_loaded, t * 16 + 16)
                nc.scalar.copy(x_hi[:, c, :], x_st[:, c, :]).then_inc(x_hi_s, 1)

            def softmax(m):
                act.wait_ge(nmx_s, m + 1)
                for k in range(2):
                    r = slice(k * S, (k + 1) * S)
                    ins = nc.scalar.activation(pe_[r, r], s_ps[r, r], ACT.Exp, bias=nmx[r, :], scale=SCALE,
                                               accum_out=rs[r, :])
                ins.then_inc(exp_s, 1)

            def split_xk(m, p):
                act.wait_ge(xk_loaded[p % 2], (m - p % 2) * 8 + 16)
                nc.scalar.copy(xk_hi[:], xk_st[:, p % 2, :]).then_inc(xk_hi_s, 1)

            def split_pt(m):
                act.wait_ge(pt_mm, m + 1)
                nc.scalar.copy(pt_hi[:], pt_ps).then_inc(pt_hi_s, 1)

            def split_y(m, p):
                act.wait_ge(y_mm, m + 1)
                nc.scalar.copy(y_hi[:, :, p * P:(p + 1) * P],
                               y_bank[:].rearrange("p (c n) -> p c n", c=DC)).then_inc(y_hi_s, 1)

            def attention(m, s):
                p = s // 4
                if s % 4 == 0:
                    softmax(m + p)
                if s % 4 == 1:
                    split_pt(m + p)
                    split_xk(m + p, p)
                if s % 4 == 2:
                    split_y(m + p, p)

            def stage_a(g, q, pos):
                for c in range(DC):
                    act.wait_ge(h_mm, g + c + 1)
                    nc.scalar.activation(a_hi[:, c, :], hb[c % 2][:], ACT.Identity,
                                         bias=bcol(BP + c)).then_inc(h_hi_s, 1)
                    split_w1(q + c + W1_AHEAD, pos + c + W1_AHEAD)

            def gelu(g, j, col):
                act.wait_ge(h_mm, g + j + 1)
                act.wait_ge(h_lo_s, g + j - 1)
                nc.scalar.activation(h_hi[:, j % 2, :], hb[j % 2][:], ACT.Gelu, bias=bcol(col + j))
                nc.scalar.activation(hf[:, j % 2, :], hb[j % 2][:], ACT.Gelu,
                                     bias=bcol(col + j)).then_inc(h_hi_s, 1)

            def stage_c(g, q, pos, n, x_next):
                for j in range(JH):
                    split_w1(q + j + W1_AHEAD, pos + j + W1_AHEAD)
                    gelu(g, j, CB1)
                    split_w2(n + j + 1, j + 1)
                    if 4 <= j < 4 + DC:
                        split_x(x_next, j - 4)

            def stage_m(g, q, pos, n, pair, last=False):
                for j in range(JH):
                    for k in (2 * j, 2 * j + 1):
                        if not last or k + W1_AHEAD < QM:
                            split_w1(q + k + W1_AHEAD, pos + k + W1_AHEAD)
                    gelu(g, j, MB1)
                    if not last or j + 1 < JH:
                        split_w2(n + j + 1, j + 1)
                    if pair is not None:
                        attention(pair, j)
                    if last:
                        split_l1(j)

            def split_l1(j):
                for load, w, j0 in ((0, wd_hi, 4), (1, wu_hi, 10)):
                    if j0 <= j < j0 + R:
                        act.wait_ge(l1_loaded[load], 16)
                        nc.scalar.copy(w[:, j - j0].rearrange("p k n -> p (k n)"), l1_st[:, j - j0, :]).then_inc(l1_hi, 1)

            def cms_hi(t):
                for c in range(DC):
                    act.wait_ge(cf_s, t * DC + c + 1)
                    nc.scalar.copy(c_hi[:, c, :], cf[:, c, :]).then_inc(c_hi_s, 1)

            for c in range(DC):
                split_x(0, c)
            act.wait_ge(wp_loaded, 16)
            nc.scalar.copy(c_hi[:], zb_rows).then_inc(qw_hi, 1)
            for k in range(DC):
                split_w1(k, k)
            act.wait_ge(zero_p, 1)
            for c in range(DC):
                act.wait_ge(h_mm, c + 1)
                nc.scalar.copy(t_hi[:, c, :], hb[c % 2][:]).then_inc(h_hi_s, 1)
            for s in range(JH):
                attention(0, s)
            for k in range(DC):
                split_w1(DC + k, DC + k)
            stage_a(DC, QT, QT)
            act.wait_ge(row_in, 16)
            act.wait_ge(w2_loaded[0], 16)
            nc.scalar.copy(w2_hi[:, 0, :], w2_st[:, 0, :]).then_inc(w2_hi_s, 1)
            for j in range(JH):
                split_w1(QT + QA + j + W1_AHEAD, j + W1_AHEAD)
                gelu(2 * DC, j, CB1)
                if j == 0:
                    act.wait_ge(w2_loaded[1], 16)
                    nc.scalar.copy(w2_hi[:, 1, :], w2_st[:, 1, :]).then_inc(w2_hi_s, 1)
                else:
                    split_w2(j + 1, j + 1)
                if 4 <= j < 4 + DC:
                    split_x(1, j - 4)
            with act.Fori(0, NT - 1) as i:
                g = i * G_ITER + G_PRE
                q = i * Q_ITER + Q_PRE
                n = i * (2 * JH) + JH
                for c in range(DC):
                    for e in ((), (0, 1), (2,), (3,))[c]:
                        act.wait_ge(cf_s, i * DC + e + 1)
                        nc.scalar.copy(c_hi[:, e, :], cf[:, e, :]).then_inc(c_hi_s, 1)
                    act.wait_ge(h_mm, g + c + 1)
                    nc.scalar.copy(t_hi[:, c, :], hb[c % 2][:]).then_inc(h_hi_s, 1)
                    split_w1(q + c + W1_AHEAD, c + W1_AHEAD)
                stage_m(g + DC, q + QT, QT, n, i * NP + NP)
                stage_a(g + DC + JH, q + QT + QM, QT + QM)
                stage_c(g + 2 * DC + JH, q + QT + QM + QA, 0, n + JH, i + 2)
            cms_hi(NT - 1)
            g, q, n = (NT - 1) * G_ITER + G_PRE, (NT - 1) * Q_ITER + Q_PRE, (NT - 1) * 2 * JH + JH
            stage_m(g, q, 0, n, None, last=True)

            def split_z(n, slot):
                act.wait_ge(zl[slot], (n - slot) * 8 + 32)
                nc.scalar.copy(z_hi[:, slot].rearrange("p c (k s) -> p c k s", k=2),
                               zs[:, slot].rearrange("p k c s -> p c k s")).then_inc(zh_s, 1)

            def gelu_pair(n, slot):
                act.wait_ge(d_mm, n + 1)
                nc.scalar.activation(hs[:, slot, :], d_ps[slot][:, 0:KD], ACT.Gelu).then_inc(gelu_s, 1)

            def normalise(n, slot):
                act.wait_ge(nb_s, n + 1)
                nc.scalar.activation(yn[:, slot, :], u_ps[slot][:], ACT.Identity, bias=nbias[:, slot:slot + 1],
                                     scale=rstd[:, slot:slot + 1]).then_inc(yn_s, 1)

            def unit(n, u, z, d, norm):
                act.wait_ge(ht_mm, n + 1)
                nc.scalar.copy(ht_hi[:, u % 2, :], ht_ps[u % 2][:, 0:KD]).then_inc(ht_hi_s, 1)
                if norm:
                    normalise(n - 1, (u - 1) % 2)
                if d:
                    gelu_pair(n + 1, (u + 1) % 2)
                if z:
                    if norm:
                        act.wait_ge(u_mm, n)
                    split_z(n + 3, (u + 3) % 4)

            for n in range(3):
                split_z(n, n)
            gelu_pair(0, 0)
            unit(0, 0, True, True, False)
            unit(1, 1, True, True, True)
            with act.Fori(0, LOOPS) as k:
                for u in range(UNROLL):
                    unit(k * UNROLL + (2 + u), 2 + u, True, True, True)
            for n in range(LOOPS * UNROLL + 2, NPAIR):
                unit(n, n % 4, False, n + 1 < NPAIR, True)
            normalise(NPAIR - 1, (NPAIR - 1) % 2)

        @block.vector
        def _(dve):
            nc.vector.memset(pe_[:], 0.0).then_inc(zero_p, 1)
            nc.vector.memset(ones[:], 1.0).then_inc(const_s, 1)
            dve.wait_ge(pool_c, 7)
            nc.vector.tensor_copy(ident_r[:], ident[:]).then_inc(const_s, 1)

            def split_projection(n, lo, hi, src):
                dve.wait_ge(qw_hi, n + 1)
                nc.vector.tensor_tensor(lo, src, f32(hi), ALU.subtract).then_inc(qw_lo, 1)

            for k in range(DC):
                split_projection(2 * k, t_lo[:, k, :], t_hi[:, k, :], x_st[:, k, :])
                split_projection(2 * k + 1, y_lo[:, k, :], y_hi[:, k, :], zb_rows[:, k, :])

            nc.vector.memset(ones2f[:], 1.0).then_inc(ones_s, 1)
            dve.wait_ge(ones_s, 1)
            nc.vector.tensor_copy(ones2[:], ones2f[:]).then_inc(ones_s, 1)
            dve.wait_ge(rows_loaded, 32)
            nc.vector.tensor_copy(brow[0:1], brow_f[:]).then_inc(row_hi, 1)
            dve.wait_ge(row_hi, 1)
            nc.vector.tensor_tensor(brow_lo[:], brow_f[:], f32(brow[0:1]), ALU.subtract).then_inc(row_lo, 1)
            split_projection(2 * DC, a_lo[:], a_hi[:], xr[:])

            def product(m):
                dve.wait_ge(wa_mm, m + 1)
                if m == DC:
                    dve.wait_ge(w1_lo_s, DC)
                    dve.wait_ge(wa_stored, 16)
                k = m % DC
                nc.vector.tensor_copy(w1_st[:, :, k * P:(k + 1) * P],
                                      hb[m % 2][:].rearrange("p (j n) -> p j n", j=DC)).then_inc(wa_out, 1)

            for m in range(DC):
                product(m)

            dve.wait_ge(const_in, 32)
            nc.vector.tensor_copy(tgt_f[:], tgt_i[:]).then_inc(const_s, 1)
            dve.wait_ge(const_s, 3)
            for c in range(DC):
                nc.vector.tensor_scalar(ohb[:, c, :], tgt_f[:], iota_p[:, c:c + 1], bcol(CB2 + c),
                                        ALU.is_equal, ALU.add).then_inc(ohb_s, 1)

            did = [0]

            def link(ins):
                did[0] += 1
                ins.then_inc(sort_v, 1)
                dve.wait_ge(sort_v, did[0])

            dve.wait_ge(sort_in, 16)
            link(nc.vector.tensor_copy(role_f[:], role_i[:]))
            link(nc.vector.tensor_scalar(role_f[:], role_f[:], 0.0, float(R - 1), ALU.max, ALU.min))
            link(nc.vector.tensor_copy(batch_f[:, 0:1], iota_p[0:B, 0:1]))
            link(nc.vector.memset(batch_f[:, 1:2], 1.0))
            link(nc.vector.tensor_copy(batch_f[:, 2:3], role_f[:]))
            link(nc.vector.tensor_scalar(onehot[:], iota_f[0:B, 0:R], role_f[:], None, ALU.is_equal))
            def sort_slots():
                dve.wait_ge(sort_mm, 2)
                for r in range(R):
                    link(nc.vector.tensor_scalar(flags[:], even[:], y_bank[0:B, R + r:R + r + 1], None, ALU.is_lt))
                    link(nc.vector.reduce_sum(half[:, r:r + 1], flags[:], AX_X))
                link(nc.vector.memset(start[:, 0:1], 0.0))
                for r in range(1, R):
                    link(nc.vector.scalar_tensor_tensor(out=start[:, r:r + 1], in0=half[:, r - 1:r], scalar=2.0,
                                                        in1=start[:, r - 1:r], op0=ALU.mult, op1=ALU.add))
                link(nc.vector.tensor_tensor(rank_r[:], y_bank[0:B, 0:R], start[:], ALU.add))
                link(nc.vector.tensor_tensor(rank_r[:], rank_r[:], onehot[:], ALU.mult))
                link(nc.vector.reduce_sum(rank[:], rank_r[:], AX_X))
                link(nc.vector.tensor_scalar(slot1[:], iota_f[0:B, :], rank[:], None, ALU.is_equal))

            def sort_pairs():
                dve.wait_ge(sort_mm, 3)
                link(nc.vector.tensor_copy(slots[:].rearrange("o v n k -> o (v n k)"), y_bank[0:1, 64:64 + 3 * NSLOT]))
                link(nc.vector.tensor_scalar(empty[:], slots[:, 1], -1.0, 1.0, ALU.mult, ALU.add))
                for v, w in ((0, 0), (2, 1)):
                    link(nc.vector.tensor_scalar(fill[:, w], empty[:, :, 0], slots[:, v, 0, 0:1], None, ALU.mult))
                    link(nc.vector.tensor_tensor(pick[:, w], fill[:, w], slots[:, v, :, 0], ALU.add))
                link(nc.vector.tensor_tensor(fill[:, 2], empty[:, :, 1], pick[:, 0], ALU.mult))
                link(nc.vector.tensor_tensor(pick[:, 2], fill[:, 2], slots[:, 0, :, 1], ALU.add))
                nc.vector.tensor_copy(first_t[:], pick[:, 0]).then_inc(sorted_s, 1)
                nc.vector.tensor_copy(role_t[:], pick[:, 1]).then_inc(sorted_s, 1)
                nc.vector.tensor_copy(second_t[:], pick[:, 2]).then_inc(sorted_s, 1)

            def split_w1(q, k):
                dve.wait_ge(w1_hi_s, q + 1)
                nc.vector.tensor_tensor(w1_lo[:, k % W1_RING, :], w1_st[:, k % W1_STAGE, :],
                                        f32(w1_hi[:, k % W1_RING, :]), ALU.subtract).then_inc(w1_lo_s, 1)

            def split_w2(n, k):
                dve.wait_ge(w2_hi_s, n + 1)
                nc.vector.tensor_tensor(w2_lo[:, k % W2_RING, :], w2_st[:, k % W2_RING, :],
                                        f32(w2_hi[:, k % W2_RING, :]), ALU.subtract).then_inc(w2_lo_s, 1)

            def split_x(t, c):
                dve.wait_ge(x_hi_s, t * DC + c + 1)
                nc.vector.tensor_tensor(x_lo[:, c, :], x_st[:, c, :], f32(x_hi[:, c, :]),
                                        ALU.subtract).then_inc(x_lo_s, 1)

            def row_max(m):
                dve.wait_ge(s_mm, m + 1)
                for k in range(2):
                    r = slice(k * S, (k + 1) * S)
                    ins = nc.vector.reduce_max(mx[r, :], s_ps[r, r], AX_X)
                    ins.then_inc(mx_s, 1)
                dve.wait_ge(mx_s, m * 2 + 2)
                nc.vector.tensor_scalar(nmx[:], mx[:], -SCALE, None, ALU.mult).then_inc(nmx_s, 1)

            def normalise_p(m):
                dve.wait_ge(exp_s, m + 1)
                nc.vector.reciprocal(rinv[:], rs[:]).then_inc(rinv_s, 1)
                dve.wait_ge(rinv_s, m + 1)
                nc.vector.tensor_scalar(pn[:], pe_[:], rinv[:], None, ALU.mult).then_inc(pn_s, 1)

            def split_xk(m, p):
                dve.wait_ge(xk_hi_s, m + 1)
                nc.vector.tensor_tensor(xk_lo[:], xk_st[:, p % 2, :], f32(xk_hi[:]),
                                        ALU.subtract).then_inc(xk_lo_s, 1)

            def split_pt(m):
                dve.wait_ge(pt_hi_s, m + 1)
                nc.vector.tensor_tensor(pt_lo[:], pt_ps, f32(pt_hi[:]), ALU.subtract).then_inc(pt_lo_s, 1)

            def split_y(m, p):
                dve.wait_ge(y_hi_s, m + 1)
                cols = slice(p * P, (p + 1) * P)
                nc.vector.tensor_tensor(y_lo[:, :, cols], y_bank[:].rearrange("p (c n) -> p c n", c=DC),
                                        f32(y_hi[:, :, cols]), ALU.subtract).then_inc(y_lo_s, 1)

            def attention(m, s):
                p = s // 4
                if s % 4 == 0:
                    row_max(m + p)
                    normalise_p(m + p)
                if s % 4 == 1:
                    split_pt(m + p)
                    split_xk(m + p, p)
                if s % 4 == 2:
                    split_y(m + p, p)

            def t_lo_half(g, c):
                dve.wait_ge(h_hi_s, g + c + 1)
                nc.vector.tensor_tensor(t_lo[:, c, :], hb[c % 2][:], f32(t_hi[:, c, :]),
                                        ALU.subtract).then_inc(h_lo_s, 1)

            def stage_a(g, q, pos, between=None):
                for c in range(DC):
                    dve.wait_ge(h_hi_s, g + c + 1)
                    nc.vector.scalar_tensor_tensor(out=a_lo[:, c, :], in0=hb[c % 2][:], scalar=bcol(BP + c),
                                                   in1=f32(a_hi[:, c, :]), op0=ALU.add,
                                                   op1=ALU.subtract).then_inc(h_lo_s, 1)
                    split_w1(q + c + W1_AHEAD, pos + c + W1_AHEAD)
                    if between and c:
                        between(c - 1)
                if between:
                    between(DC - 1)

            def h_lo_half(g, j):
                dve.wait_ge(h_hi_s, g + j + 1)
                nc.vector.tensor_tensor(h_lo[:, j % 2, :], hf[:, j % 2, :], f32(h_hi[:, j % 2, :]),
                                        ALU.subtract).then_inc(h_lo_s, 1)

            def stage_c(g, q, pos, n, x_next, more={}):
                for j in range(JH):
                    split_w1(q + j + W1_AHEAD, pos + j + W1_AHEAD)
                    h_lo_half(g, j)
                    split_w2(n + j + 1, j + 1)
                    if 4 <= j < 4 + DC:
                        split_x(x_next, j - 4)
                    if j in more:
                        more[j]()

            def stage_m(g, q, pos, n, t, pair, last=False):
                for j in range(JH):
                    for k in (2 * j, 2 * j + 1):
                        if not last or k + W1_AHEAD < QM:
                            split_w1(q + k + W1_AHEAD, pos + k + W1_AHEAD)
                    h_lo_half(g, j)
                    if 1 <= j <= DC:
                        add_x(t, j - 1)
                    if not last or j + 1 < JH:
                        split_w2(n + j + 1, j + 1)
                    if pair is not None:
                        attention(pair, j)
                    if last:
                        split_l1(j)

            def split_l1(j):
                for w_hi, w_lo, j0, at in ((wd_hi, wd_lo, 4, 0), (wu_hi, wu_lo, 10, R)):
                    if j0 <= j < j0 + R:
                        r = j - j0
                        dve.wait_ge(l1_hi, at + r + 1)
                        nc.vector.tensor_tensor(w_lo[:, r].rearrange("p k n -> p (k n)"), l1_st[:, r, :],
                                                f32(w_hi[:, r]).rearrange("p k n -> p (k n)"),
                                                ALU.subtract).then_inc(l1_lo, 1)

            def batches(ap):
                return ap.rearrange("p (b s) -> p b s", s=S)

            def cms_f32(t, c, n_end):
                if c == 0:
                    dve.wait_ge(acc_mm, n_end)
                oh = ohb[:, c, bass.ds(t * BT, BT)]
                nc.vector.tensor_tensor(batches(cf[:, c, :]), batches(acc[c][:]),
                                        oh.unsqueeze(2).to_broadcast([P, BT, S]),
                                        ALU.add).then_inc(cf_s, 1)

            def add_x(t, c):
                dve.wait_ge(cf_s, t * DC + c + 1)
                dve.wait_ge(xr_loaded, t * 16 + 16)
                nc.vector.tensor_tensor(xr[:, c, :], xr[:, c, :], cf[:, c, :], ALU.add).then_inc(xr_sum, 1)

            def cms_lo(t, c):
                dve.wait_ge(c_hi_s, t * DC + c + 1)
                nc.vector.tensor_tensor(c_lo[:, c, :], cf[:, c, :], f32(c_hi[:, c, :]),
                                        ALU.subtract).then_inc(c_lo_s, 1)

            def z_chunk(t, c, n_end):
                if c == 0:
                    dve.wait_ge(acc_mm, n_end)
                    dve.wait_ge(xr_sum, t * DC + DC)
                nc.vector.scalar_tensor_tensor(out=zt[:, c % 2, :], in0=acc[c][:], scalar=bcol(MB2 + c),
                                               in1=xr[:, c, :], op0=ALU.add, op1=ALU.add).then_inc(zt_s, 1)
                dve.wait_ge(zt_s, t * DC + c + 1)
                nc.vector.tensor_scalar(zb[:, :, c, :], batches(zt[:, c % 2, :]), 0.0, 1.0,
                                        ALU.max, ALU.min).then_inc(z_ready, 1)

            for c in range(DC):
                split_x(0, c)
            split_projection(2 * DC + 1, c_lo[:], c_hi[:], zb_rows)
            for k in range(DC):
                split_w1(k, k)
            for c in range(DC):
                t_lo_half(0, c)
            for s in range(JH):
                attention(0, s)
                if s % 4 == 0:
                    product(DC + s // 4)
            for k in range(DC):
                split_w1(DC + k, DC + k)
            stage_a(DC, QT, QT)
            split_w2(0, 0)
            stage_c(2 * DC, QT + QA, 0, 0, 1, {6: sort_slots, 12: sort_pairs})
            dve.wait_ge(ohb_s, DC)
            with dve.Fori(0, NT - 1) as i:
                g = i * G_ITER + G_PRE
                q = i * Q_ITER + Q_PRE
                n = i * (2 * JH) + JH
                t_lo_half(g, 0)
                split_w1(q + W1_AHEAD, W1_AHEAD)
                cms_f32(i, 0, n)
                cms_f32(i, 1, n)
                cms_lo(i, 0)
                t_lo_half(g, 1)
                split_w1(q + 1 + W1_AHEAD, 1 + W1_AHEAD)
                cms_f32(i, 2, n)
                cms_lo(i, 1)
                t_lo_half(g, 2)
                split_w1(q + 2 + W1_AHEAD, 2 + W1_AHEAD)
                cms_f32(i, 3, n)
                cms_lo(i, 2)
                t_lo_half(g, 3)
                split_w1(q + 3 + W1_AHEAD, 3 + W1_AHEAD)
                cms_lo(i, 3)
                stage_m(g + DC, q + QT, QT, n, i, i * NP + NP)
                qa, ga = q + QT + QM, g + DC + JH
                stage_a(ga, qa, QT + QM, between=lambda c: z_chunk(i, c, n + JH))
                stage_c(ga + DC, qa + QA, 0, n + JH, i + 2)
            g, q, n = (NT - 1) * G_ITER + G_PRE, (NT - 1) * Q_ITER + Q_PRE, (NT - 1) * 2 * JH + JH
            for c in range(DC):
                cms_f32(NT - 1, c, n)
                if c:
                    cms_lo(NT - 1, c - 1)
            cms_lo(NT - 1, DC - 1)
            stage_m(g, q, 0, n, NT - 1, None, last=True)
            for c in range(DC):
                z_chunk(NT - 1, c, n + JH)

            def split_z(n, slot):
                dve.wait_ge(zh_s, n + 1)
                nc.vector.tensor_tensor(z_lo[:, slot].rearrange("p c (k s) -> p c k s", k=2),
                                        zs[:, slot].rearrange("p k c s -> p c k s"),
                                        f32(z_hi[:, slot]).rearrange("p c (k s) -> p c k s", k=2),
                                        ALU.subtract).then_inc(zl_s, 1)

            def stats(n, slot):
                dve.wait_ge(u_mm, n + 1)
                nc.vector.bn_stats(st6[:], u_ps[slot][:]).then_inc(st_s, 1)

            def moments(n, slot):
                nc.vector.bn_aggr(mv[:], st6[:]).then_inc(mv_s, 1)
                dve.wait_ge(mv_s, n + 1)
                nc.vector.tensor_scalar(negm[:, slot:slot + 1], mv[:, 0:1], -1.0, None, ALU.mult)
                nc.vector.tensor_scalar(veps[:, slot:slot + 1], mv[:, 1:2], LN_EPS, None, ALU.add).then_inc(ve_s, 1)

            def scale_shift(n, slot, reuse):
                r = dve.value_load(role_t[0:1, bass.ds(n, 1)], min_val=0, max_val=R - 1)
                if reuse:
                    dve.wait_ge(a_stored[slot], (n - slot) * 8)
                    dve.wait_ge(b_stored[slot], (n - slot) * 8)
                dve.wait_ge(yn_s, n + 1)
                nc.vector.tensor_tensor(yg[:, slot, :], yn[:, slot, :],
                                        gam[:, bass.ds(r, 1), :].rearrange("p o d -> p (o d)"),
                                        ALU.mult).then_inc(yg_s, 1)
                dve.wait_ge(yg_s, n + 1)
                nc.vector.tensor_tensor(yo[:, slot, :], yg[:, slot, :],
                                        bet[:, bass.ds(r, 1), :].rearrange("p o d -> p (o d)"),
                                        ALU.add).then_inc(yo_s, 1)

            def unit(n, u, z, tail, scale, reuse):
                if tail:
                    stats(n - 1, (u - 1) % 2)
                    dve.wait_ge(st_s, n)
                    if scale:
                        dve.wait_ge(ve_s, n - 1)
                dve.wait_ge(ht_hi_s, n + 1)
                nc.vector.tensor_tensor(ht_lo[:, u % 2, :], ht_ps[u % 2][:, 0:KD], f32(ht_hi[:, u % 2, :]),
                                        ALU.subtract).then_inc(ht_lo_s, 1)
                if tail:
                    moments(n - 1, (u - 1) % 2)
                if z:
                    split_z(n + 2, (u + 2) % 4)
                if scale:
                    scale_shift(n - 2, u % 2, reuse)

            split_z(0, 0)
            split_z(1, 1)
            unit(0, 0, True, False, False, False)
            unit(1, 1, True, True, False, False)
            dve.wait_ge(gb_loaded, 32)
            unit(2, 2, True, True, True, False)
            unit(3, 3, True, True, True, False)
            dve_loops = (NPAIR - 6) // UNROLL
            with dve.Fori(0, dve_loops) as k:
                for u in range(UNROLL):
                    unit(k * UNROLL + (4 + u), u, True, True, True, True)
            for n in range(dve_loops * UNROLL + 4, NPAIR):
                unit(n, n % 4, n + 2 < NPAIR, True, True, True)
            stats(NPAIR - 1, (NPAIR - 1) % 2)
            dve.wait_ge(st_s, NPAIR)
            dve.wait_ge(ve_s, NPAIR - 1)
            moments(NPAIR - 1, (NPAIR - 1) % 2)
            for n in (NPAIR - 2, NPAIR - 1):
                scale_shift(n, n % 2, True)

        @block.tensor
        def _(pe):
            def mm3(ps, w, x, first, last):
                nc.tensor.matmul(ps, w[0], x[0], start=first, stop=False)
                nc.tensor.matmul(ps, w[0], x[1], start=False, stop=False)
                return nc.tensor.matmul(ps, w[1], x[0], start=False, stop=last)

            def chunk(pair, k, cols):
                return [half[:, k, cols] for half in pair]

            ALL = slice(0, TOK)

            def w1_block(k, c):
                cols = slice(c * P, (c + 1) * P)
                return w1_hi[:, k % W1_RING, cols], w1_lo[:, k % W1_RING, cols]

            def product(m):
                lhs, rhs = ((t_hi, t_lo), (y_hi, y_lo)) if m < DC else ((a_hi, a_lo), (c_hi, c_lo))
                if m >= 2:
                    pe.wait_ge(wa_out, m - 1)
                rows = slice((m % DC) * P, (m % DC + 1) * P)
                for k in range(DC):
                    if m % DC == 0:
                        pe.wait_ge(qw_lo, 2 * k + 2 if m < DC else 2 * DC + 2)
                    ins = mm3(hb[m % 2][:], chunk(lhs, k, rows), chunk(rhs, k, ALL), k == 0, k == DC - 1)
                ins.then_inc(wa_mm, 1)

            def sort_counts():
                pe.wait_ge(sort_v, 6)
                nc.tensor.matmul(y_bank[0:B, 0:R], before[:], onehot[:], start=True, stop=True).then_inc(sort_mm, 1)
                nc.tensor.matmul(y_bank[0:B, R:2 * R], ones[:], onehot[:], start=True, stop=True).then_inc(sort_mm, 1)

            def sort_gather():
                pe.wait_ge(sort_v, 6 + 2 * R + 1 + (R - 1) + 4)
                for v in range(3):
                    ins = nc.tensor.matmul(y_bank[0:1, 64 + v * NSLOT:64 + (v + 1) * NSLOT], batch_f[:, v:v + 1],
                                           slot1[:], start=True, stop=True)
                ins.then_inc(sort_mm, 1)

            def project(g, c, w, x, first=None):
                if first is not None:
                    pe.wait_ge(w1_lo_s, first)
                else:
                    pe.wait_ge(h_lo_s, g + c - 1)
                for k in range(DC):
                    ins = mm3(hb[c % 2][:], w1_block(w + c, k), chunk(x, k, ALL), k == 0, k == DC - 1)
                ins.then_inc(h_mm, 1)

            def half_step(pos, bank, kq, x, first, last, ready=None):
                for k in range(DC):
                    if ready is not None and k in (0, DC - 1):
                        pe.wait_ge(h_lo_s, ready - (k == 0))
                    ins = mm3(hb[bank][:], w1_block(pos + kq, k), chunk(x, k, ALL), first and k == 0, last and k == DC - 1)
                if last:
                    ins.then_inc(h_mm, 1)

            def second_layer(g_next, j, free=None):
                pe.wait_ge(h_lo_s, g_next)
                if free is not None:
                    pe.wait_ge(*free)
                for c in range(DC):
                    cols = slice(c * P, (c + 1) * P)
                    ins = mm3(acc[c][:], (w2_hi[:, j % W2_RING, cols], w2_lo[:, j % W2_RING, cols]),
                              (h_hi[:, j % 2, :], h_lo[:, j % 2, :]), j == 0, j == JH - 1)
                ins.then_inc(acc_mm, 1)

            def scores(m, p):
                cols = slice(p * P, (p + 1) * P)
                for k in range(DC):
                    ins = mm3(s_ps, chunk((t_hi, t_lo), k, cols), chunk((x_hi, x_lo), k, cols), k == 0, k == DC - 1)
                ins.then_inc(s_mm, 1)

            def attention(m, s):
                p = s // 4
                if s % 4 == 0:
                    scores(m + p, p)
                if s % 4 == 1:
                    pe.wait_ge(pn_s, m + p + 1)
                    nc.tensor.transpose(pt_ps, pn[:], ident[:]).then_inc(pt_mm, 1)
                if s % 4 == 2:
                    pe.wait_ge(pt_lo_s, m + p + 1)
                    pe.wait_ge(xk_lo_s, m + p + 1)
                    if not isinstance(m, int) or m + p:
                        pe.wait_ge(y_lo_s, m + p)
                    for c in range(DC):
                        cols = slice(c * P, (c + 1) * P)
                        ins = mm3(y_bank[:, cols], (xk_hi[:, cols], xk_lo[:, cols]), (pt_hi[:], pt_lo[:]), True, True)
                    ins.then_inc(y_mm, 1)

            def stage_c(g, free, more={}):
                for j in range(JH):
                    half_step(0, j % 2, j, (a_hi, a_lo), True, True, g if j == 0 else None)
                    if j:
                        second_layer(g + j, j - 1, free if j == 1 else None)
                    if j in more:
                        more[j]()

            def stage_m(g, pos, t, pair, flush=None):
                pe.wait_ge(h_lo_s, g - 1)
                half_step(pos, 0, 0, (a_hi, a_lo), True, False)
                if flush:
                    flush()
                pe.wait_ge(h_lo_s, g)
                half_step(pos, 1, 2, (a_hi, a_lo), True, False)
                pe.wait_ge(c_lo_s, t * DC + DC)
                half_step(pos, 0, 1, (c_hi, c_lo), False, True)
                if pair is not None:
                    attention(pair, 0)
                half_step(pos, 1, 3, (c_hi, c_lo), False, True)
                second_layer(g + 1, 0, (cf_s, t * DC + DC))
                if pair is not None:
                    attention(pair, 1)
                for j in range(2, JH):
                    half_step(pos, j % 2, 2 * j, (a_hi, a_lo), True, False)
                    half_step(pos, j % 2, 2 * j + 1, (c_hi, c_lo), False, True)
                    second_layer(g + j, j - 1)
                    if pair is not None:
                        attention(pair, j)

            for m in range(DC):
                product(m)
            pe.wait_ge(x_lo_s, DC)
            for c in range(DC):
                project(0, c, 0, (x_hi, x_lo), first=c + 1 if c < 2 else None)
            pe.wait_ge(h_lo_s, DC)
            for s in range(JH):
                attention(0, s)
                if s % 4 == 0:
                    product(DC + s // 4)
            pe.wait_ge(y_lo_s, NP)
            for c in range(DC):
                project(DC, c, QT, (y_hi, y_lo), first=QT + c + 1 if c < 2 else None)
            stage_c(2 * DC, None, {4: sort_counts, 10: sort_gather})
            with pe.Fori(0, NT - 1) as i:
                g = i * G_ITER + G_PRE
                pe.wait_ge(x_lo_s, i * DC + 2 * DC)
                project(g, 0, 0, (x_hi, x_lo))
                second_layer(g, JH - 1)
                for c in range(1, DC):
                    project(g, c, 0, (x_hi, x_lo))
                stage_m(g + DC, QT, i, i * NP + NP)
                ga = g + DC + JH
                pe.wait_ge(y_lo_s, i * NP + 2 * NP)
                project(ga, 0, QT + QM, (y_hi, y_lo))
                second_layer(ga, JH - 1)
                for c in range(1, DC):
                    project(ga, c, QT + QM, (y_hi, y_lo))
                stage_c(ga + DC, (zt_s, i * DC + DC))
            g = (NT - 1) * G_ITER + G_PRE
            stage_m(g, 0, NT - 1, None, flush=lambda: second_layer(g, JH - 1))
            second_layer(g + JH, JH - 1)

            pe.wait_ge(z_ready, NT * DC)
            pe.wait_ge(l1_lo, 2 * R)
            pe.wait_ge(ones_s, 2)
            pe.wait_ge(row_in, 16)

            def pair_role(n):
                return pe.value_load(role_t[0:1, bass.ds(n, 1)], min_val=0, max_val=R - 1)

            def rows(ap, r):
                return ap[:, bass.ds(r, 1)].rearrange("p o n -> p (o n)")

            def down(n, u):
                r = pair_role(n)
                pe.wait_ge(zl_s, n + 1)
                ps = d_ps[u % 2][:, 0:KD]
                nc.tensor.matmul(ps, ones2[:], rows(brow[:, :, 0:KD], r), start=True, stop=False)
                for k in range(DC):
                    w = [rows(half[:, :, k, :], r) for half in (wd_hi, wd_lo)]
                    ins = mm3(ps, (z_hi[:, u % 4, k, :], z_lo[:, u % 4, k, :]), w, False, k == DC - 1)
                ins.then_inc(d_mm, 1)

            def turn(n, u, reuse):
                r = pair_role(n)
                pe.wait_ge(gelu_s, n + 1)
                for k in range(KD // P):
                    ins = nc.tensor.transpose(ht_ps[u % 2][:, k * P:(k + 1) * P], hs[:, u % 2, k * P:(k + 1) * P],
                                              ident[:])
                ins.then_inc(ht_mm, 1)
                ps = u_ps[u % 2]
                if reuse:
                    pe.wait_ge(yn_s, n - 1)
                nc.tensor.matmul(ps[:], ones2[:], rows(brow[:, :, KD:KD + D], r), start=True, stop=False)
                for k in range(DC):
                    for z in (z_hi, z_lo):
                        nc.tensor.matmul(ps[:, k * P:(k + 1) * P], z[:, u % 4, k, :], ident_r[:], start=False,
                                         stop=False)
                return r

            def up(n, u, r):
                pe.wait_ge(ht_lo_s, n + 1)
                for k in range(KD // P):
                    w = [rows(half[:, :, k, :], r) for half in (wu_hi, wu_lo)]
                    cols = slice(k * P, (k + 1) * P)
                    ins = mm3(u_ps[u % 2][:], (ht_hi[:, u % 2, cols], ht_lo[:, u % 2, cols]), w, False,
                              k == KD // P - 1)
                ins.then_inc(u_mm, 1)

            def unit(n, u, d, reuse):
                r = turn(n, u, reuse)
                if d:
                    down(n + 1, u + 1)
                up(n, u, r)

            down(0, 0)
            unit(0, 0, True, False)
            unit(1, 1, True, False)
            with pe.Fori(0, LOOPS) as k:
                for u in range(UNROLL):
                    unit(k * UNROLL + (2 + u), 2 + u, True, True)
            for n in range(LOOPS * UNROLL + 2, NPAIR):
                unit(n, n, n + 1 < NPAIR, True)


def kernel(**inputs):
    import numpy as np
    import concourse.bacc as bacc
    from concourse.bass_utils import run_bass_kernel_spmd

    a = {k.removeprefix("L0_cond_").removeprefix("L1_cond_"): np.asarray(v) for k, v in inputs.items()}

    def rows(w):
        return w.reshape(-1, P, w.shape[-1]).transpose(1, 0, 2)

    def blocks(w):
        k, n = w.shape
        return w.reshape(k // D, DC, P, n // P, P).transpose(3, 0, 2, 1, 4).reshape(-1, P, D)

    x = a["x"].reshape(NT, TOK, DC, P)
    arrays = {
        "xT": x.transpose(0, 3, 2, 1),
        "xk": a["x"].reshape(NT * NP, P, D),
        "w1c": blocks(a["cW1"]),
        "w1m": blocks(a["mW1"]),
        "w2c": a["cW2"].reshape(JH, P, D),
        "w2m": a["mW2"].reshape(JH, P, D),
        "wqT": rows(a["Wq"].T),
        "wkT": rows(a["Wk"].T),
        "wvT": rows(a["Wv"].T),
        "wp": rows(a["Wp"]),
        "bias": np.concatenate([a[n].reshape(-1, P).T for n in ("cb1", "mb1", "bp", "cb2", "mb2")], axis=1),
        "target": a["itok_B_17_1546"].reshape(1, B),
        "role": a["itok_B_1_2"].reshape(B, 1),
        "wd": a["W_down"].reshape(R, DC, P, KD).transpose(2, 0, 1, 3),
        "wu": a["W_up"].reshape(R, KD // P, P, D).transpose(2, 0, 1, 3),
        "bd": a["b_down"].reshape(1, R, KD),
        "bu": a["b_up"].reshape(1, R, D),
        "gamma": a["gamma"].reshape(1, R, D),
        "beta": a["beta"].reshape(1, R, D),
    }
    arrays = {n: np.ascontiguousarray(v) for n, v in arrays.items()}
    nc = bacc.Bacc("TRN2", target_bir_lowering=False, num_devices=1)
    args = [nc.dram_tensor(n, v.shape, mybir.dt.from_np(v.dtype), kind="ExternalInput").ap() for n, v in arrays.items()]
    out = nc.dram_tensor("out", (B, S, D), F32, kind="ExternalOutput").ap()
    program(nc, *args, out)
    r = run_bass_kernel_spmd(nc, [arrays], core_ids=[0])
    return r.results[0]["out"]
```

```python
from contextlib import ExitStack

import concourse.bass as bass
from concourse import mybir

P = 128
F32 = mybir.dt.float32
F32R = mybir.dt.float32r
I32 = mybir.dt.int32
ALU = mybir.AluOpType
ACT = mybir.ActivationFunctionType
AX_X = mybir.AxisListType.X

B, S, D = 64, 64, 512
H = 4 * D
R, KD = 3, 256
TOK = 512
NT = B * S // TOK
BT = TOK // S
DC = D // P
JH = H // P
NP = TOK // P
SCALE = float(D) ** -0.5
LN_EPS = 1e-5

W1_STAGE, W1_RING, W2_RING = 4, 8, 2
W1_AHEAD = 4
QT, QA, QC, QM = DC, DC, JH, 2 * JH
Q_PRE = QT + QA + QC
Q_ITER = QT + QM + QA + QC
G_PRE = DC + DC + JH
G_ITER = DC + JH + DC + JH

LATE = B - BT
NG = 2 * R
NPAIR = B // 2 + 2 * (R // 2)
NSLOT = 2 * NPAIR
UNROLL = 4
LOOPS = (NPAIR - 3) // UNROLL

CB1, MB1, BP, CB2, MB2 = 0, JH, 2 * JH, 2 * JH + DC, 2 * JH + 2 * DC
NBIAS = 2 * JH + 3 * DC


def program(nc, xT, xk, w1c, w1m, w2c, w2m, wqT, wkT, wvT, wp, bias, target, role,
            wd, wu, bd, bu, gamma, beta, out):
    wa_dram = nc.dram_tensor("wa_blocks", (2 * DC, P, D), F32).ap()
    z_dram = nc.dram_tensor("z_by_batch", (B, P, DC * S), F32).ap()

    ctx = ExitStack()
    with ctx:
        def sb(name, shape, dt=F32, on=ctx):
            return on.enter_context(nc.sbuf_tensor(name, shape, dt))

        def sem(name):
            return ctx.enter_context(nc.semaphore(name))

        def f32(ap):
            return ap.bitcast(F32)

        def hl(name, shape, on=ctx):
            return sb(name + "_hi", shape, F32R, on), sb(name + "_lo", shape, F32R, on)

        bias_sb = sb("bias_sb", [P, NBIAS])
        ident = sb("ident", [P, P])
        iota_p = sb("iota_p", [P, DC])
        iota_f = sb("iota_f", [P, NSLOT])
        ohb = sb("ohb", [P, DC, B])
        first_t = sb("first_t", [1, NPAIR], I32)
        second_t = sb("second_t", [1, NPAIR], I32)
        role_t = sb("role_t", [1, NPAIR], I32)

        brow = sb("brow", [2, R, KD + D], F32R)
        mhalf = sb("mhalf", [P, 1])
        ones2f = sb("ones2f", [2, P])
        ones2 = sb("ones2", [2, P], F32R)

        early = ExitStack()
        x_st = sb("x_st", [P, DC, TOK], on=early)
        x_hl = sb("x_hi_lo", [P, 2, DC, TOK], F32R, early)
        x_hi, x_lo = x_hl[:, 0], x_hl[:, 1]
        xk_st = sb("xk_st", [P, 2, D], on=early)
        xk_hi, xk_lo = hl("xk", [P, D], early)
        t_hi, t_lo = hl("t", [P, DC, TOK], early)
        y_hi, y_lo = hl("y", [P, DC, TOK], early)

        with ExitStack() as tile0:
            role_i = sb("role_i", [B, 1], I32, tile0)
            role_f = sb("role_f", [B, 1], on=tile0)
            batch_f = sb("batch_f", [B, 3], on=tile0)
            group_f = sb("group_f", [B, 1], on=tile0)
            onehot = sb("onehot", [B, NG], on=tile0)
            before = sb("before", [B, B], on=tile0)
            ones = sb("ones", [B, B], on=tile0)
            even = sb("even", [B, B // 2], on=tile0)
            flags = sb("flags", [B, B // 2], on=tile0)
            half = sb("half", [B, NG], on=tile0)
            start = sb("start", [B, NG], on=tile0)
            rank_r = sb("rank_r", [B, NG], on=tile0)
            rank = sb("rank", [B, 1], on=tile0)
            slot1 = sb("slot1", [B, NSLOT], on=tile0)
            slots = sb("slots", [1, 3, NPAIR, 2], on=tile0)
            empty = sb("empty", [1, NPAIR, 2], on=tile0)
            fill = sb("fill", [1, 3, NPAIR], on=tile0)
            pick = sb("pick", [1, 3, NPAIR], on=tile0)
            rows_f = sb("rows_f", [R, KD + D], on=tile0)
            rows_hi, rows_lo = hl("rows", [R, KD + D], tile0)
            wv_st = sb("wv_st", [P, DC, D], on=tile0)

        main = ExitStack()
        cf = sb("cf", [P, DC, TOK], on=main)
        zt = sb("zt", [P, 2, TOK], on=main)
        h_hi, h_lo = hl("h", [P, 2, TOK], main)
        w2_hi, w2_lo = hl("w2", [P, W2_RING, D], main)
        w2_st = sb("w2_st", [P, W2_RING, D], on=main)
        w1_st = sb("w1_st", [P, W1_STAGE, D], on=main)
        w1_hi, w1_lo = hl("w1", [P, W1_RING, D], main)
        a_hi, a_lo = hl("a", [P, DC, TOK], main)
        c_hi, c_lo = hl("c", [P, DC, TOK], main)
        xr = sb("xr", [P, DC, TOK], on=main)
        zb = sb("zb", [P, BT, DC, S], on=main)
        hf = sb("hf", [P, 2, TOK], on=main)
        mx = sb("mx", [P, 1], on=main)
        nmx = sb("nmx", [P, 1], on=main)
        rs = sb("rs", [P, 1], on=main)
        rinv = sb("rinv", [P, 1], on=main)
        pe_ = sb("p_exp", [P, P], on=main)
        pn = sb("p_norm", [P, P], on=main)
        s_sb = sb("s_sb", [P, S], on=main)
        y_sb = sb("y_sb", [P, DC, P], on=main)
        pt_hl = sb("pt_hi_lo", [P, 2, P], F32R, main)
        tgt_i = sb("tgt_i", [P, B], I32, main)
        tgt_f = sb("tgt_f", [P, B], on=main)
        main.close()
        early.close()

        wd_hi, wd_lo = hl("wd", [P, R, DC, KD])
        wu_hi, wu_lo = hl("wu", [P, R, KD // P, D])
        with ExitStack() as staging:
            l1_st = sb("l1_st", [P, R, DC * KD], on=staging)
        z_hi, z_lo = hl("z", [P, 2, DC, P])
        zf = sb("zf", [P, 4, DC, P])
        zs = sb("zs", [P, 4, 2, DC, S])
        sb("zt_place", [P, 2, TOK])
        hs = sb("hs", [P, 2, KD])
        ht_hi, ht_lo = hl("ht", [P, 2, KD])
        yg = sb("yg", [P, 2, D])
        sb("w2_end", [P, 3 * D])
        gam = sb("gam", [P, R, D])
        bet = sb("bet", [P, R, D])
        yo = sb("yo", [P, UNROLL, D])
        st6 = sb("st6", [P, 6])
        mv = sb("mv", [P, 2, 2])
        veps = sb("veps", [P, 2])
        rstd = sb("rstd", [P, 2])

        def bank(name):
            return ctx.enter_context(nc.psum_tensor(name, [P, 512], F32))

        hb = [bank("hb0"), bank("hb1")]
        acc = [bank(f"acc{c}") for c in range(DC)]
        sp_bank = bank("scores")
        y_bank = bank("yb")

        def s_parts(bank):
            return bank[:, 0:2 * P].rearrange("p (h n) -> p h n", h=2)

        def pt_part(bank):
            return bank[:, 2 * P:3 * P]

        def y_parts(bank):
            return bank[:].rearrange("p (c h n) -> p c h n", c=2, h=2)

        s_banks0 = [sp_bank, hb[1]]
        y_banks0 = [y_bank, hb[0]]
        d_ps = hb
        ht_ps = [sp_bank, y_bank]
        u_ps = acc

        w1_loaded = [sem(f"w1_loaded{k}") for k in range(W1_STAGE)]
        w2_loaded = [sem(f"w2_loaded{k}") for k in range(W2_RING)]
        w1_hi_s, w1_lo_s = sem("w1_hi_split"), sem("w1_lo_split")
        w2_hi_s, w2_lo_s = sem("w2_hi_split"), sem("w2_lo_split")
        h_mm = sem("h_mm")
        h_hi_s, h_lo_s = sem("h_hi_ready"), sem("h_lo_ready")
        acc_mm = sem("acc_mm")
        x0_loaded = sem("x_of_tile0_loaded")
        x_loaded, x_hi_s, x_lo_s = sem("x_loaded"), sem("x_hi_split"), sem("x_lo_split")
        xk_loaded = [sem("xk_loaded0"), sem("xk_loaded1")]
        xk_hi_s, xk_lo_s = sem("xk_hi_split"), sem("xk_lo_split")
        s_mm, s_sum, mx_s, nmx_s, exp_s = sem("scores_mm"), sem("scores_summed"), sem("row_max"), sem("neg_max"), sem("exp_done")
        rinv_s, pn_s = sem("row_inverse"), sem("p_normalised")
        pt_mm, pt_hi_s, pt_lo_s = sem("pt_mm"), sem("pt_hi_ready"), sem("pt_lo_ready")
        y_mm, y_sum, y_hi_s, y_lo_s = sem("y_mm"), sem("y_summed"), sem("y_hi_ready"), sem("y_lo_ready")
        cf_s, c_hi_s, c_lo_s = sem("cms_f32"), sem("cms_hi_ready"), sem("cms_lo_ready")
        xr_loaded, xr_sum = sem("xr_loaded"), sem("xr_summed")
        zt_s, z_ready, z_stored = sem("z_unclipped"), sem("z_ready"), sem("z_stored")
        const_in, const_s, pool_c = sem("constants_loaded"), sem("dve_constants"), sem("pool_constants")
        ohb_s, zero_p = sem("onehot_bias"), sem("p_exp_zeroed")
        qk_loaded = [sem(f"wq_wk_loaded{k}") for k in range(DC)]
        wv_loaded, wp_loaded = sem("wv_loaded"), sem("wp_loaded")
        qw_hi, qw_lo = sem("projection_hi"), sem("projection_lo")
        wa_mm, wa_out, wa_stored = sem("product_mm"), sem("product_out"), sem("product_stored")
        sort_in, sort_v, sort_mm, sorted_s = sem("roles_loaded"), sem("sort_vector"), sem("sort_mm"), sem("order_ready")
        l1_loaded, l1_hi, l1_lo = [sem("down_loaded"), sem("up_loaded")], sem("adapter_hi"), sem("adapter_lo")
        rows_loaded = sem("bias_rows_loaded")
        row_hi, row_lo, row_in = sem("bias_row_hi"), sem("bias_row_lo"), sem("bias_row_moved")
        gb_loaded, ones_s, mhalf_s = sem("gamma_beta_loaded"), sem("ones_ready"), sem("minus_half")
        zl = [sem(f"z_loaded{k}") for k in range(4)]
        zh_s, zl_s = sem("z_hi_split"), sem("z_lo_split")
        d_mm, gelu_s, ht_mm, ht_hi_s, ht_lo_s = sem("down_mm"), sem("gelu_done"), sem("ht_mm"), sem("ht_hi_ready"), sem("ht_lo_ready")
        u_mm, st_s, mv_s, ve_s = sem("up_mm"), sem("stats"), sem("mean_var"), sem("var_eps")
        rstd_s, yg_s, yo_s = sem("rstd"), sem("times_gamma"), sem("row_ready")
        a_stored = [sem(f"first_stored{k}") for k in range(UNROLL)]
        b_stored = [sem(f"second_stored{k}") for k in range(UNROLL)]

        zb_rows = zb[:].rearrange("p b c s -> p (b c s)").rearrange("p (k n) -> p k n", k=DC)

        def bcol(col):
            return bias_sb[:, col:col + 1]

        block = ctx.enter_context(nc.Block())

        @block.sync
        def _(sp):
            for k in range(DC):
                sp.dma_start(xr[:, k, :], wqT[:, k, :]).then_inc(qk_loaded[k], 16)
                sp.dma_start(zb_rows[:, k, :], wkT[:, k, :]).then_inc(qk_loaded[k], 16)
            sp.dma_start(x_st[:], xT[0]).then_inc(x0_loaded, 16)
            sp.dma_start(wv_st[:], wvT).then_inc(wv_loaded, 16)
            sp.dma_start(role_i[:], role).then_inc(sort_in, 16)
            sp.dma_start(bias_sb[:], bias).then_inc(const_in, 16)
            sp.dma_start(tgt_i[:], target.to_broadcast([P, B])).then_inc(const_in, 16)
            sp.wait_ge(qw_lo, 2 * DC)
            sp.dma_start(zb_rows, wp).then_inc(wp_loaded, 16)
            sp.wait_ge(row_lo, 1)
            for r in range(R):
                sp.dma_start(f32(brow[0:1, r, :]), f32(rows_hi[r:r + 1, :])).then_inc(row_in, 16)
                sp.dma_start(f32(brow[1:2, r, :]), f32(rows_lo[r:r + 1, :])).then_inc(row_in, 16)
            for k in range(2):
                sp.wait_ge(wa_out, DC * (k + 1))
                sp.dma_start(wa_dram[k * DC:(k + 1) * DC].rearrange("j p n -> p j n"), w1_st[:]).then_inc(wa_stored, 16)
            sp.wait_ge(wa_stored, 32)

            def load_w1(q, k, src, reuse=True):
                if reuse:
                    sp.wait_ge(w1_lo_s, q - (W1_STAGE - 1))
                sp.dma_start(w1_st[:, k % W1_STAGE, :], src).then_inc(w1_loaded[k % W1_STAGE], 16)

            def load_w2(n, k, src, reuse=True):
                if reuse:
                    sp.wait_ge(w2_lo_s, n - (W2_RING - 1))
                sp.dma_start(w2_st[:, k % W2_RING, :], src).then_inc(w2_loaded[k % W2_RING], 16)

            def head(q, n_end, src, w2_last, w2_next):
                for c in range(W1_AHEAD):
                    load_w1(q + c, c, src[c])
                    if w2_last is w2c:
                        load_w2(n_end - 3 + c, JH - 3 + c, w2_last[JH - 3 + c] if c < 3 else w2_next[0])
                    elif c % 2:
                        load_w2(n_end - 1 + c // 2, JH - 1 + c // 2, w2_last[JH - 1] if c == 1 else w2_next[0])

            def body_m(q, n):
                for k in range(W1_AHEAD, QM):
                    load_w1(q + k, k, w1m[k])
                    if k % 2:
                        j = (k - W1_AHEAD) // 2 + 1
                        load_w2(n + j, j, w2m[j])

            def body_c(q, n):
                for k in range(W1_AHEAD, QC):
                    load_w1(q + k, k, w1c[k])
                    load_w2(n + k - 3, k - 3, w2c[k - 3], reuse=not (isinstance(n, int) and k - 3 < W2_RING))

            for k in range(W1_AHEAD):
                load_w1(2 * DC + k, k, w1c[k])
            load_w2(0, 0, w2c[0], reuse=False)
            body_c(2 * DC, 0)
            with sp.Fori(0, NT - 1) as i:
                q = i * Q_ITER + Q_PRE
                n = i * (2 * JH) + JH
                head(q, n, wa_dram, w2c, w2m)
                for k in range(W1_AHEAD):
                    load_w1(q + QT + k, k, w1m[k])
                body_m(q + QT, n)
                head(q + QT + QM, n + JH, wa_dram[DC:2 * DC], w2m, w2c)
                for k in range(W1_AHEAD):
                    load_w1(q + QT + QM + QA + k, k, w1c[k])
                body_c(q + QT + QM + QA, n + JH)
            q, n = (NT - 1) * Q_ITER + Q_PRE, (NT - 1) * 2 * JH + JH
            head(q, n, w1m, w2c, w2m)
            body_m(q, n)
            load_w2(n + JH - 1, JH - 1, w2m[JH - 1])
            n_end = n + JH

            def load_z(n, slot):
                for k, table in enumerate((first_t, second_t)):
                    b = sp.value_load(table[0:1, bass.ds(n, 1)], min_val=0, max_val=B - 1)
                    sp.dma_start(zs[:, slot, k, :, :].rearrange("p c s -> p (c s)"),
                                 z_dram[bass.ds(b, 1)].rearrange("o p f -> (o p) f")).then_inc(zl[slot], 16)

            def store_second(n, u):
                b = sp.value_load(second_t[0:1, bass.ds(n, 1)], min_val=0, max_val=B - 1)
                dst = out[bass.ds(b, 1)].rearrange("o s d -> (o s) d")
                sp.wait_ge(a_stored[u % UNROLL], (n - u % UNROLL) * (16 // UNROLL) + 16)
                sp.dma_start(dst, yo[S:2 * S, u % UNROLL, :]).then_inc(b_stored[u % UNROLL], 16)

            sp.wait_ge(sorted_s, 3)
            sp.wait_ge(z_stored, (NT - 1) * 16)
            sp.wait_ge(xr_sum, NT * DC)
            sp.wait_ge(c_lo_s, NT * DC)
            for n in range(4):
                load_z(n, n)
            sp.wait_ge(w1_lo_s, q + QM)
            sp.wait_ge(w2_lo_s, n_end)
            sp.dma_start(gam[:], gamma.to_broadcast([P, R, D])).then_inc(gb_loaded, 16)
            sp.dma_start(bet[:], beta.to_broadcast([P, R, D])).then_inc(gb_loaded, 16)

            for n in range(2):
                sp.wait_ge(zl_s, n + 1)
                load_z(n + 4, n)

            def unit(m, u, load):
                if load:
                    sp.wait_ge(zl_s, m + 3)
                    load_z(m + 6, (u + 2) % 4)
                if not isinstance(m, int) or m:
                    store_second(m - 1, u + UNROLL - 1)

            sp.wait_ge(z_stored, NT * 16)
            unit(0, 0, True)
            sp_loops = (NPAIR - 7) // UNROLL
            with sp.Fori(0, sp_loops) as k:
                for u in range(UNROLL):
                    unit(k * UNROLL + (u + 1), u + 1, True)
            for m in range(sp_loops * UNROLL + 1, NPAIR):
                unit(m, m, m + 6 < NPAIR)
            store_second(NPAIR - 1, NPAIR - 1)
            for u in range(UNROLL):
                sp.wait_ge(b_stored[u], 16 * ((NPAIR - 1 - u) // UNROLL + 1))

        @block.gpsimd
        def _(pool):
            pool.dma_start(rows_f[:, 0:KD], bd).then_inc(rows_loaded, 16)
            pool.dma_start(rows_f[:, KD:KD + D], bu).then_inc(rows_loaded, 16)
            nc.gpsimd.memset(ident[:], 0.0).then_inc(pool_c, 1)
            nc.gpsimd.memset(before[:], 1.0).then_inc(pool_c, 1)
            nc.gpsimd.memset(mhalf[:], -0.5).then_inc(mhalf_s, 1)
            pool.wait_ge(pool_c, 2)
            pool.wait_ge(mhalf_s, 1)
            nc.gpsimd.affine_select(out=ident[:], in_=ident[:], compare_op=ALU.not_equal, fill=1.0,
                                    base=0, pattern=[[-1, P]], channel_multiplier=1).then_inc(pool_c, 1)
            nc.gpsimd.affine_select(out=before[:], in_=before[:], compare_op=ALU.is_gt, fill=0.0,
                                    base=0, pattern=[[1, B]], channel_multiplier=-1).then_inc(pool_c, 1)
            nc.gpsimd.iota(iota_p[:], pattern=[[P, DC]], base=0, channel_multiplier=1,
                           allow_small_or_imprecise_dtypes=True).then_inc(pool_c, 1)
            nc.gpsimd.iota(iota_f[:], pattern=[[1, NSLOT]], base=0, channel_multiplier=0,
                           allow_small_or_imprecise_dtypes=True).then_inc(pool_c, 1)
            nc.gpsimd.iota(even[:], pattern=[[2, B // 2]], base=0, channel_multiplier=0,
                           allow_small_or_imprecise_dtypes=True).then_inc(pool_c, 1)

            def load_xk(t, p):
                pool.dma_start(xk_st[:, p % 2, :], xk[bass.ds(t * NP + p, 1)].rearrange("o p d -> (o p) d")
                               ).then_inc(xk_loaded[p % 2], 16)

            pool.wait_ge(x0_loaded, 16)
            for p in range(NP):
                if p >= 2:
                    pool.wait_ge(xk_lo_s, p - 1)
                pool.dma_start(xk_st[:, p % 2, :], xk[p]).then_inc(xk_loaded[p % 2], 16)
            pool.dma_start(xr[:], xT[0]).then_inc(xr_loaded, 16)
            pool.dma_start(x_st[:], xT[1]).then_inc(x_loaded, 16)
            with pool.Fori(0, NT - 1) as i:
                for p in range(NP):
                    pool.wait_ge(xk_lo_s, i * NP + (NP + p - 1))
                    load_xk(i + 1, p)
                pool.wait_ge(x_lo_s, i * DC + 2 * DC)
                nxt = (i + 2) % NT
                pool.dma_start(x_st[:], xT[bass.ds(nxt, 1)].rearrange("o p c n -> (o p) c n")).then_inc(x_loaded, 16)
                pool.wait_ge(z_ready, i * DC + DC)
                pool.dma_start(z_dram[bass.ds(i * BT, BT)].rearrange("b p f -> p b f"),
                               zb[:].rearrange("p b c s -> p b (c s)")).then_inc(z_stored, 16)
                pool.wait_ge(z_stored, i * 16 + 16)
                pool.dma_start(xr[:], xT[bass.ds(i + 1, 1)].rearrange("o p c n -> (o p) c n")).then_inc(xr_loaded, 16)
            pool.wait_ge(x_lo_s, (NT + 1) * DC)
            pool.dma_start(l1_st[:], wd.rearrange("p r k n -> p r (k n)")).then_inc(l1_loaded[0], 16)
            pool.wait_ge(l1_lo, R)
            pool.dma_start(l1_st[:], wu.rearrange("p r k n -> p r (k n)")).then_inc(l1_loaded[1], 16)
            pool.wait_ge(z_ready, NT * DC)
            pool.dma_start(z_dram[(NT - 1) * BT:NT * BT].rearrange("b p f -> p b f"),
                           zb[:].rearrange("p b c s -> p b (c s)")).then_inc(z_stored, 16)

            def inverse_std(n, slot):
                pool.wait_ge(ve_s, n + 1)
                nc.gpsimd.tensor_tensor(rstd[:, slot:slot + 1], veps[:, slot:slot + 1], mhalf[:],
                                        ALU.pow).then_inc(rstd_s, 1)

            def store_first(n, u):
                b = pool.value_load(first_t[0:1, bass.ds(n, 1)], min_val=0, max_val=B - 1)
                dst = out[bass.ds(b, 1)].rearrange("o s d -> (o s) d")
                pool.wait_ge(yo_s, n + 1)
                pool.dma_start(dst, yo[0:S, u % UNROLL, :]).then_inc(a_stored[u % UNROLL], 16)

            inverse_std(0, 0)
            pool_loops = (NPAIR - 2) // UNROLL
            with pool.Fori(0, pool_loops) as k:
                for u in range(UNROLL):
                    store_first(k * UNROLL + u, u)
                    inverse_std(k * UNROLL + (u + 1), (u + 1) % 2)
            for n in range(pool_loops * UNROLL, NPAIR):
                store_first(n, n)
                if n + 1 < NPAIR:
                    inverse_std(n + 1, (n + 1) % 2)
            for u in range(UNROLL):
                pool.wait_ge(a_stored[u], 16 * ((NPAIR - 1 - u) // UNROLL + 1))

        @block.scalar
        def _(act):
            for k in range(DC):
                act.wait_ge(qk_loaded[k], 32)
                nc.scalar.copy(t_hi[:, k, :], xr[:, k, :]).then_inc(qw_hi, 1)
                nc.scalar.copy(y_hi[:, k, :], zb_rows[:, k, :]).then_inc(qw_hi, 1)

            def product(m):
                act.wait_ge(wa_mm, m + 1)
                if m == DC:
                    act.wait_ge(w1_lo_s, DC)
                    act.wait_ge(wa_stored, 16)
                k = m % DC
                nc.scalar.copy(w1_st[:, :, k * P:(k + 1) * P],
                               acc[k][:].rearrange("p (j n) -> p j n", j=DC)).then_inc(wa_out, 1)

            def split_w1(q, k):
                if isinstance(q, int) and q < 2 * DC:
                    act.wait_ge(wa_out, DC if q < DC else 2 * DC)
                else:
                    act.wait_ge(w1_loaded[k % W1_STAGE], (q - 2 * DC - k % W1_STAGE) * (16 // W1_STAGE) + 16)
                nc.scalar.copy(w1_hi[:, k % W1_RING, :], w1_st[:, k % W1_STAGE, :]).then_inc(w1_hi_s, 1)

            def split_w2(n, k):
                act.wait_ge(w2_loaded[k % W2_RING], (n - k % W2_RING) * (16 // W2_RING) + 16)
                act.wait_ge(acc_mm, n - 1)
                nc.scalar.copy(w2_hi[:, k % W2_RING, :], w2_st[:, k % W2_RING, :]).then_inc(w2_hi_s, 1)

            def split_x(t, c):
                if isinstance(t, int) and t == 0:
                    act.wait_ge(x0_loaded, 16)
                else:
                    act.wait_ge(x_loaded, t * 16)
                nc.scalar.copy(x_hi[:, c, :], x_st[:, c, :]).then_inc(x_hi_s, 1)

            def softmax(m):
                act.wait_ge(nmx_s, m + 1)
                for k in range(2):
                    r = slice(k * S, (k + 1) * S)
                    ins = nc.scalar.activation(pe_[r, r], s_sb[r, :], ACT.Exp, bias=nmx[r, :], scale=SCALE,
                                               accum_out=rs[r, :])
                ins.then_inc(exp_s, 1)

            def split_xk(m, p):
                act.wait_ge(xk_loaded[p % 2], (m - p % 2) * 8 + 16)
                nc.scalar.copy(xk_hi[:], xk_st[:, p % 2, :]).then_inc(xk_hi_s, 1)

            def split_pt(m, bank):
                act.wait_ge(pt_mm, m + 1)
                nc.scalar.copy(pt_hl[:, 0], pt_part(bank)).then_inc(pt_hi_s, 1)

            def split_y(m, p, h):
                act.wait_ge(y_sum, m * 2 + h + 1)
                nc.scalar.copy(y_hi[:, 2 * h:2 * h + 2, p * P:(p + 1) * P], y_sb[:, 2 * h:2 * h + 2]).then_inc(y_hi_s, 1)

            def attention(m, s):
                p = s // 4
                if s % 4 == 0:
                    softmax(m + p)
                if s % 4 == 1:
                    split_pt(m + p, sp_bank)
                    split_xk(m + p, p)
                if s % 4 == 2:
                    split_y(m + p, p, 0)
                    split_y(m + p, p, 1)

            def stage_a(g, q, pos):
                for c in range(DC):
                    act.wait_ge(h_mm, g + c + 1)
                    nc.scalar.activation(a_hi[:, c, :], hb[c % 2][:], ACT.Identity,
                                         bias=bcol(BP + c)).then_inc(h_hi_s, 1)
                    split_w1(q + c + W1_AHEAD, pos + c + W1_AHEAD)

            def gelu(g, j, col):
                act.wait_ge(h_mm, g + j + 1)
                act.wait_ge(h_lo_s, g + j - 1)
                nc.scalar.activation(h_hi[:, j % 2, :], hb[j % 2][:], ACT.Gelu, bias=bcol(col + j))
                nc.scalar.activation(hf[:, j % 2, :], hb[j % 2][:], ACT.Gelu,
                                     bias=bcol(col + j)).then_inc(h_hi_s, 1)

            def stage_c(g, q, pos, n, x_next):
                for j in range(JH):
                    split_w1(q + j + W1_AHEAD, pos + j + W1_AHEAD)
                    gelu(g, j, CB1)
                    split_w2(n + j + 1, j + 1)
                    if 4 <= j < 4 + DC:
                        split_x(x_next, j - 4)

            def stage_m(g, q, pos, n, pair, last=False):
                for j in range(JH):
                    for k in (2 * j, 2 * j + 1):
                        if not last or k + W1_AHEAD < QM:
                            split_w1(q + k + W1_AHEAD, pos + k + W1_AHEAD)
                    gelu(g, j, MB1)
                    if not last or j + 1 < JH:
                        split_w2(n + j + 1, j + 1)
                    if pair is not None:
                        attention(pair, j)
                    if last:
                        split_l1(j)
                        if j >= JH - 2:
                            split_z(j - (JH - 2), j - (JH - 2))

            def split_l1(j):
                for load, w, j0 in ((0, wd_hi, 4), (1, wu_hi, 10)):
                    if j0 <= j < j0 + R:
                        act.wait_ge(l1_loaded[load], 16)
                        nc.scalar.copy(w[:, j - j0].rearrange("p k n -> p (k n)"), l1_st[:, j - j0, :]).then_inc(l1_hi, 1)

            def split_z(n, u):
                if isinstance(n, int) and n < 2:
                    act.wait_ge(l1_lo, 2 * R)
                slot = u % 4
                act.wait_ge(zl[slot], (n - slot) * 8 + 32)
                src = zs[:, slot].rearrange("p k c s -> p c k s")
                nc.scalar.copy(z_hi[:, u % 2].rearrange("p c (k s) -> p c k s", k=2), src)
                nc.scalar.copy(zf[:, slot].rearrange("p c (k s) -> p c k s", k=2), src).then_inc(zh_s, 1)

            def cms_hi(t):
                for c in range(DC):
                    act.wait_ge(cf_s, t * DC + c + 1)
                    nc.scalar.copy(c_hi[:, c, :], cf[:, c, :]).then_inc(c_hi_s, 1)

            for c in range(DC):
                split_x(0, c)
            for m in (1, 3):
                product(m)
            for k in range(DC):
                split_w1(k, k)
            act.wait_ge(wv_loaded, 16)
            for c in range(DC):
                act.wait_ge(h_mm, c + 1)
                nc.scalar.copy(t_hi[:, c, :], hb[c % 2][:]).then_inc(h_hi_s, 1)
                if c == 0:
                    act.wait_ge(wp_loaded, 16)
                nc.scalar.copy(a_hi[:, c, :], wv_st[:, c, :]).then_inc(qw_hi, 1)
                nc.scalar.copy(c_hi[:, c, :], zb_rows[:, c, :]).then_inc(qw_hi, 1)
            act.wait_ge(zero_p, 1)
            softmax(0)
            for p in range(NP):
                split_pt(p, s_banks0[p % 2])
                split_xk(p, p)
                if p:
                    split_y(p - 1, p - 1, 0)
                    split_y(p - 1, p - 1, 1)
                if p + 1 < NP:
                    softmax(p + 1)
                product(DC + p)
            for k in range(2):
                split_w1(DC + k, DC + k)
            split_y(NP - 1, NP - 1, 0)
            split_y(NP - 1, NP - 1, 1)
            for k in range(2, DC):
                split_w1(DC + k, DC + k)
            stage_a(DC, QT, QT)
            act.wait_ge(row_in, 2 * R * 16)
            act.wait_ge(w2_loaded[0], 16)
            nc.scalar.copy(w2_hi[:, 0, :], w2_st[:, 0, :]).then_inc(w2_hi_s, 1)
            for j in range(JH):
                split_w1(QT + QA + j + W1_AHEAD, j + W1_AHEAD)
                gelu(2 * DC, j, CB1)
                if j == 0:
                    act.wait_ge(w2_loaded[1], 16)
                    nc.scalar.copy(w2_hi[:, 1, :], w2_st[:, 1, :]).then_inc(w2_hi_s, 1)
                else:
                    split_w2(j + 1, j + 1)
                if 4 <= j < 4 + DC:
                    split_x(1, j - 4)
            with act.Fori(0, NT - 1) as i:
                g = i * G_ITER + G_PRE
                q = i * Q_ITER + Q_PRE
                n = i * (2 * JH) + JH
                for c in range(DC):
                    for e in ((), (0, 1), (2,), (3,))[c]:
                        act.wait_ge(cf_s, i * DC + e + 1)
                        nc.scalar.copy(c_hi[:, e, :], cf[:, e, :]).then_inc(c_hi_s, 1)
                    act.wait_ge(h_mm, g + c + 1)
                    nc.scalar.copy(t_hi[:, c, :], hb[c % 2][:]).then_inc(h_hi_s, 1)
                    split_w1(q + c + W1_AHEAD, c + W1_AHEAD)
                stage_m(g + DC, q + QT, QT, n, i * NP + NP)
                stage_a(g + DC + JH, q + QT + QM, QT + QM)
                stage_c(g + 2 * DC + JH, q + QT + QM + QA, 0, n + JH, i + 2)
            cms_hi(NT - 1)
            g, q, n = (NT - 1) * G_ITER + G_PRE, (NT - 1) * Q_ITER + Q_PRE, (NT - 1) * 2 * JH + JH
            stage_m(g, q, 0, n, None, last=True)

            def gelu_pair(n, slot):
                act.wait_ge(d_mm, n + 1)
                nc.scalar.activation(hs[:, slot, :], d_ps[slot][:, 0:KD], ACT.Gelu).then_inc(gelu_s, 1)

            def unit(n, u, z, d):
                act.wait_ge(ht_mm, n + 1)
                nc.scalar.copy(ht_hi[:, u % 2, :], ht_ps[u % 2][:, 0:KD]).then_inc(ht_hi_s, 1)
                if z:
                    split_z(n + 2, u + 2)
                if d:
                    gelu_pair(n + 1, (u + 1) % 2)

            gelu_pair(0, 0)
            for n in range(2):
                unit(n, n, True, True)
            with act.Fori(0, LOOPS) as k:
                for u in range(UNROLL):
                    unit(k * UNROLL + (2 + u), 2 + u, True, True)
            for n in range(LOOPS * UNROLL + 2, NPAIR):
                unit(n, n, n + 2 < NPAIR, n + 1 < NPAIR)

        @block.vector
        def _(dve):
            nc.vector.memset(pe_[:], 0.0).then_inc(zero_p, 1)
            nc.vector.memset(ones[:], 1.0).then_inc(const_s, 1)
            dve.wait_ge(pool_c, 7)

            def split_projection(n, lo, hi, src):
                dve.wait_ge(qw_hi, n + 1)
                nc.vector.tensor_tensor(lo, src, f32(hi), ALU.subtract).then_inc(qw_lo, 1)

            nc.vector.memset(ones2f[:], 1.0).then_inc(ones_s, 1)
            dve.wait_ge(ones_s, 1)
            nc.vector.tensor_copy(ones2[:], ones2f[:]).then_inc(ones_s, 1)
            for k in range(DC):
                split_projection(2 * k, t_lo[:, k, :], t_hi[:, k, :], xr[:, k, :])
                split_projection(2 * k + 1, y_lo[:, k, :], y_hi[:, k, :], zb_rows[:, k, :])

            def product(k):
                dve.wait_ge(wa_mm, k + 1)
                nc.vector.tensor_copy(w1_st[:, :, k * P:(k + 1) * P],
                                      acc[k][:].rearrange("p (j n) -> p j n", j=DC)).then_inc(wa_out, 1)

            def onehot_bias():
                dve.wait_ge(const_in, 32)
                nc.vector.tensor_copy(tgt_f[:], tgt_i[:]).then_inc(const_s, 1)
                dve.wait_ge(const_s, 2)
                for c in range(DC):
                    nc.vector.tensor_scalar(ohb[:, c, :], tgt_f[:], iota_p[:, c:c + 1], bcol(CB2 + c),
                                            ALU.is_equal, ALU.add).then_inc(ohb_s, 1)

            did = [0]

            def link(ins):
                did[0] += 1
                ins.then_inc(sort_v, 1)
                dve.wait_ge(sort_v, did[0])

            def sort_groups():
                dve.wait_ge(sort_in, 16)
                link(nc.vector.tensor_copy(role_f[:], role_i[:]))
                link(nc.vector.tensor_scalar(role_f[:], role_f[:], 0.0, float(R - 1), ALU.max, ALU.min))
                link(nc.vector.tensor_copy(batch_f[:, 0:1], iota_p[0:B, 0:1]))
                link(nc.vector.memset(batch_f[:, 1:2], 1.0))
                link(nc.vector.tensor_copy(batch_f[:, 2:3], role_f[:]))
                link(nc.vector.tensor_scalar(group_f[:], batch_f[:, 0:1], float(LATE), float(R), ALU.is_ge, ALU.mult))
                link(nc.vector.tensor_tensor(group_f[:], group_f[:], role_f[:], ALU.add))
                link(nc.vector.tensor_scalar(onehot[:], iota_f[0:B, 0:NG], group_f[:], None, ALU.is_equal))

            def sort_slots():
                dve.wait_ge(sort_mm, 2)
                for r in range(NG):
                    link(nc.vector.tensor_scalar(flags[:], even[:], y_bank[0:B, NG + r:NG + r + 1], None, ALU.is_lt))
                    link(nc.vector.reduce_sum(half[:, r:r + 1], flags[:], AX_X))
                link(nc.vector.memset(start[:, 0:1], 0.0))
                for r in range(1, NG):
                    link(nc.vector.scalar_tensor_tensor(out=start[:, r:r + 1], in0=half[:, r - 1:r], scalar=2.0,
                                                        in1=start[:, r - 1:r], op0=ALU.mult, op1=ALU.add))
                link(nc.vector.tensor_tensor(rank_r[:], y_bank[0:B, 0:NG], start[:], ALU.add))
                link(nc.vector.tensor_tensor(rank_r[:], rank_r[:], onehot[:], ALU.mult))
                link(nc.vector.reduce_sum(rank[:], rank_r[:], AX_X))
                link(nc.vector.tensor_scalar(slot1[:], iota_f[0:B, :], rank[:], None, ALU.is_equal))

            def sort_pairs():
                dve.wait_ge(sort_mm, 3)
                link(nc.vector.tensor_copy(slots[:].rearrange("o v n k -> o (v n k)"), y_bank[0:1, 64:64 + 3 * NSLOT]))
                link(nc.vector.tensor_scalar(empty[:], slots[:, 1], -1.0, 1.0, ALU.mult, ALU.add))
                for v, w in ((0, 0), (2, 1)):
                    link(nc.vector.tensor_scalar(fill[:, w], empty[:, :, 0], slots[:, v, 0, 0:1], None, ALU.mult))
                    link(nc.vector.tensor_tensor(pick[:, w], fill[:, w], slots[:, v, :, 0], ALU.add))
                link(nc.vector.tensor_tensor(fill[:, 2], empty[:, :, 1], pick[:, 0], ALU.mult))
                link(nc.vector.tensor_tensor(pick[:, 2], fill[:, 2], slots[:, 0, :, 1], ALU.add))
                nc.vector.tensor_copy(first_t[:], pick[:, 0]).then_inc(sorted_s, 1)
                nc.vector.tensor_copy(role_t[:], pick[:, 1]).then_inc(sorted_s, 1)
                nc.vector.tensor_copy(second_t[:], pick[:, 2]).then_inc(sorted_s, 1)

            def split_w1(q, k):
                dve.wait_ge(w1_hi_s, q + 1)
                nc.vector.tensor_tensor(w1_lo[:, k % W1_RING, :], w1_st[:, k % W1_STAGE, :],
                                        f32(w1_hi[:, k % W1_RING, :]), ALU.subtract).then_inc(w1_lo_s, 1)

            def split_w2(n, k):
                dve.wait_ge(w2_hi_s, n + 1)
                nc.vector.tensor_tensor(w2_lo[:, k % W2_RING, :], w2_st[:, k % W2_RING, :],
                                        f32(w2_hi[:, k % W2_RING, :]), ALU.subtract).then_inc(w2_lo_s, 1)

            def split_x(t, c):
                dve.wait_ge(x_hi_s, t * DC + c + 1)
                nc.vector.tensor_tensor(x_lo[:, c, :], x_st[:, c, :], f32(x_hi[:, c, :]),
                                        ALU.subtract).then_inc(x_lo_s, 1)

            def row_max(m, bank):
                dve.wait_ge(s_mm, m + 1)
                parts = s_parts(bank).rearrange("p h n -> p n h")
                for k in range(2):
                    r = slice(k * S, (k + 1) * S)
                    ins = nc.vector.reduce_sum(s_sb[r, :], parts[r, r, :], AX_X)
                ins.then_inc(s_sum, 1)
                dve.wait_ge(s_sum, m + 1)
                nc.vector.reduce_max(mx[:], s_sb[:], AX_X).then_inc(mx_s, 1)
                dve.wait_ge(mx_s, m + 1)
                nc.vector.tensor_scalar(nmx[:], mx[:], -SCALE, None, ALU.mult).then_inc(nmx_s, 1)

            def normalise_p(m):
                dve.wait_ge(exp_s, m + 1)
                nc.vector.reciprocal(rinv[:], rs[:]).then_inc(rinv_s, 1)
                dve.wait_ge(rinv_s, m + 1)
                nc.vector.tensor_scalar(pn[:], pe_[:], rinv[:], None, ALU.mult).then_inc(pn_s, 1)

            def split_xk(m, p):
                dve.wait_ge(xk_hi_s, m + 1)
                nc.vector.tensor_tensor(xk_lo[:], xk_st[:, p % 2, :], f32(xk_hi[:]),
                                        ALU.subtract).then_inc(xk_lo_s, 1)

            def split_pt(m, bank):
                dve.wait_ge(pt_hi_s, m + 1)
                nc.vector.tensor_tensor(pt_hl[:, 1], pt_part(bank), f32(pt_hl[:, 0]), ALU.subtract).then_inc(pt_lo_s, 1)

            def sum_y(m, h, bank):
                dve.wait_ge(y_mm, m * 2 + h + 1)
                nc.vector.reduce_sum(y_sb[:, 2 * h:2 * h + 2], y_parts(bank).rearrange("p c h n -> p c n h"),
                                     AX_X).then_inc(y_sum, 1)

            def split_y(m, p, h):
                dve.wait_ge(y_hi_s, m * 2 + h + 1)
                half = (slice(None), slice(2 * h, 2 * h + 2), slice(p * P, (p + 1) * P))
                nc.vector.tensor_tensor(y_lo[half], y_sb[:, 2 * h:2 * h + 2], f32(y_hi[half]),
                                        ALU.subtract).then_inc(y_lo_s, 1)

            def attention(m, s):
                p = s // 4
                if s % 4 == 0:
                    row_max(m + p, sp_bank)
                    normalise_p(m + p)
                if s % 4 == 1:
                    split_pt(m + p, sp_bank)
                    split_xk(m + p, p)
                if s % 4 == 2:
                    split_y(m + p, p, 0)
                    sum_y(m + p, 1, y_bank)
                    split_y(m + p, p, 1)

            def t_lo_half(g, c):
                dve.wait_ge(h_hi_s, g + c + 1)
                nc.vector.tensor_tensor(t_lo[:, c, :], hb[c % 2][:], f32(t_hi[:, c, :]),
                                        ALU.subtract).then_inc(h_lo_s, 1)

            def stage_a(g, q, pos, between=None):
                for c in range(DC):
                    dve.wait_ge(h_hi_s, g + c + 1)
                    nc.vector.scalar_tensor_tensor(out=a_lo[:, c, :], in0=hb[c % 2][:], scalar=bcol(BP + c),
                                                   in1=f32(a_hi[:, c, :]), op0=ALU.add,
                                                   op1=ALU.subtract).then_inc(h_lo_s, 1)
                    split_w1(q + c + W1_AHEAD, pos + c + W1_AHEAD)
                    if between:
                        between(c)

            def h_lo_half(g, j):
                dve.wait_ge(h_hi_s, g + j + 1)
                nc.vector.tensor_tensor(h_lo[:, j % 2, :], hf[:, j % 2, :], f32(h_hi[:, j % 2, :]),
                                        ALU.subtract).then_inc(h_lo_s, 1)

            def stage_c(g, q, pos, n, x_next, more={}, t=None):
                for j in range(JH):
                    if j == 0 and t is not None:
                        h_lo_half(g, j)
                        z_clip(t, DC - 2)
                        z_clip(t, DC - 1)
                    split_w1(q + j + W1_AHEAD, pos + j + W1_AHEAD)
                    if j or t is None:
                        h_lo_half(g, j)
                    split_w2(n + j + 1, j + 1)
                    if 4 <= j < 4 + DC:
                        split_x(x_next, j - 4)
                    if j in more:
                        more[j]()

            def stage_m(g, q, pos, n, t, pair, last=False):
                for j in range(JH):
                    for k in (2 * j, 2 * j + 1):
                        if not last or k + W1_AHEAD < QM:
                            split_w1(q + k + W1_AHEAD, pos + k + W1_AHEAD)
                    if pair is not None and j % 4 == 2:
                        sum_y(pair + j // 4, 0, y_bank)
                    h_lo_half(g, j)
                    if 1 <= j <= DC:
                        add_x(t, j - 1)
                    if not last or j + 1 < JH:
                        split_w2(n + j + 1, j + 1)
                    if pair is not None:
                        attention(pair, j)
                    if last:
                        split_l1(j)
                        if j >= JH - 2:
                            split_z(j - (JH - 2), j - (JH - 2))

            def split_l1(j):
                for w_hi, w_lo, j0, at in ((wd_hi, wd_lo, 4, 0), (wu_hi, wu_lo, 10, R)):
                    if j0 <= j < j0 + R:
                        r = j - j0
                        dve.wait_ge(l1_hi, at + r + 1)
                        nc.vector.tensor_tensor(w_lo[:, r].rearrange("p k n -> p (k n)"), l1_st[:, r, :],
                                                f32(w_hi[:, r]).rearrange("p k n -> p (k n)"),
                                                ALU.subtract).then_inc(l1_lo, 1)

            def split_z(n, u):
                dve.wait_ge(zh_s, n + 1)
                nc.vector.tensor_tensor(z_lo[:, u % 2], zf[:, u % 4], f32(z_hi[:, u % 2]), ALU.subtract).then_inc(zl_s, 1)

            def batches(ap):
                return ap.rearrange("p (b s) -> p b s", s=S)

            def cms_f32(t, c, n_end):
                if c == 0:
                    dve.wait_ge(acc_mm, n_end)
                oh = ohb[:, c, bass.ds(t * BT, BT)]
                nc.vector.tensor_tensor(batches(cf[:, c, :]), batches(acc[c][:]),
                                        oh.unsqueeze(2).to_broadcast([P, BT, S]),
                                        ALU.add).then_inc(cf_s, 1)

            def add_x(t, c):
                dve.wait_ge(cf_s, t * DC + c + 1)
                dve.wait_ge(xr_loaded, t * 16 + 16)
                nc.vector.tensor_tensor(xr[:, c, :], xr[:, c, :], cf[:, c, :], ALU.add).then_inc(xr_sum, 1)

            def cms_lo(t, c):
                dve.wait_ge(c_hi_s, t * DC + c + 1)
                nc.vector.tensor_tensor(c_lo[:, c, :], cf[:, c, :], f32(c_hi[:, c, :]),
                                        ALU.subtract).then_inc(c_lo_s, 1)

            def z_sum(t, c, n_end):
                if c == 0:
                    dve.wait_ge(acc_mm, n_end)
                    dve.wait_ge(xr_sum, t * DC + DC)
                if c >= 2:
                    dve.wait_ge(z_ready, t * DC + c - 1)
                nc.vector.scalar_tensor_tensor(out=zt[:, c % 2, :], in0=acc[c][:], scalar=bcol(MB2 + c),
                                               in1=xr[:, c, :], op0=ALU.add, op1=ALU.add).then_inc(zt_s, 1)

            def z_clip(t, c):
                dve.wait_ge(zt_s, t * DC + c + 1)
                nc.vector.tensor_scalar(zb[:, :, c, :], batches(zt[:, c % 2, :]), 0.0, 1.0,
                                        ALU.max, ALU.min).then_inc(z_ready, 1)

            def z_chunk(t, c, n_end):
                z_sum(t, c, n_end)
                z_clip(t, c)

            for c in range(DC):
                split_x(0, c)
            dve.wait_ge(rows_loaded, 32)
            nc.vector.tensor_copy(rows_hi[:], rows_f[:]).then_inc(row_hi, 1)
            dve.wait_ge(row_hi, 1)
            nc.vector.tensor_tensor(rows_lo[:], rows_f[:], f32(rows_hi[:]), ALU.subtract).then_inc(row_lo, 1)
            for m in (0, 2):
                product(m)
            for k in range(DC):
                split_w1(k, k)
            for c in range(DC):
                t_lo_half(0, c)
                split_projection(2 * DC + 2 * c, a_lo[:, c, :], a_hi[:, c, :], wv_st[:, c, :])
                split_projection(2 * DC + 2 * c + 1, c_lo[:, c, :], c_hi[:, c, :], zb_rows[:, c, :])
            row_max(0, s_banks0[0])
            normalise_p(0)
            for p in range(NP):
                split_pt(p, s_banks0[p % 2])
                split_xk(p, p)
                if p + 1 < NP:
                    row_max(p + 1, s_banks0[(p + 1) % 2])
                if p:
                    split_y(p - 1, p - 1, 0)
                    split_y(p - 1, p - 1, 1)
                if p + 1 < NP:
                    normalise_p(p + 1)
                else:
                    for k in range(2):
                        split_w1(DC + k, DC + k)
                for h in range(2):
                    sum_y(p, h, y_banks0[h])
            split_y(NP - 1, NP - 1, 0)
            split_y(NP - 1, NP - 1, 1)
            for k in range(2, DC):
                split_w1(DC + k, DC + k)
            stage_a(DC, QT, QT)
            split_w2(0, 0)
            stage_c(2 * DC, QT + QA, 0, 0, 1, {1: sort_groups, 3: onehot_bias, 6: sort_slots, 12: sort_pairs})
            dve.wait_ge(ohb_s, DC)
            with dve.Fori(0, NT - 1) as i:
                g = i * G_ITER + G_PRE
                q = i * Q_ITER + Q_PRE
                n = i * (2 * JH) + JH
                t_lo_half(g, 0)
                split_w1(q + W1_AHEAD, W1_AHEAD)
                cms_f32(i, 0, n)
                cms_f32(i, 1, n)
                cms_lo(i, 0)
                t_lo_half(g, 1)
                split_w1(q + 1 + W1_AHEAD, 1 + W1_AHEAD)
                cms_f32(i, 2, n)
                cms_lo(i, 1)
                t_lo_half(g, 2)
                split_w1(q + 2 + W1_AHEAD, 2 + W1_AHEAD)
                cms_f32(i, 3, n)
                cms_lo(i, 2)
                t_lo_half(g, 3)
                split_w1(q + 3 + W1_AHEAD, 3 + W1_AHEAD)
                cms_lo(i, 3)
                stage_m(g + DC, q + QT, QT, n, i, i * NP + NP)
                def z_between(c):
                    if c in (1, 2):
                        z_chunk(i, c - 1, n + JH)
                    if c == DC - 1:
                        z_sum(i, DC - 2, n + JH)
                        z_sum(i, DC - 1, n + JH)

                qa, ga = q + QT + QM, g + DC + JH
                stage_a(ga, qa, QT + QM, between=z_between)
                stage_c(ga + DC, qa + QA, 0, n + JH, i + 2, t=i)
            g, q, n = (NT - 1) * G_ITER + G_PRE, (NT - 1) * Q_ITER + Q_PRE, (NT - 1) * 2 * JH + JH
            for c in range(DC):
                cms_f32(NT - 1, c, n)
                if c:
                    cms_lo(NT - 1, c - 1)
            cms_lo(NT - 1, DC - 1)
            stage_m(g, q, 0, n, NT - 1, None, last=True)
            n_end = n + JH
            def stats(n, u):
                dve.wait_ge(u_mm, n + 1)
                nc.vector.bn_stats(st6[:], u_ps[u % 4][:]).then_inc(st_s, 1)

            def moments(n, slot):
                nc.vector.bn_aggr(mv[:, slot], st6[:]).then_inc(mv_s, 1)
                dve.wait_ge(mv_s, n + 1)
                nc.vector.tensor_scalar(veps[:, slot:slot + 1], mv[:, slot, 1:2], LN_EPS, None, ALU.add).then_inc(ve_s, 1)

            def of_role(table, r):
                return table[:, bass.ds(r, 1), :].rearrange("p o d -> p (o d)")

            def centre(n, u, r):
                nc.vector.scalar_tensor_tensor(out=yg[:, u % 2, :], in0=u_ps[u % 4][:], scalar=mv[:, u % 2, 0:1],
                                               in1=of_role(gam, r), op0=ALU.subtract, op1=ALU.mult).then_inc(yg_s, 1)

            def scale_shift(n, u, r, reuse):
                if reuse:
                    dve.wait_ge(b_stored[u % 4], (n - u % 4) * (16 // UNROLL))
                dve.wait_ge(yg_s, n + 1)
                dve.wait_ge(rstd_s, n + 1)
                nc.vector.scalar_tensor_tensor(out=yo[:, u % 4, :], in0=yg[:, u % 2, :], scalar=rstd[:, u % 2:u % 2 + 1],
                                               in1=of_role(bet, r), op0=ALU.mult, op1=ALU.add).then_inc(yo_s, 1)

            def unit(n, u, z, tail, reuse):
                if tail:
                    r = dve.value_load(role_t[0:1, bass.ds(n - 1, 1)], min_val=0, max_val=R - 1)
                    stats(n - 1, u - 1)
                    dve.wait_ge(st_s, n)
                dve.wait_ge(ht_hi_s, n + 1)
                nc.vector.tensor_tensor(ht_lo[:, u % 2, :], ht_ps[u % 2][:, 0:KD], f32(ht_hi[:, u % 2, :]),
                                        ALU.subtract).then_inc(ht_lo_s, 1)
                if tail:
                    moments(n - 1, (u - 1) % 2)
                    centre(n - 1, u - 1, r)
                if z:
                    split_z(n + 2, u + 2)
                if tail:
                    scale_shift(n - 1, u - 1, r, reuse)

            for c in range(2):
                z_chunk(NT - 1, c, n_end)
            unit(0, 0, True, False, False)
            for c in range(2, DC):
                z_chunk(NT - 1, c, n_end)
            dve.wait_ge(gb_loaded, 32)
            for n in range(1, 5):
                unit(n, n, True, True, False)
            dve_loops = (NPAIR - 7) // UNROLL
            with dve.Fori(0, dve_loops) as k:
                for u in range(UNROLL):
                    unit(k * UNROLL + (5 + u), 5 + u, True, True, True)
            for n in range(dve_loops * UNROLL + 5, NPAIR):
                unit(n, n, n + 2 < NPAIR, True, True)
            last = NPAIR - 1
            r = dve.value_load(role_t[0:1, last:last + 1], min_val=0, max_val=R - 1)
            stats(last, last)
            dve.wait_ge(st_s, NPAIR)
            moments(last, last % 2)
            centre(last, last, r)
            scale_shift(last, last, r, True)

        @block.tensor
        def _(pe):
            def mm3(ps, w, x, first, last):
                nc.tensor.matmul(ps, w[0], x[0], start=first, stop=False)
                nc.tensor.matmul(ps, w[0], x[1], start=False, stop=False)
                return nc.tensor.matmul(ps, w[1], x[0], start=False, stop=last)

            def chunk(pair, k, cols):
                return [half[:, k, cols] for half in pair]

            ALL = slice(0, TOK)

            def w1_block(k, c):
                cols = slice(c * P, (c + 1) * P)
                return w1_hi[:, k % W1_RING, cols], w1_lo[:, k % W1_RING, cols]

            def product_rows(m, k, lhs, rhs):
                rows = slice(m * P, (m + 1) * P)
                ins = mm3(acc[m][:], chunk(lhs, k, rows), chunk(rhs, k, ALL), k == 0, k == DC - 1)
                if k == DC - 1:
                    ins.then_inc(wa_mm, 1)

            def product2(m):
                if m == 0:
                    pe.wait_ge(wa_out, DC)
                for k in range(DC):
                    if m == 0:
                        pe.wait_ge(qw_lo, 2 * DC + 2 * k + 2)
                    product_rows(m, k, (a_hi, a_lo), (c_hi, c_lo))

            def sort_counts():
                pe.wait_ge(sort_v, 8)
                nc.tensor.matmul(y_bank[0:B, 0:NG], before[:], onehot[:], start=True, stop=True).then_inc(sort_mm, 1)
                nc.tensor.matmul(y_bank[0:B, NG:2 * NG], ones[:], onehot[:], start=True, stop=True).then_inc(sort_mm, 1)

            def sort_gather():
                pe.wait_ge(sort_v, 8 + 2 * NG + 1 + (NG - 1) + 4)
                for v in range(3):
                    ins = nc.tensor.matmul(y_bank[0:1, 64 + v * NSLOT:64 + (v + 1) * NSLOT], batch_f[:, v:v + 1],
                                           slot1[:], start=True, stop=True)
                ins.then_inc(sort_mm, 1)

            def project(g, c, w, x, first=None, before=None):
                if first is not None:
                    pe.wait_ge(w1_lo_s, first)
                else:
                    pe.wait_ge(h_lo_s, g + c - 1)
                for k in range(DC):
                    if before:
                        before(k)
                    ins = mm3(hb[c % 2][:], w1_block(w + c, k), chunk(x, k, ALL), k == 0, k == DC - 1)
                ins.then_inc(h_mm, 1)

            def half_step(pos, bank, kq, x, first, last, ready=None, before=None):
                for k in range(DC):
                    if ready is not None and k in (0, DC - 1):
                        pe.wait_ge(h_lo_s, ready - (k == 0))
                    if before:
                        before(k)
                    ins = mm3(hb[bank][:], w1_block(pos + kq, k), chunk(x, k, ALL), first and k == 0, last and k == DC - 1)
                if last:
                    ins.then_inc(h_mm, 1)

            def second_layer(g_next, j, free=None):
                pe.wait_ge(h_lo_s, g_next)
                if free is not None:
                    pe.wait_ge(*free)
                for c in range(DC):
                    cols = slice(c * P, (c + 1) * P)
                    ins = mm3(acc[c][:], (w2_hi[:, j % W2_RING, cols], w2_lo[:, j % W2_RING, cols]),
                              (h_hi[:, j % 2, :], h_lo[:, j % 2, :]), j == 0, j == JH - 1)
                ins.then_inc(acc_mm, 1)

            def scores(m, p, bank, before=None):
                cols = slice(p * P, (p + 1) * P)
                wide = s_parts(bank)
                rest = wide[:, 1]
                for k in range(DC):
                    if before:
                        before(k)
                    if k:
                        nc.tensor.matmul(rest, t_lo[:, k, cols], x_hi[:, k, cols], start=False, stop=False)
                    ins = nc.tensor.matmul(wide, t_hi[:, k, cols], x_hl[:, :, k, cols], start=k == 0,
                                           stop=k == DC - 1)
                    if k == 0:
                        nc.tensor.matmul(rest, t_lo[:, k, cols], x_hi[:, k, cols], start=False, stop=False)
                ins.then_inc(s_mm, 1)

            def turn_p(m, bank):
                pe.wait_ge(pn_s, m + 1)
                nc.tensor.transpose(pt_part(bank), pn[:], ident[:]).then_inc(pt_mm, 1)

            def values(m, h, bank):
                if h == 0:
                    pe.wait_ge(pt_lo_s, m + 1)
                    pe.wait_ge(xk_lo_s, m + 1)
                    if not isinstance(m, int) or m:
                        pe.wait_ge(y_lo_s, m * 2)
                elif bank is y_bank:
                    pe.wait_ge(y_sum, m * 2 + 1)
                wide = y_parts(bank)
                for c in range(2):
                    cols = slice((2 * h + c) * P, (2 * h + c + 1) * P)
                    nc.tensor.matmul(wide[:, c], xk_hi[:, cols], pt_hl[:], start=True, stop=False)
                    ins = nc.tensor.matmul(wide[:, c, 1], xk_lo[:, cols], pt_hl[:, 0], start=False, stop=True)
                ins.then_inc(y_mm, 1)

            def attention(m, s, before_second_layer):
                p = s // 4
                if before_second_layer:
                    if s % 4 == 2:
                        values(m + p, 0, y_bank)
                    return
                if s % 4 == 0:
                    scores(m + p, p, sp_bank)
                if s % 4 == 1:
                    turn_p(m + p, sp_bank)
                if s % 4 == 2:
                    values(m + p, 1, y_bank)

            def stage_c(g, free, more={}):
                for j in range(JH):
                    half_step(0, j % 2, j, (a_hi, a_lo), True, True, g if j == 0 else None)
                    if j:
                        second_layer(g + j, j - 1, free if j == 1 else None)
                    if j in more:
                        more[j]()

            def stage_m(g, pos, t, pair, flush=None):
                pe.wait_ge(h_lo_s, g - 1)
                half_step(pos, 0, 0, (a_hi, a_lo), True, False)
                if flush:
                    flush()
                pe.wait_ge(h_lo_s, g)
                half_step(pos, 1, 2, (a_hi, a_lo), True, False)
                if pair is None:
                    half_step(pos, 0, 1, (c_hi, c_lo), False, True,
                              before=lambda k: pe.wait_ge(c_lo_s, t * DC + k + 1))
                else:
                    pe.wait_ge(c_lo_s, t * DC + DC)
                    half_step(pos, 0, 1, (c_hi, c_lo), False, True)
                if pair is not None:
                    attention(pair, 0, False)
                half_step(pos, 1, 3, (c_hi, c_lo), False, True)
                second_layer(g + 1, 0, (cf_s, t * DC + DC))
                if pair is not None:
                    attention(pair, 1, False)
                for j in range(2, JH):
                    half_step(pos, j % 2, 2 * j, (a_hi, a_lo), True, False)
                    half_step(pos, j % 2, 2 * j + 1, (c_hi, c_lo), False, True)
                    if pair is not None:
                        attention(pair, j, True)
                    second_layer(g + j, j - 1)
                    if pair is not None:
                        attention(pair, j, False)

            for k in range(DC):
                pe.wait_ge(qw_lo, 2 * k + 2)
                for m in range(DC):
                    product_rows(m, k, (t_hi, t_lo), (y_hi, y_lo))
            pe.wait_ge(x_lo_s, DC)
            for c in range(DC):
                project(0, c, 0, (x_hi, x_lo), first=c + 1 if c < 2 else None)
            scores(0, 0, s_banks0[0], before=lambda k: pe.wait_ge(h_lo_s, k + 1))
            product2(0)
            for p in range(NP):
                turn_p(p, s_banks0[p % 2])
                if p + 1 < NP:
                    scores(p + 1, p + 1, s_banks0[(p + 1) % 2])
                    product2(p + 1)
                for h in range(2):
                    values(p, h, y_banks0[h])
            for c in range(DC):
                project(DC, c, QT, (y_hi, y_lo), first=QT + c + 1 if c < 2 else None,
                        before=(lambda k: pe.wait_ge(y_lo_s, 2 * NP - (k < 2))) if c == 0 else None)
            stage_c(2 * DC, None, {4: sort_counts, 10: sort_gather})
            with pe.Fori(0, NT - 1) as i:
                g = i * G_ITER + G_PRE
                pe.wait_ge(x_lo_s, i * DC + 2 * DC)
                project(g, 0, 0, (x_hi, x_lo))
                second_layer(g, JH - 1)
                for c in range(1, DC):
                    project(g, c, 0, (x_hi, x_lo))
                stage_m(g + DC, QT, i, i * NP + NP)
                ga = g + DC + JH
                pe.wait_ge(y_lo_s, i * (2 * NP) + 4 * NP)
                project(ga, 0, QT + QM, (y_hi, y_lo))
                second_layer(ga, JH - 1)
                for c in range(1, DC):
                    project(ga, c, QT + QM, (y_hi, y_lo))
                stage_c(ga + DC, (zt_s, i * DC + DC))
            g = (NT - 1) * G_ITER + G_PRE
            stage_m(g, 0, NT - 1, None, flush=lambda: second_layer(g, JH - 1))
            second_layer(g + JH, JH - 1)

            pe.wait_ge(l1_lo, 2 * R)
            pe.wait_ge(ones_s, 2)
            pe.wait_ge(row_in, 2 * R * 16)

            def pair_role(n):
                return pe.value_load(role_t[0:1, bass.ds(n, 1)], min_val=0, max_val=R - 1)

            def rows(ap, r):
                return ap[:, bass.ds(r, 1)].rearrange("p o n -> p (o n)")

            def down(n, u):
                r = pair_role(n)
                pe.wait_ge(zl_s, n + 1)
                ps = d_ps[u % 2][:, 0:KD]
                nc.tensor.matmul(ps, ones2[:], rows(brow[:, :, 0:KD], r), start=True, stop=False)
                for k in range(DC):
                    w = [rows(half[:, :, k, :], r) for half in (wd_hi, wd_lo)]
                    ins = mm3(ps, (z_hi[:, u % 2, k, :], z_lo[:, u % 2, k, :]), w, False, k == DC - 1)
                ins.then_inc(d_mm, 1)

            def turn(n, u):
                r = pair_role(n)
                pe.wait_ge(gelu_s, n + 1)
                for k in range(KD // P):
                    ins = nc.tensor.transpose(ht_ps[u % 2][:, k * P:(k + 1) * P], hs[:, u % 2, k * P:(k + 1) * P],
                                              ident[:])
                ins.then_inc(ht_mm, 1)
                ps = u_ps[u % 4]
                if isinstance(n, int) and n < 4:
                    pe.wait_ge(zt_s, (NT - 1) * DC + n + 1)
                else:
                    pe.wait_ge(yg_s, n - 3)
                nc.tensor.matmul(ps[:], ones2[:], rows(brow[:, :, KD:KD + D], r), start=True, stop=False)
                for k in range(DC):
                    nc.tensor.matmul(ps[:, k * P:(k + 1) * P], zf[:, u % 4, k, :], ident[:], start=False,
                                     stop=False, is_transpose=True)
                return r

            def up(n, u, r):
                pe.wait_ge(ht_lo_s, n + 1)
                for k in range(KD // P):
                    w = [rows(half[:, :, k, :], r) for half in (wu_hi, wu_lo)]
                    cols = slice(k * P, (k + 1) * P)
                    ins = mm3(u_ps[u % 4][:], (ht_hi[:, u % 2, cols], ht_lo[:, u % 2, cols]), w, False,
                              k == KD // P - 1)
                ins.then_inc(u_mm, 1)

            def unit(n, u, d):
                r = turn(n, u)
                if d:
                    down(n + 1, u + 1)
                up(n, u, r)

            down(0, 0)
            for n in range(4):
                unit(n, n, True)
            pe_loops = (NPAIR - 5) // UNROLL
            with pe.Fori(0, pe_loops) as k:
                for u in range(UNROLL):
                    unit(k * UNROLL + (4 + u), u, True)
            for n in range(pe_loops * UNROLL + 4, NPAIR):
                unit(n, n, n + 1 < NPAIR)


def kernel(**inputs):
    import numpy as np
    import concourse.bacc as bacc
    from concourse.bass_utils import run_bass_kernel_spmd

    a = {k.removeprefix("L0_cond_").removeprefix("L1_cond_"): np.asarray(v) for k, v in inputs.items()}

    def rows(w):
        return w.reshape(-1, P, w.shape[-1]).transpose(1, 0, 2)

    def blocks(w):
        k, n = w.shape
        return w.reshape(k // D, DC, P, n // P, P).transpose(3, 0, 2, 1, 4).reshape(-1, P, D)

    x = a["x"].reshape(NT, TOK, DC, P)
    arrays = {
        "xT": x.transpose(0, 3, 2, 1),
        "xk": a["x"].reshape(NT * NP, P, D),
        "w1c": blocks(a["cW1"]),
        "w1m": blocks(a["mW1"]),
        "w2c": a["cW2"].reshape(JH, P, D),
        "w2m": a["mW2"].reshape(JH, P, D),
        "wqT": rows(a["Wq"].T),
        "wkT": rows(a["Wk"].T),
        "wvT": rows(a["Wv"].T),
        "wp": rows(a["Wp"]),
        "bias": np.concatenate([a[n].reshape(-1, P).T for n in ("cb1", "mb1", "bp", "cb2", "mb2")], axis=1),
        "target": a["itok_B_17_1546"].reshape(1, B),
        "role": a["itok_B_1_2"].reshape(B, 1),
        "wd": a["W_down"].reshape(R, DC, P, KD).transpose(2, 0, 1, 3),
        "wu": a["W_up"].reshape(R, KD // P, P, D).transpose(2, 0, 1, 3),
        "bd": a["b_down"].reshape(1, R, KD),
        "bu": a["b_up"].reshape(1, R, D),
        "gamma": a["gamma"].reshape(1, R, D),
        "beta": a["beta"].reshape(1, R, D),
    }
    arrays = {n: np.ascontiguousarray(v) for n, v in arrays.items()}
    nc = bacc.Bacc("TRN2", target_bir_lowering=False, num_devices=1)
    args = [nc.dram_tensor(n, v.shape, mybir.dt.from_np(v.dtype), kind="ExternalInput").ap() for n, v in arrays.items()]
    out = nc.dram_tensor("out", (B, S, D), F32, kind="ExternalOutput").ap()
    program(nc, *args, out)
    r = run_bass_kernel_spmd(nc, [arrays], core_ids=[0])
    return r.results[0]["out"]
```
